# Optimizing a Trainium2 kernel written in Bass

```python
import numpy as np
import jax
import jax.numpy as jnp

def _softmax(x, axis=-1):
    return jax.nn.softmax(x, axis=axis)

def _gelu(x):
    return jax.nn.gelu(x, approximate=True)

def _silu(x):
    return jax.nn.silu(x)

def _sigmoid(x):
    return jax.nn.sigmoid(x)

def _layernorm(x, axis=-1, eps=1e-05):
    m = jnp.mean(x, axis=axis, keepdims=True)
    v = jnp.var(x, axis=axis, keepdims=True)
    return (x - m) / jnp.sqrt(v + eps)

def _scatter_add(tgt, idx, src, axis=0):
    return tgt.at[idx].add(src)

def _segment_sum(src, seg, n):
    return jax.ops.segment_sum(src, seg, n)
kernel_name = 'mk_prb_d2_jaxref_r8_2454fa'

def setup_inputs(seed: int=0):
    np.random.seed(seed)
    _w = jnp.asarray

    def _L0_attn_setup():
        import jax, jax.numpy as jnp
        import numpy as np
        import math
        NUM_HEADS = 8
        EMB = 128
        HEAD_DIM = 128
        B, T = (1, 512)

        def sinusoidal_pe(T, d, dtype=jnp.float32):
            pos = jnp.arange(T, dtype=dtype)[:, None]
            inv_freq = jnp.exp(-math.log(10000.0) * jnp.arange(0, d, 2, dtype=dtype) / d)
            ang = pos * inv_freq[None, :]
            pe = jnp.zeros((T, d), dtype=dtype)
            pe = pe.at[:, 0::2].set(jnp.sin(ang))
            pe = pe.at[:, 1::2].set(jnp.cos(ang))
            return pe
        key = jax.random.key(seed)
        ks = jax.random.split(key, 6)
        s = lambda fan_in: 1.0 / math.sqrt(fan_in)
        x = jax.random.normal(ks[0], (B, T, EMB), dtype=jnp.float32)
        Wq = jax.random.normal(ks[1], (EMB, NUM_HEADS * HEAD_DIM), dtype=jnp.float32) * s(EMB)
        bq = jax.random.normal(ks[2], (NUM_HEADS * HEAD_DIM,), dtype=jnp.float32) * s(EMB)
        Wkv = jax.random.normal(ks[3], (EMB, 2 * HEAD_DIM), dtype=jnp.float32) * s(EMB)
        bkv = jax.random.normal(ks[4], (2 * HEAD_DIM,), dtype=jnp.float32) * s(EMB)
        Wo = jax.random.normal(ks[5], (NUM_HEADS * HEAD_DIM, EMB), dtype=jnp.float32) * s(NUM_HEADS * HEAD_DIM)
        return {'x': x, 'Wq': Wq, 'bq': bq, 'Wkv': Wkv, 'bkv': bkv, 'Wo': Wo}
    _L0_attn_in = _L0_attn_setup()

    def _L0_ffn_setup():
        import jax, jax.numpy as jnp
        import numpy as np
        B, S, D, E, F = (2, 256, 128, 14, 256)
        key = jax.random.key(seed)
        k = jax.random.split(key, 4)
        h = jax.random.normal(k[0], (B, S, D), dtype=jnp.float32)
        router_w = jax.random.normal(k[1], (D, E), dtype=jnp.float32) * 0.02
        w1 = jax.random.uniform(k[2], (E, D, F), dtype=jnp.float32, minval=-1.0, maxval=1.0) * float(np.sqrt(6.0 / D))
        w2 = jax.random.uniform(k[3], (E, F, D), dtype=jnp.float32, minval=-1.0, maxval=1.0) * float(np.sqrt(6.0 / F))
        b1 = jnp.zeros((E, F), dtype=jnp.float32)
        b2 = jnp.zeros((E, D), dtype=jnp.float32)
        return {'h': h, 'router_w': router_w, 'w1': w1, 'b1': b1, 'w2': w2, 'b2': b2}
    _L0_ffn_in = _L0_ffn_setup()

    def _L1_attn_setup():
        import jax, jax.numpy as jnp
        import numpy as np
        key = jax.random.key(seed)
        B, L, d_model, d_state, expand = (2, 256, 128, 16, 2)
        d_inner = expand * d_model
        ks = jax.random.split(key, 8)
        s = lambda k, shape, scale: jax.random.normal(k, shape, dtype=jnp.float32) * scale
        x = s(ks[0], (B, L, d_model), 1.0)
        W_in = s(ks[1], (d_model, 2 * d_inner), 0.02)
        W_delta = s(ks[2], (d_inner, d_inner), 0.02)
        b_delta = s(ks[3], (d_inner,), 0.02)
        W_B = s(ks[4], (d_inner, d_state), 0.02)
        W_C = s(ks[5], (d_inner, d_state), 0.02)
        A_log = jnp.log(jnp.broadcast_to(jnp.arange(1, d_state + 1, dtype=jnp.float32), (d_inner, d_state)))
        D_param = jnp.ones((d_inner,), dtype=jnp.float32)
        W_out = s(ks[6], (d_inner, d_model), 0.02)
        return dict(x=x, W_in=W_in, W_delta=W_delta, b_delta=b_delta, W_B=W_B, W_C=W_C, A_log=A_log, D_param=D_param, W_out=W_out)
    _L1_attn_in = _L1_attn_setup()

    def _L1_ffn_setup():
        import jax, jax.numpy as jnp
        import numpy as np
        D_MODEL = 128
        NUM_EXPERTS = 8
        TOP_K = 2
        key = jax.random.key(seed)
        k_x, k_g, k_w1, k_w2 = jax.random.split(key, 4)
        B, S, D, E = (4, 256, D_MODEL, NUM_EXPERTS)
        s_in = 1.0 / np.sqrt(D)
        s_hid = 1.0 / np.sqrt(4 * D)
        return {'x': jax.random.normal(k_x, (B, S, D), dtype=jnp.float32), 'gate_w': jax.random.uniform(k_g, (E, D), jnp.float32, -s_in, s_in), 'w1': jax.random.uniform(k_w1, (E, 4 * D, D), jnp.float32, -s_in, s_in), 'w2': jax.random.uniform(k_w2, (E, D, 4 * D), jnp.float32, -s_hid, s_hid)}
    _L1_ffn_in = _L1_ffn_setup()
    _d = {'L0_attn_x': _L0_attn_in['x'], 'L0_attn_Wq': _L0_attn_in['Wq'], 'L0_attn_bq': _L0_attn_in['bq'], 'L0_attn_Wkv': _L0_attn_in['Wkv'], 'L0_attn_bkv': _L0_attn_in['bkv'], 'L0_attn_Wo': _L0_attn_in['Wo'], 'L0_ffn_router_w': _L0_ffn_in['router_w'], 'L0_ffn_w1': _L0_ffn_in['w1'], 'L0_ffn_b1': _L0_ffn_in['b1'], 'L0_ffn_w2': _L0_ffn_in['w2'], 'L0_ffn_b2': _L0_ffn_in['b2'], 'L1_attn_W_in': _L1_attn_in['W_in'], 'L1_attn_W_delta': _L1_attn_in['W_delta'], 'L1_attn_b_delta': _L1_attn_in['b_delta'], 'L1_attn_W_B': _L1_attn_in['W_B'], 'L1_attn_W_C': _L1_attn_in['W_C'], 'L1_attn_A_log': _L1_attn_in['A_log'], 'L1_attn_D_param': _L1_attn_in['D_param'], 'L1_attn_W_out': _L1_attn_in['W_out'], 'L1_ffn_gate_w': _L1_ffn_in['gate_w'], 'L1_ffn_w1': _L1_ffn_in['w1'], 'L1_ffn_w2': _L1_ffn_in['w2']}
    _x0 = _d['L0_attn_x']
    _d['L0_attn_x'] = jax.random.normal(jax.random.fold_in(jax.random.key(seed), 1), (2, 1024, 128), dtype=_x0.dtype)
    del _x0
    return _d

def reference(L0_attn_x, L0_attn_Wq, L0_attn_bq, L0_attn_Wkv, L0_attn_bkv, L0_attn_Wo, L0_ffn_router_w, L0_ffn_w1, L0_ffn_b1, L0_ffn_w2, L0_ffn_b2, L1_attn_W_in, L1_attn_W_delta, L1_attn_b_delta, L1_attn_W_B, L1_attn_W_C, L1_attn_A_log, L1_attn_D_param, L1_attn_W_out, L1_ffn_gate_w, L1_ffn_w1, L1_ffn_w2):

    def _L0_attn_ref(x, Wq, bq, Wkv, bkv, Wo):
        import jax, jax.numpy as jnp
        import numpy as np
        import math
        NUM_HEADS = 8
        EMB = 128
        HEAD_DIM = 128
        B, T = (1, 512)

        def sinusoidal_pe(T, d, dtype=jnp.float32):
            pos = jnp.arange(T, dtype=dtype)[:, None]
            inv_freq = jnp.exp(-math.log(10000.0) * jnp.arange(0, d, 2, dtype=dtype) / d)
            ang = pos * inv_freq[None, :]
            pe = jnp.zeros((T, d), dtype=dtype)
            pe = pe.at[:, 0::2].set(jnp.sin(ang))
            pe = pe.at[:, 1::2].set(jnp.cos(ang))
            return pe
        Bsz, Tlen, E = x.shape
        q = (x @ Wq + bq).reshape(Bsz, Tlen, NUM_HEADS, HEAD_DIM)
        kv = x @ Wkv + bkv
        k, v = (kv[..., :HEAD_DIM], kv[..., HEAD_DIM:])
        q = jnp.transpose(q, (0, 2, 1, 3))
        pe = sinusoidal_pe(Tlen, HEAD_DIM, x.dtype)
        q = q + pe[None, None, :, :]
        k = k + pe[None, :, :]
        scale = 1.0 / math.sqrt(HEAD_DIM)
        scores = jnp.einsum('bhqd,bkd->bhqk', q, k) * scale
        causal = jnp.tril(jnp.ones((Tlen, Tlen), dtype=bool))
        scores = jnp.where(causal[None, None, :, :], scores, jnp.finfo(scores.dtype).min)
        probs = jax.nn.softmax(scores, axis=-1)
        attn = jnp.einsum('bhqk,bkd->bhqd', probs, v)
        out = jnp.transpose(attn, (0, 2, 1, 3)).reshape(Bsz, Tlen, NUM_HEADS * HEAD_DIM)
        return out @ Wo

    def _L0_ffn_ref(h, router_w, w1, b1, w2, b2):
        import jax, jax.numpy as jnp
        import numpy as np
        B, S, D, E, F = (2, 256, 128, 14, 256)
        Bb, Ss, Dd = h.shape
        x = h.reshape(-1, Dd)
        logits = x @ router_w
        assignments = jnp.argmax(logits, axis=-1)
        probs = jax.nn.softmax(logits, axis=-1)
        weights = jnp.take_along_axis(probs, assignments[:, None], axis=1)[:, 0]
        hid = jnp.einsum('nd,edf->nef', x, w1) + b1
        hid = jax.nn.gelu(hid, approximate=False)
        all_out = jnp.einsum('nef,efd->ned', hid, w2) + b2
        sel = jnp.take_along_axis(all_out, assignments[:, None, None], axis=1)[:, 0, :]
        moe_out = (sel * weights[:, None]).reshape(Bb, Ss, Dd)
        return moe_out

    def _L1_attn_ref(x, W_in, W_delta, b_delta, W_B, W_C, A_log, D_param, W_out):
        import jax, jax.numpy as jnp
        import numpy as np
        d_inner = W_delta.shape[0]
        x_and_res = x @ W_in
        u, res = (x_and_res[..., :d_inner], x_and_res[..., d_inner:])
        u = jax.nn.silu(u)
        delta = jax.nn.softplus(u @ W_delta + b_delta)
        Bm = u @ W_B
        Cm = u @ W_C
        A = -jnp.exp(A_log)

        def step(h, inp):
            d_t, B_t, C_t, u_t = inp
            dA = jnp.exp(d_t[..., None] * A)
            h = dA * h + d_t[..., None] * B_t[:, None, :] * u_t[..., None]
            y_t = jnp.einsum('bdn,bn->bd', h, C_t)
            return (h, y_t)
        Bsz = x.shape[0]
        h0 = jnp.zeros((Bsz, d_inner, A.shape[1]), dtype=x.dtype)
        xs = (jnp.swapaxes(delta, 0, 1), jnp.swapaxes(Bm, 0, 1), jnp.swapaxes(Cm, 0, 1), jnp.swapaxes(u, 0, 1))
        _, ys = jax.lax.scan(step, h0, xs)
        y = jnp.swapaxes(ys, 0, 1) + u * D_param
        y = y * jax.nn.silu(res)
        return y @ W_out

    def _L1_ffn_ref(x, gate_w, w1, w2):
        import jax, jax.numpy as jnp
        import numpy as np
        D_MODEL = 128
        NUM_EXPERTS = 8
        TOP_K = 2
        gate_logits = jnp.einsum('bsd,ed->bse', x, gate_w)
        top_v, top_i = jax.lax.top_k(gate_logits, TOP_K)
        gates = jax.nn.softmax(top_v, axis=-1)
        combine = jnp.sum(jax.nn.one_hot(top_i, NUM_EXPERTS, dtype=x.dtype) * gates[..., None], axis=-2)
        out = jnp.zeros_like(x)
        for e in range(NUM_EXPERTS):
            h = jax.nn.relu(jnp.einsum('bsd,fd->bsf', x, w1[e]))
            y = jnp.einsum('bsf,df->bsd', h, w2[e])
            out = out + combine[..., e, None] * y
        return out
    x = L0_attn_x
    xn = _layernorm(x, axis=-1)
    x = x + _L0_attn_ref(xn, L0_attn_Wq, L0_attn_bq, L0_attn_Wkv, L0_attn_bkv, L0_attn_Wo) + _L0_ffn_ref(xn, L0_ffn_router_w, L0_ffn_w1, L0_ffn_b1, L0_ffn_w2, L0_ffn_b2)
    xn = _layernorm(x, axis=-1)
    x = x + _L1_attn_ref(xn, L1_attn_W_in, L1_attn_W_delta, L1_attn_b_delta, L1_attn_W_B, L1_attn_W_C, L1_attn_A_log, L1_attn_D_param, L1_attn_W_out) + _L1_ffn_ref(xn, L1_ffn_gate_w, L1_ffn_w1, L1_ffn_w2)
    return x

_drawn_inputs = setup_inputs


def setup_inputs(seed=0):
    import zlib

    import numpy as np

    out = dict(_drawn_inputs(seed))
    spreads = {'L0_ffn_b1': (0.0, 0.486), 'L0_ffn_b2': (0.0, 0.485), 'L1_attn_D_param': (1.0, 0.6)}
    factors = {'L1_attn_W_in': 8.0,
     'L1_attn_W_delta': 8.0,
     'L1_attn_b_delta': 8.0,
     'L1_attn_W_B': 8.0,
     'L1_attn_W_C': 8.0,
     'L1_attn_A_log': 8.0,
     'L1_attn_W_out': 8.0,
     'L1_ffn_gate_w': 8.0,
     'L1_ffn_w1': 8.0,
     'L1_ffn_w2': 8.0}
    for name, (base, spread) in spreads.items():
        noise = np.random.default_rng([zlib.crc32(name.encode()), seed]).standard_normal(out[name].shape)
        drawn = base * np.exp(spread * noise) if base else spread * noise
        out[name] = jnp.asarray(drawn.astype(out[name].dtype))
    for name, factor in factors.items():
        out[name] = (out[name] * factor).astype(out[name].dtype)
    return out
```

```python
from contextlib import ExitStack

import numpy as np

import concourse.bass as bass
from concourse import mybir

ALU = mybir.AluOpType
ACT = mybir.ActivationFunctionType
F32 = mybir.dt.float32
BF16 = mybir.dt.bfloat16
I32 = mybir.dt.int32
U32 = mybir.dt.uint32
AX_X = mybir.AxisListType.X

P = 128
B, T, D = 2, 1024, 128
NT = B * T // P
TB = T // P
BANK = 512
HEADS = 8
EPS = 1e-5
SCALE = float(D) ** -0.5
MASKED = -1e30
STATE = 16
INNER = 2
KEPT = 3e38

MOE = [(14, 1, 2), (8, 2, 4)]
TILES = [4 * -(-((B * T * k + e * (P - 1)) // P) // 4) for e, k, _ in MOE]
PAIRS = [n // 2 for n in TILES]


def small_constants():
    k, m = np.arange(P)[:, None], np.arange(P)[None, :]
    parts = {
        "ident": (k == m),
        "causal": np.where(m > k, MASKED, 0.0),
        "before": (k < m),
        "pick": (k % 32 == np.arange(32)[None, :]) & (k < 96),
        "iota": np.broadcast_to(np.arange(16)[None, :] - 16.0, (P, 16)),
        "first": np.broadcast_to(np.arange(max(TILES))[None, :] * P, (P, max(TILES))),
    }
    at, cols, where = 0, [], {}
    for name, a in parts.items():
        a = np.asarray(a, np.float32)
        where[name] = (at, at + a.shape[1])
        at += a.shape[1]
        cols.append(a)
    return np.ascontiguousarray(np.concatenate(cols, 1)), where


def positions():
    pos = np.arange(T, dtype=np.float32)[:, None]
    step = np.exp(np.float32(-np.log(10000.0)) * np.arange(0, D, 2, dtype=np.float32) / np.float32(D))
    angle = pos * step.astype(np.float32)[None, :]
    pe = np.zeros((T, D), np.float32)
    pe[:, 0::2] = np.sin(angle)
    pe[:, 1::2] = np.cos(angle)
    return np.ascontiguousarray(pe.T)


def build(nc, A, out, scratch):
    _, WHERE = small_constants()
    with ExitStack() as ctx:
        def sb(name, shape, dt=F32):
            return ctx.enter_context(nc.sbuf_tensor(name, shape, dt))

        def sem(name):
            return ctx.enter_context(nc.semaphore(name))

        X = sb("X", [P, NT, D])
        XN = sb("XN", [P, NT, D])
        XNT = sb("XNT", [P, B * T])
        CST = sb("CST", [P, sum(b - a for a, b in list(WHERE.values())[-1:]) + list(WHERE.values())[-1][0]])
        cst = {n: CST[:, a:b] for n, (a, b) in WHERE.items()}
        ident = cst["ident"]
        identb = sb("identb", [P, P], BF16)
        causalb = sb("causalb", [P, P], BF16)
        beforeb = sb("beforeb", [P, P], BF16)
        onesb = sb("onesb", [P, P], BF16)
        pickb = sb("pickb", [P, 32, P], BF16)
        ones1 = sb("ones1", [1, P])
        zero = sb("zero", [P, BANK])
        peT = sb("peT", [P, T])
        wkv = sb("wkv", [P, 2 * D])
        bk = sb("bk", [P, 1])
        bv = sb("bv", [1, D])
        bq = sb("bq", [P, HEADS])
        wo = sb("wo", [P, HEADS, D])
        wgate = [sb(f"wgate{m}", [P, MOE[m][0]]) for m in range(2)]
        wq = sb("wq", [P, 2, D])
        KT = sb("KT", [P, B, T])
        V = sb("V", [P, NT, D])
        QT = sb("QT", [P, T])
        PR = sb("PR", [P, 2, T])
        PTa = sb("PTa", [P, 4, BANK])
        PTb = sb("PTb", [P, 8, BANK])
        OT = sb("OT", [P, 2, BANK])
        nmax = sb("nmax", [P, 4])
        rsum = sb("rsum", [P, TB])
        rinv = sb("rinv", [P, TB])
        stats = sb("stats", [P, NT, 6])
        mv = sb("mv", [P, NT, 2])
        lnt = sb("lnt", [P, 6, NT])
        EM = 14
        lg = sb("lg", [P, NT * EM])
        oh = sb("oh", [P, 3, NT * EM])
        ohb = sb("ohb", [P, NT * EM], BF16)
        rt = sb("rt", [P, 5, NT * EM])
        seg = [sb(f"seg{m}", [P, NT * MOE[m][0]]) for m in range(2)]
        rs1 = sb("rs1", [P, 12, NT])
        re1 = sb("re1", [P, 6, 16])
        rei = sb("rei", [P, 2, 16], I32)
        tl = sb("tl", [P, max(TILES) * EM])
        wsel = [sb(f"wsel{m}", [P, MOE[m][1], NT]) for m in range(2)]
        slot = [sb(f"slot{m}", [P, MOE[m][1], NT], U32) for m in range(2)]
        eid = [sb(f"eid{m}", [P, TILES[m]], I32) for m in range(2)]
        mw1 = sb("mw1", [P, 2, 512])
        mw2 = sb("mw2", [P, 2, 4, D])
        mb1 = sb("mb1", [P, 2, 2])
        mb2 = sb("mb2", [1, 2, D])
        MX = sb("MX", [P, 2, 2, D])
        MXT = sb("MXT", [P, 2, P])
        MH = sb("MH", [P, 2, 4, P])
        MY = sb("MY", [P, 2, 2, D])
        GA = sb("GA", [P, 4, D * 4])
        w_in = sb("w_in", [P, 4 * D])
        w_dl = sb("w_dl", [P, 2, 2 * D])
        b_dl = sb("b_dl", [P, 2])
        w_bc = sb("w_bc", [P, 2, 32])
        a_lg = sb("a_lg", [P, 2, STATE])
        a_sc = sb("a_sc", [P, 2, STATE])
        d_par = sb("d_par", [P, 2])
        w_out = sb("w_out", [P, 2, D])
        UT = sb("UT", [P, 2, T])
        SR = sb("SR", [P, 2, T])
        DL = sb("DL", [P, 2, T])
        DU = sb("DU", [P, 2, T])
        DA = sb("DA", [P, 2, T])
        DB = sb("DB", [P, 2, T])
        HS = GA[:, :, :].rearrange("p (c a) n -> p c (a n)", c=2)
        HC = PTb[:, 0:4, :].rearrange("p (c a) n -> p c (a n)", c=2)
        YA = PTb[:, 4:8, :].rearrange("p (c a) n -> p c (a n)", c=2)
        R3 = sb("R3", [P, T], BF16)
        PS = ctx.enter_context(nc.psum_tensor("PS", [P, 8, BANK], F32))

        def bank(k, n=BANK):
            return PS[:, k, 0:n]

        s_x = sem("x_loaded")
        s_cst = sem("constants_loaded")
        s_cnv = sem("constants_converted")
        s_wat = sem("attention_weights_loaded")
        s_wsc = sem("scan_weights_loaded")
        s_zero = sem("zero_tile_ready")
        s_zf = sem("rows_zeroed")
        s_v = sem("vector_step")
        s_var = sem("variance_ready")
        s_sd = sem("deviation_ready")
        s_xn = sem("normalised_ready")
        s_tp = sem("transposed_in_psum")
        s_xnt = sem("transposed_ready")
        s_lg = sem("logits_in_psum")
        s_lgr = sem("logits_read")
        s_kp = sem("keys_in_psum")
        s_ke = sem("keys_ready")
        s_vp = sem("values_in_psum")
        s_ve = sem("values_ready")
        s_ein = sem("gate_exponent_in")
        s_eout = sem("gate_exponent_out")
        s_ohb = sem("onehot_ready")
        s_rk = sem("ranks_in_psum")
        s_rkr = sem("ranks_read")
        s_slot = sem("slots_ready")
        s_eid = sem("tile_experts_ready")
        s_sc = [sem(f"rows_scattered{m}") for m in range(2)]
        s_wq = [sem(f"wq_loaded{i}") for i in range(2)]
        s_qp = sem("query_in_psum")
        s_qe = sem("query_ready")
        s_qk = sem("scores_ready")
        s_nm = sem("negmax_ready")
        s_ex = sem("probs_ready")
        s_tc = sem("probs_transposed")
        s_ed = sem("probsT_by_vector")
        s_ea = sem("probsT_by_scalar")
        s_pv = sem("head_out_in_psum")
        s_ue = sem("head_out_ready")
        s_ri = sem("inverse_sum_ready")
        s_wo = sem("projected_in_psum")
        s_we = sem("projected_added")
        s_mw = [[sem(f"expert_weights{m}{i}") for i in range(2)] for m in range(2)]
        s_mx = [[sem(f"expert_rows{m}{i}") for i in range(2)] for m in range(2)]
        s_mtp = [sem(f"expert_rowsT_in_psum{m}") for m in range(2)]
        s_mt = [sem(f"expert_rowsT_ready{m}") for m in range(2)]
        s_mhp = [sem(f"expert_hidden_in_psum{m}") for m in range(2)]
        s_mh = [sem(f"expert_hidden_ready{m}") for m in range(2)]
        s_myp = [sem(f"expert_out_in_psum{m}") for m in range(2)]
        s_my = [sem(f"expert_out_ready{m}") for m in range(2)]
        s_mo = [[sem(f"expert_out_stored{m}{i}") for i in range(2)] for m in range(2)]
        s_ga = sem("rows_gathered")
        s_gu = sem("gathered_added")
        s_up = sem("inner_in_psum")
        s_ue2 = sem("inner_ready")
        s_dp = sem("delta_in_psum")
        s_da1 = sem("delta_abs_ready")
        s_dr = sem("delta_psum_read")
        s_dw = sem("delta_one_plus_ready")
        s_dl = sem("delta_log_ready")
        s_du = sem("delta_u_ready")
        s_bp = sem("bc_rows_in_psum")
        s_r3 = sem("bc_split_ready")
        s_as = sem("decay_rates_ready")
        s_b = sem("b_spread")
        s_c = sem("c_spread")
        s_dA = sem("decay_ready")
        s_db = sem("drive_ready")
        s_sn = sem("state_ready")
        s_hc = sem("state_c_ready")
        s_ya = sem("y_added")
        s_y0 = sem("y_cleared")
        s_yt = sem("y_gated")
        s_op = sem("scan_out_in_psum")
        s_oe = sem("scan_out_added")
        s_end = sem("output_stored")

        xs = scratch["rows_in"]
        ys = scratch["rows_out"]
        n_cst_rows = 0

        def bc(ap, axis, n):
            shape = list(ap.shape)
            return ap.unsqueeze(axis).broadcast_to(shape[:axis] + [n] + shape[axis:])

        block = ctx.enter_context(nc.Block())

        @block.sync
        def _(sp):
            for q in range(4):
                sp.dma_start(X[:, 4 * q:4 * q + 4, :],
                             A["x"].rearrange("b (t p) d -> p (b t) d", p=P)[:, 4 * q:4 * q + 4, :]
                             ).then_inc(s_x, 16)
            sp.dma_start(CST[:], A["cst"]).then_inc(s_cst, 16)
            for dst, src in ((wkv[:], A["Wkv"]), (peT[:], A["peT"]),
                             (bk[:], A["bkv"][0:D].rearrange("(p o) -> p o", o=1)),
                             (bv[:], A["bkv"][D:2 * D].rearrange("(o d) -> o d", o=1)),
                             (bq[:], A["bq"]),
                             (wgate[0][:], A["router_w"]),
                             (wo[:], A["Wo"].rearrange("(h p) d -> p h d", p=P)),
                             (wgate[1][:], A["gate_wT"])):
                sp.dma_start(dst, src).then_inc(s_wat, 16)
            sp.wait_ge(s_zero, 1)
            for m in range(2):
                flat = xs[m].rearrange("(p r) d -> p (r d)", p=P)
                for c in range(0, TILES[m] * D, 512):
                    w = min(512, TILES[m] * D - c)
                    sp.dma_start(flat[:, c:c + w], zero[:, 0:w]).then_inc(s_zf, 16)
            for dst, src in ((w_in[:], A["W_in"]),
                             (w_dl[:], A["W_delta"].rearrange("(k p) n -> p k n", p=P)),
                             (b_dl[:], A["b_delta"]),
                             (w_bc[:, :, 0:STATE], A["W_B"].rearrange("(k p) n -> p k n", p=P)),
                             (w_bc[:, :, STATE:32], A["W_C"].rearrange("(k p) n -> p k n", p=P)),
                             (a_lg[:], A["A_log"].rearrange("(k p) n -> p k n", p=P)),
                             (d_par[:], A["D_param"]),
                             (w_out[:], A["W_out"].rearrange("(k p) n -> p k n", p=P))):
                sp.dma_start(dst, src).then_inc(s_wsc, 16)

            def load_wq(g, h, i, free):
                if free is not None:
                    sp.wait_ge(s_qp, free)
                sp.dma_start(wq[:, i, :], A["WqH"][h]).then_inc(s_wq[i], 16)

            def attention_loads(b):
                load_wq(8 * b, 0, 0, None if b == 0 else 16 * b - 2)
                load_wq(8 * b + 1, 1, 1, None if b == 0 else 16 * b)
                with sp.Fori(1, 4) as r:
                    load_wq(None, 2 * r, 0, 16 * b + 4 * r - 2)
                    load_wq(None, 2 * r + 1, 1, 16 * b + 4 * r)

            def expert_loads(m):
                e_n, k_n, f_n = MOE[m]
                sp.wait_ge(s_eid, m + 1)
                sp.wait_ge(s_sc[m], 16 * NT * k_n)

                def pair(p, s, first):
                    if not first:
                        sp.wait_ge(s_mtp[m], p - 1)
                    sp.dma_start(MX[:, s, :, :], xs[m][bass.ds(p * 2 * P, 2 * P), :].rearrange("(i p) d -> p i d", p=P)
                                 ).then_inc(s_mx[m][s], 16)
                    for i in range(2):
                        e = sp.value_load(eid[m][0:1, bass.ds(2 * p + i, 1)], min_val=0, max_val=e_n - 1)
                        if not (first and s == 0):
                            sp.wait_ge(s_myp[m], 2 * p + i - 1)
                        sp.dma_start(mw1[:, i, 0:f_n * P], A[f"w1_{m}"][bass.ds(e, 1)].rearrange("o p n -> (o p) n")
                                     ).then_inc(s_mw[m][i], 16)
                        sp.dma_start(mw2[:, i, 0:f_n, :], A[f"w2_{m}"][bass.ds(e, 1)].rearrange("o (c p) n -> (o p) c n", p=P)
                                     ).then_inc(s_mw[m][i], 16)
                        if m == 0:
                            sp.dma_start(mb1[:, i, :], A["b1"][bass.ds(e, 1)].rearrange("o p c -> (o p) c")
                                         ).then_inc(s_mw[m][i], 16)
                            sp.dma_start(mb2[:, i, :], A["b2"][bass.ds(e, 1)]).then_inc(s_mw[m][i], 16)

                pair(0, 0, True)
                pair(1, 1, True)
                with sp.Fori(1, PAIRS[m] // 2) as r:
                    pair(2 * r, 0, False)
                    pair(2 * r + 1, 1, False)

            attention_loads(0)
            expert_loads(0)
            attention_loads(1)
            sp.wait_ge(s_my[0], PAIRS[0])
            expert_loads(1)
            sp.wait_ge(s_gu, 16 + 32)
            ov = out.rearrange("b (t p) d -> p (b t) d", p=P)
            for q in range(4):
                sp.dma_start(ov[:, 4 * q:4 * q + 4, :], X[:, 4 * q:4 * q + 4, :]).then_inc(s_end, 16)
            sp.wait_ge(s_end, 64)

        @block.gpsimd
        def _(pool):
            nc.gpsimd.memset(zero[:], 0.0).then_inc(s_zero, 1)
            zf = sum(-(-TILES[m] * D // 512) for m in range(2))

            def scatter(m):
                pool.wait_ge(s_slot, m + 1)
                pool.wait_ge(s_zf, 16 * zf)
                for k in range(MOE[m][1]):
                    for t in range(NT):
                        nc.gpsimd.indirect_dma_start(
                            out=xs[m][:, :], out_offset=bass.IndirectOffsetOnAxis(ap=slot[m][:, k, t:t + 1], axis=0),
                            in_=XN[:, t, :], in_offset=None).then_inc(s_sc[m], 16)

            def gather(m):
                for i in range(2):
                    pool.wait_ge(s_mo[m][i], 16 * (PAIRS[m] // 2))
                for k in range(MOE[m][1]):
                    if m + k:
                        pool.wait_ge(s_gu, 16 * (m + k))
                    for t in range(NT):
                        nc.gpsimd.indirect_dma_start(
                            out=GA[:, t // 4, (t % 4) * D:(t % 4 + 1) * D], out_offset=None, in_=ys[m][:, :],
                            in_offset=bass.IndirectOffsetOnAxis(ap=slot[m][:, k, t:t + 1], axis=0)).then_inc(s_ga, 16)

            scatter(0)
            gather(0)
            scatter(1)
            for b in range(B):
                if b:
                    pool.wait_ge(s_yt, 2 * b)
                nc.gpsimd.memset(YA, 0.0).then_inc(s_y0, 1)
                pool.wait_ge(s_y0, b + 1)

                def add(n, c, self_free):
                    pool.wait_ge(s_hc, 32 * b + 2 * n + c + 1)
                    if self_free:
                        pool.wait_ge(s_ya, 32 * b + 2 * n + c - 1)
                    nc.gpsimd.tensor_tensor(YA[:, c, :], YA[:, c, :], HC[:, c, :], ALU.add).then_inc(s_ya, 1)

                add(0, 0, False)
                add(0, 1, False)
                with pool.Fori(1, STATE) as n:
                    add(n, 0, True)
                    add(n, 1, True)
            gather(1)

        @block.scalar
        def _(act):
            def deviation(ph):
                act.wait_ge(s_var, ph + 1)
                nc.scalar.activation(lnt[:, 1, :], lnt[:, 0, :], ACT.Sqrt).then_inc(s_sd, 1)

            def gate_exp(ph):
                act.wait_ge(s_ein, ph + 1)
                n = NT * MOE[0][0] if ph == 0 else NT
                src = rt[:, 0, 0:n] if ph == 0 else rs1[:, 5, :]
                dst = rt[:, 1, 0:n] if ph == 0 else rs1[:, 6, :]
                nc.scalar.activation(dst, src, ACT.Exp).then_inc(s_eout, 1)

            deviation(0)
            for q in range(4):
                act.wait_ge(s_vp, q + 1)
                nc.scalar.copy(V[:, 4 * q:4 * q + 4, :], bank((5, 6, 7, 1)[q])).then_inc(s_ve, 1)
            gate_exp(0)

            def out_evac(s, done):
                act.wait_ge(s_pv, done)
                nc.scalar.copy(OT[:, s, :], bank(6)).then_inc(s_ue, 1)

            def evac(i, chunk_done):
                act.wait_ge(s_tc, chunk_done)
                dst = PTb[:, 0:4, (i - 4) * P:(i - 3) * P]
                nc.scalar.copy(dst, bank(4).rearrange("p (j q) -> p j q", q=P)).then_inc(s_ea, 1)

            def exps(g, i):
                act.wait_ge(s_nm, 8 * g + i + 1)
                nk = (i + 1) * P
                s = i % 2
                sc = PS[:, 2 * s:2 * s + 2, :].rearrange("p a n -> p (a n)")
                nc.scalar.activation(PR[:, s, 0:nk], sc[:, 0:nk], ACT.Exp, bias=nmax[:, i % 4:i % 4 + 1],
                                     accum_out=rsum[:, i:i + 1]).then_inc(s_ex, 1)

            def head(g, pending):
                for i in range(8):
                    if i == 0 and pending:
                        out_evac(0, 2 * g - 1)
                        evac(7, 12 * (g - 1) + 11)
                    exps(g, i)
                    if i == 4 and pending:
                        out_evac(1, 2 * g)
                    if i >= 5:
                        evac(i - 1, 12 * g + 2 * (i - 5) + 5)

            def attention(b):
                head(8 * b, False)
                with act.Fori(8 * b + 1, 8 * b + 8) as g:
                    head(g, True)
                g = 8 * b + 8
                out_evac(0, 2 * g - 1)
                evac(7, 12 * (g - 1) + 11)
                out_evac(1, 2 * g)

            def experts(m):
                _, _, f_n = MOE[m]

                def hidden(j, i):
                    act.wait_ge(s_mhp[m], j + 1)
                    if m == 0:
                        for c in range(f_n):
                            r = nc.scalar.activation(MH[:, i, c, :], PS[:, 5 + i, c * P:(c + 1) * P], ACT.Gelu,
                                                     bias=mb1[:, i, c:c + 1])
                    else:
                        r = nc.scalar.activation(MH[:, i, :, :], bank(5 + i).rearrange("p (c n) -> p c n", n=P), ACT.Relu)
                    r.then_inc(s_mh[m], 1)

                def store(p, s):
                    act.wait_ge(s_my[m], p + 1)
                    act.dma_start(ys[m][bass.ds(p * 2 * P, 2 * P), :].rearrange("(i p) d -> p i d", p=P), MY[:, s, :, :]
                                  ).then_inc(s_mo[m][s], 16)

                with act.Fori(0, PAIRS[m] // 2) as r:
                    for s in range(2):
                        p = 2 * r + s
                        hidden(2 * p, 0)
                        hidden(2 * p + 1, 1)
                        store(p, s)

            attention(0)
            experts(0)
            attention(1)
            deviation(1)
            gate_exp(1)
            act.wait_ge(s_wsc, 16 * 8)
            nc.scalar.activation(a_sc[:], a_lg[:], ACT.Exp).then_inc(s_as, 1)
            for b in range(B):
                for q in range(8):
                    act.wait_ge(s_up, 8 * b + q + 1)
                    c, hf = q // 2, q % 2
                    dst = (UT if c < 2 else SR)[:, c % 2, hf * BANK:(hf + 1) * BANK]
                    if b and q == 0:
                        act.wait_ge(s_yt, 2 * b)
                    nc.scalar.activation(dst, bank(4 + q % 4), ACT.Silu).then_inc(s_ue2, 1)
                act.wait_ge(s_dr, 4 * b + 4)
                nc.scalar.activation(DA[:], DL[:], ACT.Abs).then_inc(s_da1, 1)
                act.wait_ge(s_da1, 2 * b + 1)
                nc.scalar.activation(DB[:], DA[:], ACT.Exp, scale=-1.0).then_inc(s_da1, 1)
                act.wait_ge(s_dw, b + 1)
                nc.scalar.activation(HS[:], DA[:], ACT.Ln).then_inc(s_dl, 1)
                act.wait_ge(s_du, b + 1)

                def decay(n, c, free):
                    if free:
                        act.wait_ge(s_sn, 32 * b + 2 * n + c - 1)
                    nc.scalar.activation(DA[:, c, :], DL[:, c, :], ACT.Exp,
                                         scale=a_sc[:, c, bass.ds(n, 1)]).then_inc(s_dA, 1)

                decay(0, 0, False)
                decay(0, 1, False)
                with act.Fori(1, STATE) as n:
                    decay(n, 0, True)
                    decay(n, 1, True)
            experts(1)

        @block.tensor
        def _(pe):
            mm = nc.tensor.matmul

            def transposes(ph):
                for q in range(4):
                    pe.wait_ge(s_xn, 4 * ph + q + 1)
                    for t in range(4):
                        r = nc.tensor.transpose(PS[:, 4 + q, t * P:(t + 1) * P], XN[:, 4 * q + t, :], ident)
                    r.then_inc(s_tp, 1)

            def logits(ph):
                e_n = MOE[ph][0]
                pe.wait_ge(s_xnt, 4 * ph + 4)
                for t in range(NT):
                    r = mm(PS[:, 0, t * e_n:(t + 1) * e_n], XNT[:, t * P:(t + 1) * P], wgate[ph][:], start=True, stop=True)
                r.then_inc(s_lg, 1)

            def ranks(ph):
                n = NT * MOE[ph][0]
                pe.wait_ge(s_ohb, ph + 1)
                mm(PS[:, 2, 0:n], beforeb[:], ohb[:, 0:n], start=True, stop=True)
                mm(PS[:, 3, 0:n], onesb[:], ohb[:, 0:n], start=True, stop=True).then_inc(s_rk, 1)

            pe.wait_ge(s_cst, 16)
            transposes(0)
            pe.wait_ge(s_wat, 16 * 8)
            logits(0)
            for q in range(4):
                mm(bank(1 + q), wkv[:, 0:D], XNT[:, q * BANK:(q + 1) * BANK], start=True, stop=True).then_inc(s_kp, 1)
            pe.wait_ge(s_cnv, 1)
            for q in range(4):
                if q == 3:
                    pe.wait_ge(s_ke, 1)
                bk_ = (5, 6, 7, 1)[q]
                for t in range(4):
                    dst = PS[:, bk_, t * D:(t + 1) * D]
                    mm(dst, XNT[:, (4 * q + t) * P:(4 * q + t + 1) * P], wkv[:, D:2 * D], start=True, stop=False)
                    r = mm(dst, ones1[:], bv[:], start=False, stop=True)
                r.then_inc(s_vp, 1)
            pe.wait_ge(s_ke, 4)
            ranks(0)
            pe.wait_ge(s_ve, 4)
            pe.wait_ge(s_rkr, 1)

            def wait_if(s, v, on=True):
                if on:
                    pe.wait_ge(s, v)

            def query(g, b, hf):
                if hf == 0:
                    pass
                i = hf
                r = mm(bank(7), wq[:, q_slot[0], :], XNT[:, b * T + hf * BANK:b * T + (hf + 1) * BANK], start=True, stop=True)
                r.then_inc(s_qp, 1)

            q_slot = [0]

            def scores(g, b, i, free):
                if free:
                    pe.wait_ge(s_ex, 8 * g + i - 1)
                nk = (i + 1) * P
                s = 2 * (i % 2)
                q = QT[:, i * P:(i + 1) * P]
                mm(PS[:, s, 0:min(nk, BANK)], q, KT[:, b, 0:min(nk, BANK)], start=True, stop=True)
                if i >= 4:
                    mm(PS[:, s + 1, 0:nk - BANK], q, KT[:, b, BANK:nk], start=True, stop=True)
                mm(PS[:, s + i // 4, (i % 4) * P:(i % 4 + 1) * P], identb[:], causalb[:], start=False, stop=True,
                   skip_group_check=True).then_inc(s_qk, 1)

            def turn(g, i, first=False):
                pe.wait_ge(s_ex, 8 * g + i + 1)
                for part in range(1 if i < 4 else 2):
                    c = i if i < 4 else 4 + 2 * (i - 4) + part
                    prev = c - 2
                    if prev < 0:
                        if not first:
                            pe.wait_ge(*((s_ea, 4 * g) if c == 0 else (s_ed, 8 * g)))
                    elif prev < 4 or prev % 2:
                        pe.wait_ge(s_ed, 8 * g + (prev if prev < 4 else 4 + (prev - 5) // 2) + 1)
                    else:
                        pe.wait_ge(s_ea, 4 * g + (prev - 4) // 2 + 1)
                    lo, hi = 4 * part, min(i + 1, 4 * part + 4)
                    for j in range(lo, hi):
                        r = nc.tensor.transpose(PS[:, 4 + c % 2, (j - lo) * P:(j - lo + 1) * P],
                                                PR[:, i % 2, j * P:(j + 1) * P], ident)
                    r.then_inc(s_tc, 1)

            def out_a(g, b, part, free=True):
                if part == 0:
                    pe.wait_ge(s_ed, 8 * g + 4)
                    if free:
                        pe.wait_ge(s_ue, 2 * g)
                j = part
                r = mm(PS[:, 6, j * P:BANK], V[:, b * TB + j, :], PTa[:, j, j * P:BANK], start=(j == 0), stop=True,
                       skip_group_check=True)
                if part == 3:
                    r.then_inc(s_pv, 1)

            def out_b(g, b, part):
                if part == 0:
                    pe.wait_ge(s_ea, 4 * g + 4)
                    pe.wait_ge(s_ue, 2 * g + 1)
                if part == 2:
                    pe.wait_ge(s_ed, 8 * g + 8)
                for j in (2 * part, 2 * part + 1):
                    lo = max(0, j - 4) * P
                    r = mm(PS[:, 6, lo:BANK], V[:, b * TB + j, :], PTb[:, j, lo:BANK], start=(j == 0), stop=True,
                           skip_group_check=True)
                if part == 3:
                    r.then_inc(s_pv, 1)

            def project(g, h, s):
                pe.wait_ge(s_ue, 2 * g + 1 + s)
                for t in range(4):
                    r = mm(PS[:, 7, t * P:(t + 1) * P], OT[:, s, t * P:(t + 1) * P],
                           wo[:, bass.ds(h, 1), :].rearrange("p o d -> p (o d)"), start=True, stop=True)
                r.then_inc(s_wo, 1)

            def head(g, b, h, slot_, slot_count, pending):
                q_slot[0] = slot_
                pe.wait_ge(s_wq[slot_], slot_count)
                if pending:
                    pe.wait_ge(s_we, 2 * (g - 1))
                query(g, b, 0)
                if pending:
                    out_a(g - 1, b, 3)
                    turn(g - 1, 7)
                pe.wait_ge(s_qe, 2 * g + 1)
                for i in range(8):
                    if i == 4:
                        pe.wait_ge(s_qe, 2 * g + 2)
                    scores(g, b, i, not (isinstance(g, int) and g == 0 and i < 2))
                    if pending and 1 <= i <= 4:
                        out_b(g - 1, b, i - 1)
                    if i >= 5:
                        out_a(g, b, i - 5, pending)
                    if i >= 1:
                        turn(g, i - 1, isinstance(g, int) and g == 0)
                    if i == 1 and pending:
                        pe.wait_ge(s_qe, 2 * g + 1)
                        project(g - 1, h - 1, 0)
                    if i == 2:
                        if pending:
                            pe.wait_ge(s_we, 2 * g - 1)
                        query(g, b, 1)
                    if i == 5 and pending:
                        pe.wait_ge(s_qe, 2 * g + 2)
                        project(g - 1, h - 1, 1)

            def attention(b):
                head(8 * b, b, 0, 0, 64 * b + 16, False)
                head(8 * b + 1, b, 1, 1, 64 * b + 16, True)
                with pe.Fori(1, 4) as r:
                    head(8 * b + 2 * r, b, 2 * r, 0, 64 * b + 16 * r + 16, True)
                    head(8 * b + 2 * r + 1, b, 2 * r + 1, 1, 64 * b + 16 * r + 16, True)
                g = 8 * b + 7
                out_a(g, b, 3)
                turn(g, 7)
                for part in range(4):
                    out_b(g, b, part)
                pe.wait_ge(s_we, 2 * g)
                project(g, 7, 0)
                pe.wait_ge(s_we, 2 * g + 1)
                project(g, 7, 1)
                pe.wait_ge(s_we, 2 * g + 2)

            def experts(m):
                _, _, f_n = MOE[m]
                n_w = 64 if m == 0 else 32

                def pair(p, s, times, first):
                    free = not (first and s == 0)
                    pe.wait_ge(s_mx[m][s], 16 * times)
                    if free:
                        pe.wait_ge(s_mt[m], p)
                    for i in range(2):
                        r = nc.tensor.transpose(PS[:, 4, i * P:(i + 1) * P], MX[:, s, i, :], ident)
                    r.then_inc(s_mtp[m], 1)
                    pe.wait_ge(s_mt[m], p + 1)
                    for i in range(2):
                        pe.wait_ge(s_mw[m][i], n_w * p + n_w)
                        if free:
                            pe.wait_ge(s_mh[m], 2 * p + i - 1)
                        for c in range(f_n):
                            r = mm(PS[:, 5 + i, c * P:(c + 1) * P], mw1[:, i, c * P:(c + 1) * P], MXT[:, i, :],
                                   start=True, stop=True)
                        r.then_inc(s_mhp[m], 1)
                    if free:
                        pe.wait_ge(s_my[m], p)
                    for i in range(2):
                        pe.wait_ge(s_mh[m], 2 * p + i + 1)
                        dst = PS[:, 7, i * P:(i + 1) * P]
                        if m == 0:
                            mm(dst, ones1[:], mb2[:, i, :], start=True, stop=False)
                        for c in range(f_n):
                            r = mm(dst, MH[:, i, c, :], mw2[:, i, c, :], start=(m == 1 and c == 0), stop=(c == f_n - 1))
                        r.then_inc(s_myp[m], 1)

                pair(0, 0, 1, True)
                pair(1, 1, 1, True)
                with pe.Fori(1, PAIRS[m] // 2) as r:
                    pair(2 * r, 0, r + 1, False)
                    pair(2 * r + 1, 1, r + 1, False)
                pe.wait_ge(s_my[m], PAIRS[m])

            attention(0)
            experts(0)
            attention(1)
            transposes(1)
            logits(1)
            ranks(1)
            pe.wait_ge(s_wsc, 16 * 8)
            pe.wait_ge(s_rkr, 2)
            for b in range(B):
                for q in range(8):
                    c, hf = q // 2, q % 2
                    if q >= 4 or b:
                        pe.wait_ge(s_ue2, 8 * b + q - 3 if q >= 4 else 8 * b)
                    if b and q < 2:
                        pe.wait_ge(s_oe, 2 * b)
                    if b and q >= 2:
                        pe.wait_ge(s_dr, 4 * b)
                    mm(bank(4 + q % 4), w_in[:, c * P:(c + 1) * P], XNT[:, b * T + hf * BANK:b * T + (hf + 1) * BANK],
                       start=True, stop=True).then_inc(s_up, 1)
                pe.wait_ge(s_ue2, 8 * b + 8)
                for q in range(4):
                    c, hf = q // 2, q % 2
                    for k in range(2):
                        r = mm(bank(4 + q), w_dl[:, k, c * P:(c + 1) * P], UT[:, k, hf * BANK:(hf + 1) * BANK],
                               start=(k == 0), stop=(k == 1))
                    r.then_inc(s_dp, 1)
                if b:
                    pe.wait_ge(s_hc, 32 * b)
                    pe.wait_ge(s_db, 32 * b)
                for hf in range(2):
                    for k in range(2):
                        r = mm(PS[0:32, hf, :], w_bc[:, k, :], UT[:, k, hf * BANK:(hf + 1) * BANK],
                               start=(k == 0), stop=(k == 1))
                r.then_inc(s_bp, 1)
                pe.wait_ge(s_r3, b + 1)
                pe.wait_ge(s_cnv, 2)

                def spread(n, free):
                    if free:
                        pe.wait_ge(s_db, 32 * b + 2 * n)
                    for hf in range(2):
                        r = mm(bank(hf), pickb[:, bass.ds(n, 1), :].rearrange("p o m -> p (o m)"), R3[:, hf * BANK:(hf + 1) * BANK],
                               start=True, stop=True)
                    r.then_inc(s_b, 1)
                    if free:
                        pe.wait_ge(s_hc, 32 * b + 2 * n)
                    for hf in range(2):
                        r = mm(bank(2 + hf), pickb[:, bass.ds(n + STATE, 1), :].rearrange("p o m -> p (o m)"),
                               R3[:, hf * BANK:(hf + 1) * BANK], start=True, stop=True)
                    r.then_inc(s_c, 1)

                spread(0, False)
                with pe.Fori(1, STATE) as n:
                    spread(n, True)
                pe.wait_ge(s_yt, 2 * b + 2)
                for q in range(2):
                    for t in range(4):
                        tt = 4 * q + t
                        for k in range(2):
                            r = mm(PS[:, 4 + q, t * P:(t + 1) * P], SR[:, k, tt * P:(tt + 1) * P], w_out[:, k, :],
                                   start=(k == 0), stop=(k == 1))
                    r.then_inc(s_op, 1)
            pe.wait_ge(s_oe, 4)
            experts(1)

        @block.vector
        def _(dve):
            count = [0]

            def link(ins):
                count[0] += 1
                ins.then_inc(s_v, 1)
                dve.wait_ge(s_v, count[0])

            ts, tt = nc.vector.tensor_scalar, nc.vector.tensor_tensor
            stt, cp = nc.vector.scalar_tensor_tensor, nc.vector.tensor_copy

            def normalise(ph):
                for t in range(NT):
                    if ph == 0 and t % 4 == 0:
                        dve.wait_ge(s_x, 16 * (t // 4 + 1))
                    r = nc.vector.bn_stats(stats[:, t, :], X[:, t, :])
                link(r)
                for t in range(NT):
                    r = nc.vector.bn_aggr(mv[:, t, :], stats[:, t, :])
                link(r)
                ve, sd, r0, a, r1 = (lnt[:, i, :] for i in range(5))
                ts(ve, mv[:, :, 1], EPS, None, ALU.add).then_inc(s_var, 1)
                dve.wait_ge(s_sd, ph + 1)
                link(nc.vector.reciprocal(r0, sd))
                link(tt(a, r0, r0, ALU.mult))
                link(tt(a, a, ve, ALU.mult))
                link(ts(a, a, -0.5, 1.5, ALU.mult, ALU.add))
                link(tt(r1, r0, a, ALU.mult))
                if ph:
                    dve.wait_ge(s_sc[0], 16 * NT)
                for t in range(NT):
                    r = ts(XN[:, t, :], X[:, t, :], mv[:, t, 0:1], lnt[:, 4, t:t + 1], ALU.subtract, ALU.mult)
                    if t % 4 == 3:
                        r.then_inc(s_xn, 1)
                for q in range(4):
                    dve.wait_ge(s_tp, 4 * ph + q + 1)
                    cp(XNT[:, q * BANK:(q + 1) * BANK], bank(4 + q)).then_inc(s_xnt, 1)

            def route(m, between):
                e_n, k_n, _ = MOE[m]
                n = NT * e_n
                v3 = lambda ap: ap.rearrange("p (t e) -> p t e", e=e_n)
                L = v3(lg[:, 0:n])
                dve.wait_ge(s_lg, m + 1)
                cp(lg[:, 0:n], PS[:, 0, 0:n]).then_inc(s_lgr, 1)
                dve.wait_ge(s_lgr, m + 1)
                iota = bc(cst["iota"][:, 0:e_n], 1, NT)
                mx = [rs1[:, 0, :], rs1[:, 1, :]]
                for k in range(k_n):
                    src = L
                    if k:
                        link(stt(v3(rt[:, 0, 0:n]), v3(oh[:, 0, 0:n]), -KEPT, L, ALU.mult, ALU.add))
                        src = v3(rt[:, 0, 0:n])
                    link(nc.vector.tensor_reduce(mx[k], src, AX_X, ALU.max))
                    link(tt(v3(rt[:, 1, 0:n]), src, bc(mx[k], 2, e_n), ALU.is_equal))
                    link(tt(v3(rt[:, 2, 0:n]), v3(rt[:, 1, 0:n]), iota, ALU.mult))
                    link(nc.vector.tensor_reduce(rs1[:, 2 + k, :], v3(rt[:, 2, 0:n]), AX_X, ALU.min))
                    link(tt(v3(oh[:, k, 0:n]), iota, bc(rs1[:, 2 + k, :], 2, e_n), ALU.is_equal))
                if k_n == 1:
                    cp(ohb[:, 0:n], oh[:, 0, 0:n]).then_inc(s_ohb, 1)
                    tt(v3(rt[:, 0, 0:n]), L, bc(mx[0], 2, e_n), ALU.subtract).then_inc(s_ein, 1)
                else:
                    tt(ohb[:, 0:n], oh[:, 0, 0:n], oh[:, 1, 0:n], ALU.add).then_inc(s_ohb, 1)
                    tt(rs1[:, 5, :], mx[1], mx[0], ALU.subtract).then_inc(s_ein, 1)
                between()
                dve.wait_ge(s_eout, m + 1)
                if k_n == 1:
                    link(nc.vector.tensor_reduce(rs1[:, 4, :], v3(rt[:, 1, 0:n]), AX_X, ALU.add))
                    link(nc.vector.reciprocal(wsel[m][:, 0, :], rs1[:, 4, :]))
                else:
                    link(ts(rs1[:, 4, :], rs1[:, 6, :], 1.0, None, ALU.add))
                    link(nc.vector.reciprocal(wsel[m][:, 0, :], rs1[:, 4, :]))
                    link(tt(wsel[m][:, 1, :], wsel[m][:, 0, :], rs1[:, 6, :], ALU.mult))
                dve.wait_ge(s_rk, m + 1)
                et = lambda ap: ap.rearrange("p (e t) -> p e t", t=NT)
                link(cp(et(rt[:, 2, 0:n]), PS[:, 3, 0:n].rearrange("p (t e) -> p e t", e=e_n)))
                link(nc.vector.tensor_tensor_scan(rt[:, 3, 0:n], seg[m][:], rt[:, 2, 0:n], 0.0, ALU.mult, ALU.add))
                total = et(rt[:, 3, 0:n])[:, :, NT - 1]
                link(ts(rei[:, 0, 0:e_n], total, float(P - 1), None, ALU.add))
                link(ts(rei[:, 1, 0:e_n], rei[:, 0, 0:e_n], 7, 7, ALU.logical_shift_right, ALU.logical_shift_left))
                link(cp(re1[:, 0, 0:e_n], rei[:, 1, 0:e_n]))
                link(nc.vector.tensor_tensor_scan(re1[:, 1, 0:e_n], re1[:, 3, 0:e_n], re1[:, 0, 0:e_n], 0.0, ALU.mult, ALU.add))
                link(tt(re1[:, 2, 0:e_n], re1[:, 1, 0:e_n], re1[:, 0, 0:e_n], ALU.subtract))
                link(tt(rt[:, 3, 0:n], rt[:, 3, 0:n], rt[:, 2, 0:n], ALU.subtract))
                r = tt(v3(rt[:, 4, 0:n]), v3(PS[:, 2, 0:n]), rt[:, 3, 0:n].rearrange("p (e t) -> p t e", t=NT), ALU.add)
                r.then_inc(s_rkr, 1)
                dve.wait_ge(s_rkr, m + 1)
                link(tt(v3(rt[:, 4, 0:n]), v3(rt[:, 4, 0:n]), bc(re1[:, 2, 0:e_n], 1, NT), ALU.add))
                for k in range(k_n):
                    link(tt(rt[:, 2, 0:n], rt[:, 4, 0:n], oh[:, k, 0:n], ALU.mult))
                    link(nc.vector.tensor_reduce(rs1[:, 7 + k, :], v3(rt[:, 2, 0:n]), AX_X, ALU.add))
                    r = cp(slot[m][:, k, :], rs1[:, 7 + k, :])
                r.then_inc(s_slot, 1)
                tn = TILES[m]
                cmp = tl[:, 0:tn * e_n].rearrange("p (j e) -> p j e", e=e_n)
                link(tt(cmp, bc(re1[:, 1, 0:e_n], 1, tn), bc(cst["first"][:, 0:tn], 2, e_n), ALU.is_le))
                link(nc.vector.tensor_reduce(lg[:, 0:tn], cmp, AX_X, ALU.add))
                ts(eid[m][:], lg[:, 0:tn], float(e_n - 1), None, ALU.min).then_inc(s_eid, 1)

            nc.vector.memset(onesb[:], 1.0)
            nc.vector.memset(ones1[:], 1.0)
            link(nc.vector.memset(re1[:, 3, :], 1.0))
            for m in range(2):
                link(nc.vector.memset(seg[m][:], 1.0))
                link(nc.vector.memset(seg[m][:].rearrange("p (e t) -> p e t", t=NT)[:, :, 0:1], 0.0))
            dve.wait_ge(s_cst, 16)
            cp(identb[:], ident)
            cp(causalb[:], cst["causal"])
            cp(beforeb[:], cst["before"]).then_inc(s_cnv, 1)
            normalise(0)

            def keys():
                dve.wait_ge(s_wat, 16 * 8)
                for q in range(4):
                    dve.wait_ge(s_kp, q + 1)
                    b, hf = q // 2, q % 2
                    k = KT[:, b, hf * BANK:(hf + 1) * BANK]
                    link(stt(k, bank(1 + q), bk[:, 0:1], peT[:, hf * BANK:(hf + 1) * BANK], ALU.add, ALU.add))
                    ts(k, k, SCALE, None, ALU.mult).then_inc(s_ke, 1)

            route(0, keys)

            def q_evac(g, hf):
                dve.wait_ge(s_qp, 2 * g + hf + 1)
                h = g - 8 * batch[0]
                sl = slice(hf * BANK, (hf + 1) * BANK)
                stt(QT[:, sl], bank(7), bq[:, bass.ds(h, 1)], peT[:, sl], ALU.add, ALU.add).then_inc(s_qe, 1)

            batch = [0]

            def neg_max(g, i):
                dve.wait_ge(s_qk, 8 * g + i + 1)
                s = i % 2
                sc = PS[:, 2 * s:2 * s + 2, :].rearrange("p a n -> p (a n)")
                nc.vector.tensor_reduce(nmax[:, i % 4:i % 4 + 1], sc[:, 0:(i + 1) * P], AX_X, ALU.max,
                                        negate=True).then_inc(s_nm, 1)

            def evac(g, i):
                c = i if i < 4 else 4 + 2 * (i - 4) + 1
                dve.wait_ge(s_tc, 12 * g + c + 1)
                n = i + 1 if i < 4 else i - 3
                src = PS[:, 4 + c % 2, 0:n * P].rearrange("p (j q) -> p j q", q=P)
                dst = PTa[:, 0:n, i * P:(i + 1) * P] if i < 4 else PTb[:, 4:4 + n, (i - 4) * P:(i - 3) * P]
                cp(dst, src).then_inc(s_ed, 1)

            def inverse(g, s):
                dve.wait_ge(s_ex, 8 * g + 4 + 4 * s)
                nc.vector.reciprocal(rinv[:, 4 * s:4 * s + 4], rsum[:, 4 * s:4 * s + 4]).then_inc(s_ri, 1)

            def add_out(g, s, x_prev):
                dve.wait_ge(s_wo, 2 * g + 1 + s)
                dve.wait_ge(s_ri, 2 * g + 1 + s)
                if x_prev:
                    dve.wait_ge(s_we, 2 * g + s - 1)
                for t in range(4):
                    q = 4 * s + t
                    x = X[:, 8 * batch[0] + q, :]
                    r = stt(x, PS[:, 7, t * P:(t + 1) * P], rinv[:, q:q + 1], x, ALU.mult, ALU.add)
                r.then_inc(s_we, 1)

            def head(g, pending, x_prev=True):
                q_evac(g, 0)
                if pending:
                    evac(g - 1, 7)
                    inverse(g - 1, 1)
                for i in range(8):
                    neg_max(g, i)
                    if i >= 1 and i < 8:
                        evac(g, i - 1)
                    if i == 1 and pending:
                        add_out(g - 1, 0, x_prev)
                    if i == 2:
                        q_evac(g, 1)
                    if i == 4:
                        inverse(g, 0)
                    if i == 5 and pending:
                        add_out(g - 1, 1, x_prev)

            def attention(b):
                batch[0] = b
                head(8 * b, False)
                head(8 * b + 1, True, False)
                with dve.Fori(8 * b + 2, 8 * b + 8) as g:
                    head(g, True)
                g = 8 * b + 7
                evac(g, 7)
                inverse(g, 1)
                add_out(g, 0, True)
                add_out(g, 1, True)

            def experts(m):
                def pair(p, s, times, first):
                    dve.wait_ge(s_mtp[m], p + 1)
                    cp(MXT[:], PS[:, 4, 0:2 * P].rearrange("p (i n) -> p i n", i=2)).then_inc(s_mt[m], 1)
                    dve.wait_ge(s_myp[m], 2 * p + 2)
                    if not first:
                        dve.wait_ge(s_mo[m][s], 16 * times)
                    elif m:
                        dve.wait_ge(s_mo[0][s], 16 * (PAIRS[0] // 2))
                    cp(MY[:, s, :, :], PS[:, 7, 0:2 * P].rearrange("p (i n) -> p i n", i=2)).then_inc(s_my[m], 1)

                pair(0, 0, 0, True)
                pair(1, 1, 0, True)
                with dve.Fori(1, PAIRS[m] // 2) as r:
                    pair(2 * r, 0, r, False)
                    pair(2 * r + 1, 1, r, False)

            def combine(m):
                for k in range(MOE[m][1]):
                    dve.wait_ge(s_ga, 16 * 16 * (m + k + 1))
                    for t in range(NT):
                        if m + k:
                            dve.wait_ge(s_gu, 16 * (m + k - 1) + t + 1)
                        stt(X[:, t, :], GA[:, t // 4, (t % 4) * D:(t % 4 + 1) * D], wsel[m][:, k, t:t + 1], X[:, t, :],
                            ALU.mult, ALU.add).then_inc(s_gu, 1)

            attention(0)
            experts(0)
            cp(pickb[:], bc(cst["pick"], 2, P)).then_inc(s_cnv, 1)
            attention(1)
            dve.wait_ge(s_we, 32)
            combine(0)
            dve.wait_ge(s_gu, 16)
            normalise(1)
            route(1, lambda: None)
            dve.wait_ge(s_as, 1)
            link(ts(a_sc[:], a_sc[:], -1.0, None, ALU.mult))
            link(nc.vector.memset(R3[96:128, :], 0.0))
            for b in range(B):
                for q in range(4):
                    dve.wait_ge(s_dp, 4 * b + q + 1)
                    c, hf = q // 2, q % 2
                    r = ts(DL[:, c, hf * BANK:(hf + 1) * BANK], bank(4 + q), b_dl[:, c:c + 1], None, ALU.add)
                    r.then_inc(s_dr, 1)
                dve.wait_ge(s_da1, 2 * b + 2)
                ts(DA[:], DB[:], 1.0, None, ALU.add).then_inc(s_dw, 1)
                dve.wait_ge(s_dw, b + 1)
                link(stt(DU[:], DA[:], 1.0, DB[:], ALU.subtract, ALU.subtract))
                dve.wait_ge(s_dr, 4 * b + 4)
                link(stt(DL[:], DL[:], 0.0, DU[:], ALU.max, ALU.subtract))
                dve.wait_ge(s_dl, b + 1)
                link(tt(DL[:], DL[:], HS[:], ALU.add))
                dve.wait_ge(s_ue2, 8 * b + 8)
                r = tt(DU[:], DL[:], UT[:], ALU.mult)
                r.then_inc(s_du, 1)
                dve.wait_ge(s_du, b + 1)
                dve.wait_ge(s_bp, b + 1)
                bcr = PS[0:32, 0:2, :].rearrange("p a n -> p (a n)")
                rest, mid = DB[0:32, 0, :], HS[0:32, 0, 0:BANK].bitcast(BF16)
                link(cp(R3[0:32, :], bcr))
                link(tt(rest, bcr, R3[0:32, :], ALU.subtract))
                link(cp(mid, rest))
                link(cp(R3[32:64, :], mid))
                link(tt(rest, rest, mid, ALU.subtract))
                cp(R3[64:96, :], rest).then_inc(s_r3, 1)
                dve.wait_ge(s_r3, b + 1)

                def state(n, free):
                    u = 32 * b + 2 * n
                    dve.wait_ge(s_b, 16 * b + n + 1)
                    for c in range(2):
                        if free:
                            dve.wait_ge(s_sn, u + c - 1)
                        spread = PS[:, 0:2, :].rearrange("p a n -> p (a n)")
                        tt(DB[:, c, :], DU[:, c, :], spread, ALU.mult).then_inc(s_db, 1)
                    for c in range(2):
                        dve.wait_ge(s_dA, u + c + 1)
                        dve.wait_ge(s_db, u + c + 1)
                        if free:
                            dve.wait_ge(s_hc, u + c - 1)
                        nc.vector.tensor_tensor_scan(HS[:, c, :], DA[:, c, :], DB[:, c, :], 0.0, ALU.mult,
                                                     ALU.add).then_inc(s_sn, 1)
                    dve.wait_ge(s_c, 16 * b + n + 1)
                    for c in range(2):
                        dve.wait_ge(s_sn, u + c + 1)
                        if free:
                            dve.wait_ge(s_ya, u + c - 1)
                        spread = PS[:, 2:4, :].rearrange("p a n -> p (a n)")
                        tt(HC[:, c, :], HS[:, c, :], spread, ALU.mult).then_inc(s_hc, 1)

                state(0, False)
                with dve.Fori(1, STATE) as n:
                    state(n, True)
                for c in range(2):
                    dve.wait_ge(s_ya, 32 * b + 32)
                    link(stt(YA[:, c, :], UT[:, c, :], d_par[:, c:c + 1], YA[:, c, :], ALU.mult, ALU.add))
                    tt(SR[:, c, :], YA[:, c, :], SR[:, c, :], ALU.mult).then_inc(s_yt, 1)
                for q in range(2):
                    dve.wait_ge(s_op, 2 * b + q + 1)
                    x = X[:, 8 * b + 4 * q:8 * b + 4 * q + 4, :].rearrange("p t d -> p (t d)")
                    tt(x, bank(4 + q), x, ALU.add).then_inc(s_oe, 1)
            experts(1)
            dve.wait_ge(s_oe, 4)
            combine(1)


def kernel(**inputs):
    import concourse.bacc as bacc
    from concourse.bass_utils import run_bass_kernel_spmd as run

    get = lambda n: np.asarray(inputs[n])
    by_partition = lambda a: a.reshape(-1, P).T
    cst, _ = small_constants()
    data = {
        "x": get("L0_attn_x"), "Wkv": get("L0_attn_Wkv"), "bkv": get("L0_attn_bkv"), "bq": by_partition(get("L0_attn_bq")),
        "WqH": get("L0_attn_Wq").reshape(D, HEADS, D).transpose(1, 0, 2), "Wo": get("L0_attn_Wo"),
        "router_w": get("L0_ffn_router_w"), "w1_0": get("L0_ffn_w1"), "b1": get("L0_ffn_b1").reshape(-1, 2, P).transpose(0, 2, 1),
        "w2_0": get("L0_ffn_w2"), "b2": get("L0_ffn_b2"), "W_in": get("L1_attn_W_in"),
        "W_delta": get("L1_attn_W_delta"), "b_delta": by_partition(get("L1_attn_b_delta")), "W_B": get("L1_attn_W_B"),
        "W_C": get("L1_attn_W_C"), "A_log": get("L1_attn_A_log"), "D_param": by_partition(get("L1_attn_D_param")),
        "W_out": get("L1_attn_W_out"), "gate_wT": get("L1_ffn_gate_w").T,
        "w1_1": get("L1_ffn_w1").transpose(0, 2, 1), "w2_1": get("L1_ffn_w2").transpose(0, 2, 1),
        "cst": cst, "peT": positions(),
    }
    nc = bacc.Bacc("TRN2", target_bir_lowering=False, num_devices=1)
    arrays, args = {}, {}
    for name, a in data.items():
        a = np.ascontiguousarray(a)
        arrays[f"in_{name}"] = a
        args[name] = nc.dram_tensor(f"in_{name}", a.shape, mybir.dt.from_np(a.dtype), kind="ExternalInput").ap()
    out = nc.dram_tensor("out_0", (B, T, D), F32, kind="ExternalOutput").ap()
    scratch = {
        "rows_in": [nc.dram_tensor(f"rows_in{m}", (TILES[m] * P, D), F32, kind="Internal").ap() for m in range(2)],
        "rows_out": [nc.dram_tensor(f"rows_out{m}", (TILES[m] * P, D), F32, kind="Internal").ap() for m in range(2)],
    }
    build(nc, args, out, scratch)
    r = run(nc, [arrays], core_ids=[0])
    return r.results[0]["out_0"]
```

```python
from contextlib import ExitStack

import numpy as np

import concourse.bass as bass
from concourse import mybir

ALU = mybir.AluOpType
ACT = mybir.ActivationFunctionType
F32 = mybir.dt.float32
BF16 = mybir.dt.bfloat16
F32R = mybir.dt.float32r
I32 = mybir.dt.int32
U32 = mybir.dt.uint32
AX_X = mybir.AxisListType.X

P = 128
B, T, D = 2, 1024, 128
NT = B * T // P
TB = T // P
BANK = 512
HEADS = 8
EPS = 1e-5
SCALE = float(D) ** -0.5
MASKED = -1e30
STATE = 16
INNER = 2
KEPT = 3e38

MOE = [(14, 1, 2), (8, 2, 4)]
TILES = [4 * -(-((B * T * k + e * (P - 1)) // P) // 4) for e, k, _ in MOE]
QUADS = TILES[0] // 4
PAIRS = TILES[1] // 2
LATE = PAIRS - (STATE - 6)
EARLY = 6
W_ROW = [2 * f * P + (2 + D if m == 0 else 0) for m, (_, _, f) in enumerate(MOE)]


def small_constants():
    k, m = np.arange(P)[:, None], np.arange(P)[None, :]
    parts = {
        "ident": (k == m),
        "causal": np.where(m > k, MASKED, 0.0),
        "before": (k < m),
        "pick": (k % 32 == np.arange(32)[None, :]) & (k < 96),
        "iota": np.broadcast_to(np.arange(16)[None, :] - 16.0, (P, 16)),
        "first": np.broadcast_to(np.arange(max(TILES))[None, :] * P, (P, max(TILES))),
    }
    at, cols, where = 0, [], {}
    for name, a in parts.items():
        a = np.asarray(a, np.float32)
        where[name] = (at, at + a.shape[1])
        at += a.shape[1]
        cols.append(a)
    return np.ascontiguousarray(np.concatenate(cols, 1)), where


def positions():
    pos = np.arange(T, dtype=np.float32)[:, None]
    step = np.exp(np.float32(-np.log(10000.0)) * np.arange(0, D, 2, dtype=np.float32) / np.float32(D))
    angle = pos * step.astype(np.float32)[None, :]
    pe = np.zeros((T, D), np.float32)
    pe[:, 0::2] = np.sin(angle)
    pe[:, 1::2] = np.cos(angle)
    return np.ascontiguousarray(pe.T)


def build(nc, A, out, scratch):
    _, WHERE = small_constants()
    with ExitStack() as ctx:
        def sb(name, shape, dt=F32):
            return ctx.enter_context(nc.sbuf_tensor(name, shape, dt))

        def sem(name):
            return ctx.enter_context(nc.semaphore(name))

        X = sb("X", [P, NT, D])
        XN = sb("XN", [P, NT, D])
        XNT = sb("XNT", [P, B * T])
        CST = sb("CST", [P, sum(b - a for a, b in list(WHERE.values())[-1:]) + list(WHERE.values())[-1][0]])
        cst = {n: CST[:, a:b] for n, (a, b) in WHERE.items()}
        ident = cst["ident"]
        identb = sb("identb", [P, P], BF16)
        causalb = sb("causalb", [P, P], BF16)
        beforeb = sb("beforeb", [P, P], BF16)
        onesb = sb("onesb", [P, P], BF16)
        ones1 = sb("ones1", [1, P])
        zero = sb("zero", [P, BANK])
        wgate = [sb(f"wgate{m}", [P, MOE[m][0]]) for m in range(2)]
        stats = sb("stats", [P, NT, 6])
        mv = sb("mv", [P, NT, 2])
        lnt = sb("lnt", [P, 6, NT])
        EM = 14
        lg = sb("lg", [P, NT * EM])
        oh = sb("oh", [P, 3, NT * EM])
        ohb = sb("ohb", [P, NT * EM], BF16)
        rt = sb("rt", [P, 5, NT * EM])
        seg = [sb(f"seg{m}", [P, NT * MOE[m][0]]) for m in range(2)]
        rs1 = sb("rs1", [P, 12, NT])
        re1 = sb("re1", [P, 6, 16])
        rei = sb("rei", [P, 2, 16], I32)
        tl = sb("tl", [P, max(TILES) * EM])
        wsel = [sb(f"wsel{m}", [P, MOE[m][1], NT]) for m in range(2)]
        slot = [sb(f"slot{m}", [P, MOE[m][1], NT], U32) for m in range(2)]
        eid = [sb(f"eid{m}", [P, TILES[m]], I32) for m in range(2)]
        mw0 = sb("mw0", [P, 8, W_ROW[0]])
        MX = sb("MX", [P, 8, D])
        MXT = sb("MXT", [P, 8, P])
        MH = sb("MH", [P, 8, P])
        MY = sb("MY", [P, 8, D])
        GA = sb("GA", [P, NT, D])
        w_in = sb("w_in", [P, 4 * D])
        w_dl = sb("w_dl", [P, 2, 2 * D])
        b_dl = sb("b_dl", [P, 2])
        w_bc = sb("w_bc", [P, 2, 32])
        a_lg = sb("a_lg", [P, 2, STATE])
        a_sc = sb("a_sc", [P, 2, STATE])
        d_par = sb("d_par", [P, 2])
        w_out = sb("w_out", [P, 2, D])

        with ExitStack() as first_layer:
            def sb1(name, shape, dt=F32):
                return first_layer.enter_context(nc.sbuf_tensor(name, shape, dt))

            peT = sb1("peT", [P, T])
            wkv = sb1("wkv", [P, 2 * D])
            bk = sb1("bk", [P, 1])
            bv = sb1("bv", [1, D])
            bq = sb1("bq", [P, HEADS])
            wo = sb1("wo", [P, HEADS, D])
            wq = sb1("wq", [P, 2, D])
            KH, KL = sb1("KH", [P, B, T], F32R), sb1("KL", [P, B, T], F32R)
            VH, VL = sb1("VH", [P, NT, D], F32R), sb1("VL", [P, NT, D], F32R)
            QH, QL = sb1("QH", [P, T], F32R), sb1("QL", [P, T], F32R)
            QF = sb1("QF", [P, BANK])
            PR = sb1("PR", [P, 2, T])
            PTH, PTL = sb1("PTH", [P, 12, BANK], F32R), sb1("PTL", [P, 12, BANK], F32R)
            OT = sb1("OT", [P, 2, BANK])
            nmax = sb1("nmax", [P, 4])
            rsum = sb1("rsum", [P, TB])
            rinv = sb1("rinv", [P, TB])

        def sb2(name, shape, dt=F32):
            return ctx.enter_context(nc.sbuf_tensor(name, shape, dt))

        pickb = sb2("pickb", [P, 32, P], BF16)
        UT = sb2("UT", [P, 2, T])
        SR = sb2("SR", [P, 2, T])
        DL = sb2("DL", [P, 2, T])
        DU = sb2("DU", [P, 2, T])
        DA = sb2("DA", [P, 2, T])
        DB = sb2("DB", [P, 2, T])
        HS = sb2("HS", [P, 2, T])
        HC = sb2("HC", [P, 2, T])
        YA = sb2("YA", [P, 2, T])
        GB = sb2("GB", [P, NT, D])
        R3 = sb2("R3", [P, T], BF16)
        mw1 = sb2("mw1", [P, 4, W_ROW[1]])
        PS = ctx.enter_context(nc.psum_tensor("PS", [P, 8, BANK], F32))

        def bank(k, n=BANK):
            return PS[:, k, 0:n]

        s_x = sem("x_loaded")
        s_cst = sem("constants_loaded")
        s_cnv = sem("constants_converted")
        s_wat = sem("attention_weights_loaded")
        s_wsc = sem("scan_weights_loaded")
        s_zero = sem("zero_tile_ready")
        s_zf = sem("rows_zeroed")
        s_v = sem("vector_step")
        s_var = sem("variance_ready")
        s_sd = sem("deviation_ready")
        s_xn = sem("normalised_ready")
        s_tp = sem("transposed_in_psum")
        s_xnt = sem("transposed_ready")
        s_lg = sem("logits_in_psum")
        s_lgr = sem("logits_read")
        s_kp = sem("keys_in_psum")
        s_ke = sem("keys_ready")
        s_vp = sem("values_in_psum")
        s_ve = sem("values_ready")
        s_ein = sem("gate_exponent_in")
        s_eout = sem("gate_exponent_out")
        s_ohb = sem("onehot_ready")
        s_rk = sem("ranks_in_psum")
        s_rkr = sem("ranks_read")
        s_slot = sem("slots_ready")
        s_eid = sem("tile_experts_ready")
        s_sc = [sem(f"rows_scattered{m}") for m in range(2)]
        s_wq = [sem(f"wq_loaded{i}") for i in range(2)]
        s_qp = sem("query_in_psum")
        s_qr = sem("query_left_psum")
        s_qh = sem("query_high_ready")
        s_qe = sem("query_ready")
        s_kf = sem("key_summed")
        s_kh = sem("key_high_ready")
        s_vh = sem("value_high_ready")
        s_qk = sem("scores_ready")
        s_nm = sem("negmax_ready")
        s_ex = sem("probs_ready")
        s_tc = sem("probs_transposed")
        s_ea = sem("probsT_high_ready")
        s_ed = sem("probsT_ready")
        s_pv = sem("head_out_in_psum")
        s_ue = sem("head_out_ready")
        s_ri = sem("inverse_sum_ready")
        s_wo = sem("projected_in_psum")
        s_we = sem("projected_added")
        s_mw = [[sem(f"expert_weights{m}{i}") for i in range(2)] for m in range(2)]
        s_mx = [[sem(f"expert_rows{m}{i}") for i in range(2)] for m in range(2)]
        s_mtp = [sem(f"expert_rowsT_in_psum{m}") for m in range(2)]
        s_mt = [sem(f"expert_rowsT_ready{m}") for m in range(2)]
        s_mhp = [sem(f"expert_hidden_in_psum{m}") for m in range(2)]
        s_mh = [sem(f"expert_hidden_ready{m}") for m in range(2)]
        s_myp = [sem(f"expert_out_in_psum{m}") for m in range(2)]
        s_my = [sem(f"expert_out_ready{m}") for m in range(2)]
        s_mo = [[sem(f"expert_out_stored{m}{i}") for i in range(2)] for m in range(2)]
        s_g0 = sem("first_rows_gathered")
        s_g1 = [sem(f"second_rows_gathered{q}") for q in range(4)]
        s_gu = sem("gathered_added")
        s_up = sem("inner_in_psum")
        s_ue2 = sem("inner_ready")
        s_dp = sem("delta_in_psum")
        s_da1 = sem("delta_abs_ready")
        s_dr = sem("delta_psum_read")
        s_dw = sem("delta_one_plus_ready")
        s_dl = sem("delta_log_ready")
        s_du = sem("delta_u_ready")
        s_bp = sem("bc_rows_in_psum")
        s_r3 = sem("bc_split_ready")
        s_as = sem("decay_rates_ready")
        s_b = sem("b_spread")
        s_c = sem("c_spread")
        s_dA = sem("decay_ready")
        s_db = sem("drive_ready")
        s_sn = sem("state_ready")
        s_hc = sem("state_c_ready")
        s_ya = sem("y_added")
        s_y0 = sem("y_cleared")
        s_yt = sem("y_gated")
        s_op = sem("scan_out_in_psum")
        s_oe = sem("scan_out_added")
        s_end = sem("output_stored")

        xs = scratch["rows_in"]
        ys = scratch["rows_out"]
        n_cst_rows = 0

        def bc(ap, axis, n):
            shape = list(ap.shape)
            return ap.unsqueeze(axis).broadcast_to(shape[:axis] + [n] + shape[axis:])

        def turned(pt, i, part, c):
            n, at = (i + 1, 0) if i < 4 else (4, 4) if part == 0 else (i - 3, 8)
            src = PS[:, 4 + c % 2, 0:n * P].rearrange("p (j q) -> p j q", q=P)
            return pt[:, at:at + n, (i % 4) * P:(i % 4 + 1) * P], src

        block = ctx.enter_context(nc.Block())

        @block.sync
        def _(sp):
            for q in range(4):
                sp.dma_start(X[:, 4 * q:4 * q + 4, :],
                             A["x"].rearrange("b (t p) d -> p (b t) d", p=P)[:, 4 * q:4 * q + 4, :]
                             ).then_inc(s_x, 16)
            sp.dma_start(CST[:], A["cst"]).then_inc(s_cst, 16)
            for dst, src in ((wkv[:], A["Wkv"]), (peT[:], A["peT"]),
                             (bk[:], A["bkv"][0:D].rearrange("(p o) -> p o", o=1)),
                             (bv[:], A["bkv"][D:2 * D].rearrange("(o d) -> o d", o=1)),
                             (bq[:], A["bq"]),
                             (wgate[0][:], A["router_w"]),
                             (wo[:], A["Wo"].rearrange("(h p) d -> p h d", p=P)),
                             (wgate[1][:], A["gate_wT"])):
                sp.dma_start(dst, src).then_inc(s_wat, 16)
            sp.wait_ge(s_zero, 1)
            for m in range(2):
                flat = xs[m].rearrange("(p r) d -> p (r d)", p=P)
                for c in range(0, TILES[m] * D, 512):
                    w = min(512, TILES[m] * D - c)
                    sp.dma_start(flat[:, c:c + w], zero[:, 0:w]).then_inc(s_zf, 16)
            for dst, src in ((w_in[:], A["W_in"]),
                             (w_dl[:], A["W_delta"].rearrange("(k p) n -> p k n", p=P)),
                             (b_dl[:], A["b_delta"]),
                             (w_bc[:, :, 0:STATE], A["W_B"].rearrange("(k p) n -> p k n", p=P)),
                             (w_bc[:, :, STATE:32], A["W_C"].rearrange("(k p) n -> p k n", p=P)),
                             (a_lg[:], A["A_log"].rearrange("(k p) n -> p k n", p=P)),
                             (d_par[:], A["D_param"]),
                             (w_out[:], A["W_out"].rearrange("(k p) n -> p k n", p=P))):
                sp.dma_start(dst, src).then_inc(s_wsc, 16)

            def load_wq(g, h, i, free):
                if free is not None:
                    sp.wait_ge(s_qp, free)
                sp.dma_start(wq[:, i, :], A["WqH"][h]).then_inc(s_wq[i], 16)

            def attention_loads(b):
                load_wq(8 * b, 0, 0, None if b == 0 else 16 * b - 2)
                load_wq(8 * b + 1, 1, 1, None if b == 0 else 16 * b)
                with sp.Fori(1, 4) as r:
                    load_wq(None, 2 * r, 0, 16 * b + 4 * r - 2)
                    load_wq(None, 2 * r + 1, 1, 16 * b + 4 * r)

            def expert_loads(m):
                e_n, k_n, f_n = MOE[m]
                sp.wait_ge(s_eid, m + 1)
                sp.wait_ge(s_sc[m], 16 * NT * k_n)

                tiles, groups = (4, QUADS) if m == 0 else (2, PAIRS)
                mw = (mw0, mw1)[m]

                def group(p, s, first):
                    if not first:
                        sp.wait_ge(s_mtp[m], p - 1)
                    sp.dma_start(MX[:, tiles * s:tiles * s + tiles, :],
                                 xs[m][bass.ds(p * tiles * P, tiles * P), :].rearrange("(i p) d -> p i d", p=P)
                                 ).then_inc(s_mx[m][s], 16)
                    if not first:
                        sp.wait_ge((s_my, s_myp)[m][m], p - 1)
                    for i in range(tiles):
                        e = sp.value_load(eid[m][0:1, bass.ds(tiles * p + i, 1)], min_val=0, max_val=e_n - 1)
                        sp.dma_start(mw[:, tiles * s + i, :], A[f"w_{m}"][bass.ds(e, 1)].rearrange("o p n -> (o p) n")
                                     ).then_inc(s_mw[m][s], 16)

                group(0, 0, True)
                group(1, 1, True)
                with sp.Fori(1, groups // 2) as r:
                    group(2 * r, 0, False)
                    group(2 * r + 1, 1, False)

            attention_loads(0)
            expert_loads(0)
            attention_loads(1)
            sp.wait_ge(s_myp[0], QUADS)
            sp.wait_ge(s_we, 4 * HEADS)
            expert_loads(1)
            ov = out.rearrange("b (t p) d -> p (b t) d", p=P)
            for q in range(4):
                sp.wait_ge(s_gu, NT + 8 * (q + 1))
                sp.dma_start(ov[:, 4 * q:4 * q + 4, :], X[:, 4 * q:4 * q + 4, :]).then_inc(s_end, 16)
            sp.wait_ge(s_end, 64)

        @block.gpsimd
        def _(pool):
            nc.gpsimd.memset(zero[:], 0.0).then_inc(s_zero, 1)
            zf = sum(-(-TILES[m] * D // 512) for m in range(2))

            def scatter(m, tiles):
                for k in range(MOE[m][1]):
                    for t in tiles:
                        nc.gpsimd.indirect_dma_start(
                            out=xs[m][:, :], out_offset=bass.IndirectOffsetOnAxis(ap=slot[m][:, k, t:t + 1], axis=0),
                            in_=XN[:, t, :], in_offset=None).then_inc(s_sc[m], 16)

            def gather(m, k, t, dst, s):
                nc.gpsimd.indirect_dma_start(
                    out=dst, out_offset=None, in_=ys[m][:, :],
                    in_offset=bass.IndirectOffsetOnAxis(ap=slot[m][:, k, t:t + 1], axis=0)).then_inc(s, 16)

            def query_low(g, hf):
                pool.wait_ge(s_qh, 2 * g + hf + 1)
                sl = slice(hf * BANK, (hf + 1) * BANK)
                nc.gpsimd.tensor_tensor(QL[:, sl], QF[:], QH[:, sl].bitcast(F32), ALU.subtract).then_inc(s_qe, 1)

            def attention(b):
                query_low(8 * b, 0)
                for h in range(HEADS):
                    query_low(8 * b + h, 1)
                    if b == 0:
                        if h == 0:
                            pool.wait_ge(s_slot, 1)
                            pool.wait_ge(s_zf, 16 * zf)
                        scatter(0, (2 * h, 2 * h + 1))
                    else:
                        for t in (2 * h, 2 * h + 1):
                            gather(0, 0, t, GA[:, t, :], s_g0)
                    if h < HEADS - 1:
                        query_low(8 * b + h + 1, 0)

            attention(0)
            for i in range(2):
                pool.wait_ge(s_mo[0][i], 16 * (QUADS // 2))
            attention(1)

            pool.wait_ge(s_slot, 2)
            scatter(1, range(NT))

            def add(b, n, c, self_free):
                pool.wait_ge(s_hc, 32 * b + 2 * n + c + 1)
                if self_free:
                    pool.wait_ge(s_ya, 32 * b + 2 * n + c - 1)
                nc.gpsimd.tensor_tensor(YA[:, c, :], YA[:, c, :], HC[:, c, :], ALU.add).then_inc(s_ya, 1)

            def clear(b):
                if b:
                    pool.wait_ge(s_yt, 2 * b)
                nc.gpsimd.memset(YA[:], 0.0).then_inc(s_y0, 1)
                pool.wait_ge(s_y0, b + 1)

            clear(0)
            add(0, 0, 0, False)
            add(0, 0, 1, False)
            with pool.Fori(1, STATE) as n:
                add(0, n, 0, True)
                add(0, n, 1, True)
            clear(1)
            add(1, 0, 0, False)
            add(1, 0, 1, False)
            with pool.Fori(1, LATE) as n:
                add(1, n, 0, True)
                add(1, n, 1, True)
            rows = [(q, k, t) for q in range(4) for k in range(2) for t in range(4)]

            def gather_next(count):
                for q, k, t in rows[:count]:
                    gather(1, k, 4 * q + t, (GA, GB)[q // 2][:, 8 * (q % 2) + 4 * k + t, :], s_g1[q])
                del rows[:count]

            for n in range(LATE, STATE):
                add(1, n, 0, True)
                add(1, n, 1, True)
                if n == LATE:
                    for i in range(2):
                        pool.wait_ge(s_mo[1][i], 16 * (PAIRS // 2))
                gather_next(2)
            gather_next(len(rows))

        @block.scalar
        def _(act):
            def deviation(ph):
                act.wait_ge(s_var, ph + 1)
                nc.scalar.activation(lnt[:, 1, :], lnt[:, 0, :], ACT.Sqrt).then_inc(s_sd, 1)

            def gate_exp(ph):
                act.wait_ge(s_ein, ph + 1)
                n = NT * MOE[0][0] if ph == 0 else NT
                src = rt[:, 0, 0:n] if ph == 0 else rs1[:, 5, :]
                dst = rt[:, 1, 0:n] if ph == 0 else rs1[:, 6, :]
                nc.scalar.activation(dst, src, ACT.Exp).then_inc(s_eout, 1)

            deviation(0)
            for q in range(4):
                act.wait_ge(s_vp, q + 1)
                nc.scalar.copy(VH[:, 4 * q:4 * q + 4, :], bank((5, 6, 7, 1)[q])).then_inc(s_vh, 1)
                act.wait_ge(s_kf, 2 * q + 2)
                nc.scalar.copy(KH[:, q // 2, (q % 2) * BANK:(q % 2 + 1) * BANK], QF[:]).then_inc(s_kh, 1)
            gate_exp(0)

            def out_evac(s, done):
                act.wait_ge(s_pv, done)
                nc.scalar.copy(OT[:, s, :], bank(6)).then_inc(s_ue, 1)

            def query_high(g, hf):
                act.wait_ge(s_qr, 2 * g + hf + 1)
                nc.scalar.copy(QH[:, hf * BANK:(hf + 1) * BANK], QF[:]).then_inc(s_qh, 1)

            def high(g, i):
                for part in range(1 if i < 4 else 2):
                    c = i if i < 4 else 4 + 2 * (i - 4) + part
                    act.wait_ge(s_tc, 12 * g + c + 1)
                    dst, src = turned(PTH, i, part, c)
                    nc.scalar.copy(dst, src).then_inc(s_ea, 1)

            def exps(g, i):
                act.wait_ge(s_nm, 8 * g + i + 1)
                nk = (i + 1) * P
                s = i % 2
                sc = PS[:, 2 * s:2 * s + 2, :].rearrange("p a n -> p (a n)")
                nc.scalar.activation(PR[:, s, 0:nk], sc[:, 0:nk], ACT.Exp, bias=nmax[:, i % 4:i % 4 + 1],
                                     accum_out=rsum[:, i:i + 1]).then_inc(s_ex, 1)

            def head(g, pending, follow):
                for i in range(8):
                    if i == 3:
                        query_high(g, 1)
                    if i == 7 and follow:
                        query_high(g + 1, 0)
                    if i == 0 and pending:
                        out_evac(0, 2 * g - 1)
                        high(g - 1, 7)
                    if i == 4 and pending:
                        out_evac(1, 2 * g)
                    if i >= 1:
                        high(g, i - 1)
                    exps(g, i)

            def attention(b):
                query_high(8 * b, 0)
                head(8 * b, False, True)
                with act.Fori(8 * b + 1, 8 * b + 7) as g:
                    head(g, True, True)
                g = 8 * b + 7
                head(g, True, False)
                g += 1
                out_evac(0, 2 * g - 1)
                high(g - 1, 7)
                out_evac(1, 2 * g)

            def experts_first():
                def quad(p, s):
                    for i in range(4):
                        for c in range(2):
                            if c == 0 and i % 2 == 0:
                                act.wait_ge(s_mhp[0], 2 * p + i // 2 + 1)
                            w = mw0[:, 4 * s + i, 4 * P:4 * P + 2]
                            r = nc.scalar.activation(MH[:, 2 * i + c, :], PS[:, 2 + i // 2, (2 * (i % 2) + c) * P:(2 * (i % 2) + c + 1) * P],
                                                     ACT.Gelu, bias=w[:, c:c + 1])
                        r.then_inc(s_mh[0], 1)

                def store(p, s):
                    act.wait_ge(s_my[0], p + 1)
                    act.dma_start(ys[0][bass.ds(p * 4 * P, 4 * P), :].rearrange("(i p) d -> p i d", p=P), MY[:, 4 * s:4 * s + 4, :]
                                  ).then_inc(s_mo[0][s], 16)

                with act.Fori(0, QUADS // 2) as r:
                    for s in range(2):
                        quad(2 * r + s, s)
                        store(2 * r + s, s)

            def pair_in(p):
                act.wait_ge(s_mtp[1], p + 1)
                nc.scalar.copy(MXT[:, 0:2, :], PS[:, 4, 0:2 * P].rearrange("p (i n) -> p i n", i=2)).then_inc(s_mt[1], 1)

            def pair_out(p, s, times):
                act.wait_ge(s_myp[1], p)
                if times is not None:
                    act.wait_ge(s_mo[1][s], times)
                nc.scalar.copy(MY[:, 2 * s:2 * s + 2, :], PS[:, 7, 0:2 * P].rearrange("p (i n) -> p i n", i=2)).then_inc(s_my[1], 1)
                act.wait_ge(s_my[1], p)
                act.dma_start(ys[1][bass.ds((p - 1) * 2 * P, 2 * P), :].rearrange("(i p) d -> p i d", p=P), MY[:, 2 * s:2 * s + 2, :]
                              ).then_inc(s_mo[1][s], 16)

            def pair_hidden(p):
                for i in range(2):
                    act.wait_ge(s_mhp[1], 2 * p + i + 1)
                    nc.scalar.activation(MH[:, 4 * i:4 * i + 4, :], bank(5 + i).rearrange("p (c n) -> p c n", n=P),
                                         ACT.Relu).then_inc(s_mh[1], 1)

            attention(0)
            experts_first()
            attention(1)
            deviation(1)
            gate_exp(1)
            act.wait_ge(s_wsc, 16 * 8)
            nc.scalar.activation(a_sc[:], a_lg[:], ACT.Exp).then_inc(s_as, 1)
            for b in range(B):
                for q in range(8):
                    act.wait_ge(s_up, 8 * b + q + 1)
                    c, hf = q // 2, q % 2
                    dst = (UT if c < 2 else SR)[:, c % 2, hf * BANK:(hf + 1) * BANK]
                    if b and q == 0:
                        act.wait_ge(s_yt, 2 * b)
                    nc.scalar.activation(dst, bank(4 + q % 4), ACT.Silu).then_inc(s_ue2, 1)
                act.wait_ge(s_dr, 4 * b + 4)
                nc.scalar.activation(DA[:], DL[:], ACT.Abs).then_inc(s_da1, 1)
                act.wait_ge(s_da1, 2 * b + 1)
                nc.scalar.activation(DB[:], DA[:], ACT.Exp, scale=-1.0).then_inc(s_da1, 1)
                act.wait_ge(s_dw, b + 1)
                nc.scalar.activation(HS[:], DA[:], ACT.Ln).then_inc(s_dl, 1)
                act.wait_ge(s_du, b + 1)

                def decay(n, free):
                    for c in range(2):
                        if free:
                            act.wait_ge(s_sn, 32 * b + 2 * n + c - 1)
                        nc.scalar.activation(DA[:, c, :], DL[:, c, :], ACT.Exp,
                                             scale=a_sc[:, c, bass.ds(n, 1)]).then_inc(s_dA, 1)

                def beside(n, p, s, times):
                    decay(n, True)
                    pair_in(p)
                    pair_out(p, 1 - s, times)
                    pair_hidden(p)

                if b == 0:
                    decay(0, False)
                    with act.Fori(1, EARLY) as n:
                        decay(n, True)
                    decay(EARLY, True)
                    pair_in(0)
                    pair_hidden(0)
                    beside(EARLY + 1, 1, 1, None)
                    decay(EARLY + 2, True)
                    pair_in(2)
                    pair_out(2, 1, None)
                    pair_hidden(2)
                    beside(EARLY + 3, 3, 1, 16)
                    with act.Fori(2, (STATE - EARLY) // 2) as r:
                        beside(EARLY + 2 * r, 2 * r, 0, 16 * r - 16)
                        beside(EARLY + 2 * r + 1, 2 * r + 1, 1, 16 * r)
                else:
                    done = STATE - EARLY
                    with act.Fori(0, LATE // 2) as r:
                        beside(2 * r, done + 2 * r, 0, 16 * r + 8 * done - 16)
                        beside(2 * r + 1, done + 2 * r + 1, 1, 16 * r + 8 * done)
                    pair_out(PAIRS, 1, 8 * PAIRS - 16)
                    with act.Fori(LATE, STATE) as n:
                        decay(n, True)

        @block.tensor
        def _(pe):
            mm = nc.tensor.matmul

            def transposes(ph):
                for q in range(4):
                    pe.wait_ge(s_xn, 4 * ph + q + 1)
                    for t in range(4):
                        r = nc.tensor.transpose(PS[:, 4 + q, t * P:(t + 1) * P], XN[:, 4 * q + t, :], ident)
                    r.then_inc(s_tp, 1)

            def logits(ph):
                e_n = MOE[ph][0]
                pe.wait_ge(s_xnt, 4 * ph + 4)
                for t in range(NT):
                    r = mm(PS[:, 0, t * e_n:(t + 1) * e_n], XNT[:, t * P:(t + 1) * P], wgate[ph][:], start=True, stop=True)
                r.then_inc(s_lg, 1)

            def ranks(ph):
                n = NT * MOE[ph][0]
                pe.wait_ge(s_ohb, ph + 1)
                mm(PS[:, 7, 0:n], beforeb[:], ohb[:, 0:n], start=True, stop=True)
                mm(PS[:, 7, 256:256 + n], onesb[:], ohb[:, 0:n], start=True, stop=True).then_inc(s_rk, 1)

            pe.wait_ge(s_cst, 16)
            transposes(0)
            pe.wait_ge(s_wat, 16 * 8)
            logits(0)
            for q in range(4):
                mm(bank(1 + q), wkv[:, 0:D], XNT[:, q * BANK:(q + 1) * BANK], start=True, stop=True).then_inc(s_kp, 1)
            pe.wait_ge(s_cnv, 1)
            for q in range(4):
                if q == 3:
                    pe.wait_ge(s_kf, 1)
                bk_ = (5, 6, 7, 1)[q]
                for t in range(4):
                    dst = PS[:, bk_, t * D:(t + 1) * D]
                    mm(dst, XNT[:, (4 * q + t) * P:(4 * q + t + 1) * P], wkv[:, D:2 * D], start=True, stop=False)
                    r = mm(dst, ones1[:], bv[:], start=False, stop=True)
                r.then_inc(s_vp, 1)
            pe.wait_ge(s_ve, 3)
            ranks(0)
            pe.wait_ge(s_ke, 4)
            pe.wait_ge(s_ve, 4)
            pe.wait_ge(s_rkr, 1)

            def query(g, h, b, hf):
                r = mm(bank(7), wq[:, h % 2 if isinstance(h, int) else parity[0], :],
                       XNT[:, b * T + hf * BANK:b * T + (hf + 1) * BANK], start=True, stop=True)
                r.then_inc(s_qp, 1)

            parity = [0]

            def three(dst, a, b_, ra, rb, first):
                mm(dst, a[0][ra], b_[0][rb], start=first, stop=False, skip_group_check=True)
                mm(dst, a[0][ra], b_[1][rb], start=False, stop=False, skip_group_check=True)
                return mm(dst, a[1][ra], b_[0][rb], start=False, stop=True, skip_group_check=True)

            def scores(g, b, i, free):
                if free:
                    pe.wait_ge(s_ex, 8 * g + i - 1)
                nk = (i + 1) * P
                s = 2 * (i % 2)
                q = (slice(None), slice(i * P, (i + 1) * P))
                for lo in range(0, nk, BANK):
                    hi = min(nk, lo + BANK)
                    three(PS[:, s + lo // BANK, 0:hi - lo], (QH, QL), (KH, KL), q, (slice(None), b, slice(lo, hi)), True)
                mm(PS[:, s + i // 4, (i % 4) * P:(i % 4 + 1) * P], identb[:], causalb[:], start=False, stop=True,
                   skip_group_check=True).then_inc(s_qk, 1)

            def turn(g, i, first=False):
                pe.wait_ge(s_ex, 8 * g + i + 1)
                for part in range(1 if i < 4 else 2):
                    c = i if i < 4 else 4 + 2 * (i - 4) + part
                    if not (first and c < 2):
                        pe.wait_ge(s_ed, 12 * g + c - 1)
                    lo, hi = 4 * part, min(i + 1, 4 * part + 4)
                    for j in range(lo, hi):
                        r = nc.tensor.transpose(PS[:, 4 + c % 2, (j - lo) * P:(j - lo + 1) * P],
                                                PR[:, i % 2, j * P:(j + 1) * P], ident)
                    r.then_inc(s_tc, 1)

            def out_part(g, b, group, part, free=True):
                if part == 0:
                    pe.wait_ge(s_ed, 12 * g + (11 if group else 4))
                    if group or free:
                        pe.wait_ge(s_ue, 2 * g + group)
                if part == 2 and group:
                    pe.wait_ge(s_ed, 12 * g + 12)
                for j in ((2 * part, 2 * part + 1) if group else (part,)):
                    lo = max(0, j - 4 * group) * P
                    r = three(PS[:, 6, lo:BANK], (VH, VL), (PTH, PTL), (slice(None), b * TB + j, slice(None)),
                              (slice(None), 4 * group + j, slice(lo, BANK)), j == 0)
                if part == 3:
                    r.then_inc(s_pv, 1)

            def project(g, h, s):
                pe.wait_ge(s_ue, 2 * g + 1 + s)
                for t in range(4):
                    r = mm(PS[:, 7, t * P:(t + 1) * P], OT[:, s, t * P:(t + 1) * P],
                           wo[:, bass.ds(h, 1), :].rearrange("p o d -> p (o d)"), start=True, stop=True)
                r.then_inc(s_wo, 1)

            def head(g, b, h, s, pending, follow):
                pe.wait_ge(s_qe, 2 * g + 1)
                for i in range(8):
                    if i == 4:
                        pe.wait_ge(s_qe, 2 * g + 2)
                    scores(g, b, i, not (isinstance(g, int) and g == 0 and i < 2))
                    if i == 0 and pending:
                        out_part(g - 1, b, 0, 3)
                        turn(g - 1, 7)
                    if pending and 1 <= i <= 4:
                        out_part(g - 1, b, 1, i - 1)
                    if i >= 5:
                        out_part(g, b, 0, i - 5, not (isinstance(g, int) and g == 0))
                    if i >= 1:
                        turn(g, i - 1, isinstance(g, int) and g == 0)
                    if i == 1 and pending:
                        pe.wait_ge(s_qr, 2 * g + 1)
                        project(g - 1, h - 1, 0)
                    if i == 2:
                        pe.wait_ge(*((s_we, 2 * g - 1) if pending else (s_qr, 2 * g + 1)))
                        parity[0] = s
                        query(g, h, b, 1)
                    if i == 5 and pending:
                        pe.wait_ge(s_qr, 2 * g + 2)
                        project(g - 1, h - 1, 1)
                    if i == 6 and follow is not None:
                        pe.wait_ge(*((s_we, 2 * g) if pending else (s_qr, 2 * g + 2)))
                        pe.wait_ge(s_wq[1 - s], follow)
                        parity[0] = 1 - s
                        query(g + 1, h + 1, b, 0)

            def attention(b):
                pe.wait_ge(s_wq[0], 64 * b + 16)
                query(8 * b, 0, b, 0)
                head(8 * b, b, 0, 0, False, 64 * b + 16)
                with pe.Fori(0, 3) as r:
                    head(8 * b + 1 + 2 * r, b, 1 + 2 * r, 1, True, 64 * b + 16 * r + 32)
                    head(8 * b + 2 + 2 * r, b, 2 + 2 * r, 0, True, 64 * b + 16 * r + 32)
                g = 8 * b + 7
                head(g, b, 7, 1, True, None)
                out_part(g, b, 0, 3)
                turn(g, 7)
                for part in range(4):
                    out_part(g, b, 1, part)
                pe.wait_ge(s_we, 2 * g)
                project(g, 7, 0)
                pe.wait_ge(s_we, 2 * g + 1)
                project(g, 7, 1)
                pe.wait_ge(s_we, 2 * g + 2)

            def experts_first():
                def turn_rows(p, s, times, first=False):
                    pe.wait_ge(s_mx[0][s], 16 * times)
                    if not first:
                        pe.wait_ge(s_mt[0], p - 1)
                    for i in range(4):
                        r = nc.tensor.transpose(PS[:, s, i * P:(i + 1) * P], MX[:, 4 * s + i, :], ident)
                    r.then_inc(s_mtp[0], 1)

                def hidden(p, s, times):
                    pe.wait_ge(s_mt[0], p + 1)
                    pe.wait_ge(s_mw[0][s], 64 * times)
                    for i in range(4):
                        for c in range(2):
                            r = mm(PS[:, 2 + i // 2, (2 * (i % 2) + c) * P:(2 * (i % 2) + c + 1) * P],
                                   mw0[:, 4 * s + i, c * P:(c + 1) * P], MXT[:, 4 * s + i, :], start=True, stop=True)
                        if i % 2:
                            r.then_inc(s_mhp[0], 1)

                def result(p, s, first=False):
                    if not first:
                        pe.wait_ge(s_my[0], p)
                    for i in range(4):
                        pe.wait_ge(s_mh[0], 4 * p + i + 1)
                        for c in range(2):
                            r = mm(PS[:, 4, i * P:(i + 1) * P], MH[:, 2 * i + c, :], mw0[:, 4 * s + i, (2 + c) * P:(3 + c) * P],
                                   start=(c == 0), stop=(c == 1))
                    r.then_inc(s_myp[0], 1)

                turn_rows(0, 0, 1, True)
                hidden(0, 0, 1)
                turn_rows(1, 1, 1, True)
                result(0, 0, True)
                hidden(1, 1, 1)
                with pe.Fori(1, QUADS // 2) as r:
                    for s in range(2):
                        turn_rows(2 * r + s, s, r + 1)
                        result(2 * r + s - 1, 1 - s)
                        hidden(2 * r + s, s, r + 1)
                result(QUADS - 1, 1)
                pe.wait_ge(s_my[0], QUADS)

            def turn_pair(p, s, times):
                pe.wait_ge(s_mx[1][s], 16 * times)
                if not (isinstance(p, int) and p == 0):
                    pe.wait_ge(s_mt[1], p)
                for i in range(2):
                    r = nc.tensor.transpose(PS[:, 4, i * P:(i + 1) * P], MX[:, 2 * s + i, :], ident)
                r.then_inc(s_mtp[1], 1)

            def hidden_pair(p, s, times):
                pe.wait_ge(s_mt[1], p + 1)
                pe.wait_ge(s_mw[1][s], 32 * times)
                for i in range(2):
                    for c in range(4):
                        r = mm(PS[:, 5 + i, c * P:(c + 1) * P], mw1[:, 2 * s + i, c * P:(c + 1) * P], MXT[:, i, :],
                               start=True, stop=True)
                    r.then_inc(s_mhp[1], 1)

            def result_pair(p, s):
                if not (isinstance(p, int) and p == 0):
                    pe.wait_ge(s_my[1], p)
                for i in range(2):
                    pe.wait_ge(s_mh[1], 2 * p + i + 1)
                    for c in range(4):
                        r = mm(PS[:, 7, i * P:(i + 1) * P], MH[:, 4 * i + c, :], mw1[:, 2 * s + i, (4 + c) * P:(5 + c) * P],
                               start=(c == 0), stop=(c == 3))
                r.then_inc(s_myp[1], 1)

            attention(0)
            experts_first()
            attention(1)
            transposes(1)
            logits(1)
            ranks(1)
            pe.wait_ge(s_wsc, 16 * 8)
            pe.wait_ge(s_rkr, 2)
            for b in range(B):
                for q in range(8):
                    c, hf = q // 2, q % 2
                    if q >= 4 or b:
                        pe.wait_ge(s_ue2, 8 * b + q - 3 if q >= 4 else 8 * b)
                    if b and q == 0:
                        pe.wait_ge(s_oe, 2 * b)
                        pe.wait_ge(s_my[1], STATE - EARLY - 1)
                    if b and q >= 2:
                        pe.wait_ge(s_dr, 4 * b)
                    mm(bank(4 + q % 4), w_in[:, c * P:(c + 1) * P], XNT[:, b * T + hf * BANK:b * T + (hf + 1) * BANK],
                       start=True, stop=True).then_inc(s_up, 1)
                pe.wait_ge(s_ue2, 8 * b + 8)
                for q in range(4):
                    c, hf = q // 2, q % 2
                    for k in range(2):
                        r = mm(bank(4 + q), w_dl[:, k, c * P:(c + 1) * P], UT[:, k, hf * BANK:(hf + 1) * BANK],
                               start=(k == 0), stop=(k == 1))
                    r.then_inc(s_dp, 1)
                if b:
                    pe.wait_ge(s_hc, 32 * b)
                    pe.wait_ge(s_db, 32 * b)
                for hf in range(2):
                    for k in range(2):
                        r = mm(PS[0:32, hf, :], w_bc[:, k, :], UT[:, k, hf * BANK:(hf + 1) * BANK],
                               start=(k == 0), stop=(k == 1))
                r.then_inc(s_bp, 1)
                pe.wait_ge(s_r3, b + 1)
                pe.wait_ge(s_cnv, 2)

                def spread(n, free):
                    if free:
                        pe.wait_ge(s_db, 32 * b + 2 * n)
                    for hf in range(2):
                        r = mm(bank(hf), pickb[:, bass.ds(n, 1), :].rearrange("p o m -> p (o m)"), R3[:, hf * BANK:(hf + 1) * BANK],
                               start=True, stop=True)
                    r.then_inc(s_b, 1)
                    if free:
                        pe.wait_ge(s_hc, 32 * b + 2 * n)
                    for hf in range(2):
                        r = mm(bank(2 + hf), pickb[:, bass.ds(n + STATE, 1), :].rearrange("p o m -> p (o m)"),
                               R3[:, hf * BANK:(hf + 1) * BANK], start=True, stop=True)
                    r.then_inc(s_c, 1)

                def beside(n, p, s, times):
                    spread(n, True)
                    turn_pair(p, s, times)
                    result_pair(p - 1, 1 - s)
                    hidden_pair(p, s, times)

                if b == 0:
                    spread(0, False)
                    with pe.Fori(1, EARLY) as n:
                        spread(n, True)
                    spread(EARLY, True)
                    pe.wait_ge(s_dr, 4)
                    turn_pair(0, 0, 1)
                    hidden_pair(0, 0, 1)
                    beside(EARLY + 1, 1, 1, 1)
                    with pe.Fori(1, (STATE - EARLY) // 2) as r:
                        beside(EARLY + 2 * r, 2 * r, 0, r + 1)
                        beside(EARLY + 2 * r + 1, 2 * r + 1, 1, r + 1)
                else:
                    done = STATE - EARLY
                    pe.wait_ge(s_dr, 8)
                    with pe.Fori(0, LATE // 2) as r:
                        beside(2 * r, done + 2 * r, 0, r + done // 2 + 1)
                        beside(2 * r + 1, done + 2 * r + 1, 1, r + done // 2 + 1)
                    result_pair(PAIRS - 1, 1)
                    with pe.Fori(LATE, STATE) as n:
                        spread(n, True)
                pe.wait_ge(s_yt, 2 * b + 2)
                if b == 0:
                    pe.wait_ge(s_mt[1], STATE - EARLY)
                    pe.wait_ge(s_mh[1], 2 * (STATE - EARLY))
                for q in range(2):
                    for t in range(4):
                        tt = 4 * q + t
                        for k in range(2):
                            r = mm(PS[:, 4 + q, t * P:(t + 1) * P], SR[:, k, tt * P:(tt + 1) * P], w_out[:, k, :],
                                   start=(k == 0), stop=(k == 1))
                    r.then_inc(s_op, 1)
            pe.wait_ge(s_oe, 4)

        @block.vector
        def _(dve):
            count = [0]

            def link(ins):
                count[0] += 1
                ins.then_inc(s_v, 1)
                dve.wait_ge(s_v, count[0])

            ts, tt = nc.vector.tensor_scalar, nc.vector.tensor_tensor
            stt, cp = nc.vector.scalar_tensor_tensor, nc.vector.tensor_copy

            def normalise(ph):
                for t in range(NT):
                    if ph == 0 and t % 4 == 0:
                        dve.wait_ge(s_x, 16 * (t // 4 + 1))
                    r = nc.vector.bn_stats(stats[:, t, :], X[:, t, :])
                link(r)
                for t in range(NT):
                    r = nc.vector.bn_aggr(mv[:, t, :], stats[:, t, :])
                link(r)
                ve, sd, r0, a, r1 = (lnt[:, i, :] for i in range(5))
                ts(ve, mv[:, :, 1], EPS, None, ALU.add).then_inc(s_var, 1)
                dve.wait_ge(s_sd, ph + 1)
                link(nc.vector.reciprocal(r0, sd))
                link(tt(a, r0, r0, ALU.mult))
                link(tt(a, a, ve, ALU.mult))
                link(ts(a, a, -0.5, 1.5, ALU.mult, ALU.add))
                link(tt(r1, r0, a, ALU.mult))
                if ph:
                    dve.wait_ge(s_sc[0], 16 * NT)
                for t in range(NT):
                    r = ts(XN[:, t, :], X[:, t, :], mv[:, t, 0:1], lnt[:, 4, t:t + 1], ALU.subtract, ALU.mult)
                    if t % 4 == 3:
                        r.then_inc(s_xn, 1)
                for q in range(4):
                    dve.wait_ge(s_tp, 4 * ph + q + 1)
                    cp(XNT[:, q * BANK:(q + 1) * BANK], bank(4 + q)).then_inc(s_xnt, 1)

            def route(m):
                e_n, k_n, _ = MOE[m]
                n = NT * e_n
                v3 = lambda ap: ap.rearrange("p (t e) -> p t e", e=e_n)
                L = v3(lg[:, 0:n])
                dve.wait_ge(s_lg, m + 1)
                cp(lg[:, 0:n], PS[:, 0, 0:n]).then_inc(s_lgr, 1)
                dve.wait_ge(s_lgr, m + 1)
                iota = bc(cst["iota"][:, 0:e_n], 1, NT)
                mx = [rs1[:, 0, :], rs1[:, 1, :]]
                for k in range(k_n):
                    src = L
                    if k:
                        link(stt(v3(rt[:, 0, 0:n]), v3(oh[:, 0, 0:n]), -KEPT, L, ALU.mult, ALU.add))
                        src = v3(rt[:, 0, 0:n])
                    link(nc.vector.tensor_reduce(mx[k], src, AX_X, ALU.max))
                    link(tt(v3(rt[:, 1, 0:n]), src, bc(mx[k], 2, e_n), ALU.is_equal))
                    link(tt(v3(rt[:, 2, 0:n]), v3(rt[:, 1, 0:n]), iota, ALU.mult))
                    link(nc.vector.tensor_reduce(rs1[:, 2 + k, :], v3(rt[:, 2, 0:n]), AX_X, ALU.min))
                    link(tt(v3(oh[:, k, 0:n]), iota, bc(rs1[:, 2 + k, :], 2, e_n), ALU.is_equal))
                if k_n == 1:
                    cp(ohb[:, 0:n], oh[:, 0, 0:n]).then_inc(s_ohb, 1)
                    tt(v3(rt[:, 0, 0:n]), L, bc(mx[0], 2, e_n), ALU.subtract).then_inc(s_ein, 1)
                else:
                    tt(ohb[:, 0:n], oh[:, 0, 0:n], oh[:, 1, 0:n], ALU.add).then_inc(s_ohb, 1)
                    tt(rs1[:, 5, :], mx[1], mx[0], ALU.subtract).then_inc(s_ein, 1)

            def place(m):
                e_n, k_n, _ = MOE[m]
                n = NT * e_n
                v3 = lambda ap: ap.rearrange("p (t e) -> p t e", e=e_n)
                dve.wait_ge(s_eout, m + 1)
                if k_n == 1:
                    link(nc.vector.tensor_reduce(rs1[:, 4, :], v3(rt[:, 1, 0:n]), AX_X, ALU.add))
                    link(nc.vector.reciprocal(wsel[m][:, 0, :], rs1[:, 4, :]))
                else:
                    link(ts(rs1[:, 4, :], rs1[:, 6, :], 1.0, None, ALU.add))
                    link(nc.vector.reciprocal(wsel[m][:, 0, :], rs1[:, 4, :]))
                    link(tt(wsel[m][:, 1, :], wsel[m][:, 0, :], rs1[:, 6, :], ALU.mult))
                et = lambda ap: ap.rearrange("p (e t) -> p e t", t=NT)
                link(cp(et(rt[:, 2, 0:n]), tl[:, 256:256 + n].rearrange("p (t e) -> p e t", e=e_n)))
                link(nc.vector.tensor_tensor_scan(rt[:, 3, 0:n], seg[m][:], rt[:, 2, 0:n], 0.0, ALU.mult, ALU.add))
                total = et(rt[:, 3, 0:n])[:, :, NT - 1]
                link(ts(rei[:, 0, 0:e_n], total, float(P - 1), None, ALU.add))
                link(ts(rei[:, 1, 0:e_n], rei[:, 0, 0:e_n], 7, 7, ALU.logical_shift_right, ALU.logical_shift_left))
                link(cp(re1[:, 0, 0:e_n], rei[:, 1, 0:e_n]))
                link(nc.vector.tensor_tensor_scan(re1[:, 1, 0:e_n], re1[:, 3, 0:e_n], re1[:, 0, 0:e_n], 0.0, ALU.mult, ALU.add))
                link(tt(re1[:, 2, 0:e_n], re1[:, 1, 0:e_n], re1[:, 0, 0:e_n], ALU.subtract))
                link(tt(rt[:, 3, 0:n], rt[:, 3, 0:n], rt[:, 2, 0:n], ALU.subtract))
                link(tt(v3(rt[:, 4, 0:n]), v3(tl[:, 0:n]), rt[:, 3, 0:n].rearrange("p (e t) -> p t e", t=NT), ALU.add))
                link(tt(v3(rt[:, 4, 0:n]), v3(rt[:, 4, 0:n]), bc(re1[:, 2, 0:e_n], 1, NT), ALU.add))
                for k in range(k_n):
                    link(tt(rt[:, 2, 0:n], rt[:, 4, 0:n], oh[:, k, 0:n], ALU.mult))
                    link(nc.vector.tensor_reduce(rs1[:, 7 + k, :], v3(rt[:, 2, 0:n]), AX_X, ALU.add))
                    r = cp(slot[m][:, k, :], rs1[:, 7 + k, :])
                r.then_inc(s_slot, 1)
                tn = TILES[m]
                cmp = tl[:, 0:tn * e_n].rearrange("p (j e) -> p j e", e=e_n)
                link(tt(cmp, bc(re1[:, 1, 0:e_n], 1, tn), bc(cst["first"][:, 0:tn], 2, e_n), ALU.is_le))
                link(nc.vector.tensor_reduce(lg[:, 0:tn], cmp, AX_X, ALU.add))
                ts(eid[m][:], lg[:, 0:tn], float(e_n - 1), None, ALU.min).then_inc(s_eid, 1)

            def take_ranks(m):
                dve.wait_ge(s_rk, m + 1)
                n = NT * MOE[m][0]
                for at in (0, 256):
                    r = cp(tl[:, at:at + n], PS[:, 7, at:at + n])
                r.then_inc(s_rkr, 1)
                dve.wait_ge(s_rkr, m + 1)

            nc.vector.memset(onesb[:], 1.0)
            nc.vector.memset(ones1[:], 1.0)
            link(nc.vector.memset(re1[:, 3, :], 1.0))
            for m in range(2):
                link(nc.vector.memset(seg[m][:], 1.0))
                link(nc.vector.memset(seg[m][:].rearrange("p (e t) -> p e t", t=NT)[:, :, 0:1], 0.0))
            dve.wait_ge(s_cst, 16)
            cp(identb[:], ident)
            cp(causalb[:], cst["causal"])
            cp(beforeb[:], cst["before"]).then_inc(s_cnv, 1)
            normalise(0)

            def keys_values():
                dve.wait_ge(s_wat, 16 * 8)
                for q in range(4):
                    dve.wait_ge(s_kp, q + 1)
                    b, sl = q // 2, slice((q % 2) * BANK, (q % 2 + 1) * BANK)
                    if q:
                        dve.wait_ge(s_ke, q)
                    stt(QF[:], bank(1 + q), bk[:, 0:1], peT[:, sl], ALU.add, ALU.add).then_inc(s_kf, 1)
                    dve.wait_ge(s_kf, 2 * q + 1)
                    ts(QF[:], QF[:], SCALE, None, ALU.mult).then_inc(s_kf, 1)
                    dve.wait_ge(s_vh, q + 1)
                    tt(VL[:, 4 * q:4 * q + 4, :], bank((5, 6, 7, 1)[q]).rearrange("p (t d) -> p t d", d=D),
                       VH[:, 4 * q:4 * q + 4, :].bitcast(F32), ALU.subtract).then_inc(s_ve, 1)
                    dve.wait_ge(s_kh, q + 1)
                    tt(KL[:, b, sl], QF[:], KH[:, b, sl].bitcast(F32), ALU.subtract).then_inc(s_ke, 1)

            route(0)
            keys_values()
            take_ranks(0)

            def q_evac(g, hf, first=False):
                dve.wait_ge(s_qp, 2 * g + hf + 1)
                if not first:
                    dve.wait_ge(s_qe, 2 * g + hf)
                h = g - 8 * batch[0]
                stt(QF[:], bank(7), bq[:, bass.ds(h, 1)], peT[:, hf * BANK:(hf + 1) * BANK], ALU.add,
                    ALU.add).then_inc(s_qr, 1)

            batch = [0]

            def neg_max(g, i):
                dve.wait_ge(s_qk, 8 * g + i + 1)
                s = i % 2
                sc = PS[:, 2 * s:2 * s + 2, :].rearrange("p a n -> p (a n)")
                nc.vector.tensor_reduce(nmax[:, i % 4:i % 4 + 1], sc[:, 0:(i + 1) * P], AX_X, ALU.max,
                                        negate=True).then_inc(s_nm, 1)

            def low(g, i):
                for part in range(1 if i < 4 else 2):
                    c = i if i < 4 else 4 + 2 * (i - 4) + part
                    dve.wait_ge(s_ea, 12 * g + c + 1)
                    dst, src = turned(PTL, i, part, c)
                    tt(dst, src, turned(PTH, i, part, c)[0].bitcast(F32), ALU.subtract).then_inc(s_ed, 1)

            def inverse(g, s):
                dve.wait_ge(s_ex, 8 * g + 4 + 4 * s)
                nc.vector.reciprocal(rinv[:, 4 * s:4 * s + 4], rsum[:, 4 * s:4 * s + 4]).then_inc(s_ri, 1)

            def add_out(g, s, x_prev):
                dve.wait_ge(s_wo, 2 * g + 1 + s)
                dve.wait_ge(s_ri, 2 * g + 1 + s)
                if x_prev:
                    dve.wait_ge(s_we, 2 * g + s - 1)
                for t in range(4):
                    q = 4 * s + t
                    x = X[:, 8 * batch[0] + q, :]
                    r = stt(x, PS[:, 7, t * P:(t + 1) * P], rinv[:, q:q + 1], x, ALU.mult, ALU.add)
                r.then_inc(s_we, 1)

            def head(g, pending, follow, x_prev=True):
                for i in range(8):
                    neg_max(g, i)
                    if i == 0 and pending:
                        low(g - 1, 7)
                        inverse(g - 1, 1)
                    if i >= 1:
                        low(g, i - 1)
                    if i == 1 and pending:
                        add_out(g - 1, 0, x_prev)
                    if i == 2:
                        q_evac(g, 1)
                    if i == 4:
                        inverse(g, 0)
                    if i == 5 and pending:
                        add_out(g - 1, 1, x_prev)
                    if i == 6 and follow:
                        q_evac(g + 1, 0)

            def attention_start(b):
                batch[0] = b
                q_evac(8 * b, 0, b == 0)
                head(8 * b, False, True)

            def attention_rest(b):
                g = 8 * b + 1
                head(g, True, True, False)
                with dve.Fori(g + 1, g + 6) as gg:
                    head(gg, True, True)
                g = 8 * b + 7
                head(g, True, False)
                low(g, 7)
                inverse(g, 1)
                add_out(g, 0, True)
                add_out(g, 1, True)

            def experts_first():
                def rows(p, s):
                    dve.wait_ge(s_mtp[0], p + 1)
                    cp(MXT[:, 4 * s:4 * s + 4, :], bank(s).rearrange("p (i n) -> p i n", n=P)).then_inc(s_mt[0], 1)

                def result(p, s, times):
                    dve.wait_ge(s_myp[0], p + 1)
                    if times is not None:
                        dve.wait_ge(s_mo[0][s], 16 * times)
                    tt(MY[:, 4 * s:4 * s + 4, :], bank(4).rearrange("p (i n) -> p i n", n=P),
                       mw0[:, 4 * s:4 * s + 4, 4 * P + 2:4 * P + 2 + D], ALU.add).then_inc(s_my[0], 1)

                rows(0, 0)
                rows(1, 1)
                result(0, 0, None)
                rows(2, 0)
                result(1, 1, None)
                with dve.Fori(1, QUADS // 2 - 1) as r:
                    rows(2 * r + 1, 1)
                    result(2 * r, 0, r)
                    rows(2 * r + 2, 0)
                    result(2 * r + 1, 1, r)
                rows(QUADS - 1, 1)
                result(QUADS - 2, 0, QUADS // 2 - 1)
                result(QUADS - 1, 1, QUADS // 2 - 1)

            def combine_first():
                dve.wait_ge(s_g0, 16 * NT)
                for t in range(NT):
                    r = stt(X[:, t, :], GA[:, t, :], wsel[0][:, 0, t:t + 1], X[:, t, :], ALU.mult, ALU.add)
                    r.then_inc(s_gu, 1)

            def combine_second():
                for q in range(4):
                    dve.wait_ge(s_g1[q], 16 * 8)
                    for k in range(2):
                        if k:
                            dve.wait_ge(s_gu, NT + 8 * q + 4)
                        for t in range(4):
                            x = X[:, 4 * q + t, :]
                            stt(x, (GA, GB)[q // 2][:, 8 * (q % 2) + 4 * k + t, :], wsel[1][:, k, 4 * q + t:4 * q + t + 1], x,
                                ALU.mult, ALU.add).then_inc(s_gu, 1)

            attention_start(0)
            place(0)
            attention_rest(0)
            experts_first()
            attention_start(1)
            attention_rest(1)
            dve.wait_ge(s_we, 32)
            combine_first()
            dve.wait_ge(s_gu, NT)
            normalise(1)
            route(1)
            take_ranks(1)
            place(1)
            cp(pickb[:], bc(cst["pick"], 2, P)).then_inc(s_cnv, 1)
            dve.wait_ge(s_as, 1)
            link(ts(a_sc[:], a_sc[:], -1.0, None, ALU.mult))
            link(nc.vector.memset(R3[96:128, :], 0.0))
            for b in range(B):
                for q in range(4):
                    dve.wait_ge(s_dp, 4 * b + q + 1)
                    c, hf = q // 2, q % 2
                    r = ts(DL[:, c, hf * BANK:(hf + 1) * BANK], bank(4 + q), b_dl[:, c:c + 1], None, ALU.add)
                    r.then_inc(s_dr, 1)
                dve.wait_ge(s_da1, 2 * b + 2)
                ts(DA[:], DB[:], 1.0, None, ALU.add).then_inc(s_dw, 1)
                dve.wait_ge(s_dw, b + 1)
                link(stt(DU[:], DA[:], 1.0, DB[:], ALU.subtract, ALU.subtract))
                dve.wait_ge(s_dr, 4 * b + 4)
                link(stt(DL[:], DL[:], 0.0, DU[:], ALU.max, ALU.subtract))
                dve.wait_ge(s_dl, b + 1)
                link(tt(DL[:], DL[:], HS[:], ALU.add))
                dve.wait_ge(s_ue2, 8 * b + 8)
                r = tt(DU[:], DL[:], UT[:], ALU.mult)
                r.then_inc(s_du, 1)
                dve.wait_ge(s_du, b + 1)
                dve.wait_ge(s_bp, b + 1)
                bcr = PS[0:32, 0:2, :].rearrange("p a n -> p (a n)")
                rest, mid = DB[0:32, 0, :], HS[0:32, 0, 0:BANK].bitcast(BF16)
                link(cp(R3[0:32, :], bcr))
                link(tt(rest, bcr, R3[0:32, :], ALU.subtract))
                link(cp(mid, rest))
                link(cp(R3[32:64, :], mid))
                link(tt(rest, rest, mid, ALU.subtract))
                cp(R3[64:96, :], rest).then_inc(s_r3, 1)
                dve.wait_ge(s_r3, b + 1)

                def state(n, free):
                    u = 32 * b + 2 * n
                    dve.wait_ge(s_b, 16 * b + n + 1)
                    for c in range(2):
                        if free:
                            dve.wait_ge(s_sn, u + c - 1)
                        spread = PS[:, 0:2, :].rearrange("p a n -> p (a n)")
                        tt(DB[:, c, :], DU[:, c, :], spread, ALU.mult).then_inc(s_db, 1)
                    for c in range(2):
                        dve.wait_ge(s_dA, u + c + 1)
                        dve.wait_ge(s_db, u + c + 1)
                        if free:
                            dve.wait_ge(s_hc, u + c - 1)
                        nc.vector.tensor_tensor_scan(HS[:, c, :], DA[:, c, :], DB[:, c, :], 0.0, ALU.mult,
                                                     ALU.add).then_inc(s_sn, 1)
                    dve.wait_ge(s_c, 16 * b + n + 1)
                    for c in range(2):
                        dve.wait_ge(s_sn, u + c + 1)
                        if free:
                            dve.wait_ge(s_ya, u + c - 1)
                        spread = PS[:, 2:4, :].rearrange("p a n -> p (a n)")
                        tt(HC[:, c, :], HS[:, c, :], spread, ALU.mult).then_inc(s_hc, 1)

                state(0, False)
                with dve.Fori(1, STATE) as n:
                    state(n, True)
                for c in range(2):
                    dve.wait_ge(s_ya, 32 * b + 32)
                    link(stt(YA[:, c, :], UT[:, c, :], d_par[:, c:c + 1], YA[:, c, :], ALU.mult, ALU.add))
                    tt(SR[:, c, :], YA[:, c, :], SR[:, c, :], ALU.mult).then_inc(s_yt, 1)
                for q in range(2):
                    dve.wait_ge(s_op, 2 * b + q + 1)
                    x = X[:, 8 * b + 4 * q:8 * b + 4 * q + 4, :].rearrange("p t d -> p (t d)")
                    tt(x, bank(4 + q), x, ALU.add).then_inc(s_oe, 1)
            dve.wait_ge(s_oe, 4)
            combine_second()


def kernel(**inputs):
    import concourse.bacc as bacc
    from concourse.bass_utils import run_bass_kernel_spmd as run

    get = lambda n: np.asarray(inputs[n])
    by_partition = lambda a: a.reshape(-1, P).T
    cst, _ = small_constants()

    def rows_of(w):
        e, r, n = w.shape
        return w.reshape(e, r // P, P, n).transpose(0, 2, 1, 3).reshape(e, P, -1)

    b1, b2 = get("L0_ffn_b1"), get("L0_ffn_b2")
    w_0 = np.concatenate([rows_of(get("L0_ffn_w1")), rows_of(get("L0_ffn_w2")), b1.reshape(-1, 2, P).transpose(0, 2, 1),
                          np.broadcast_to(b2[:, None, :], (b2.shape[0], P, D))], 2)
    w_1 = np.concatenate([rows_of(get("L1_ffn_w1").transpose(0, 2, 1)), rows_of(get("L1_ffn_w2").transpose(0, 2, 1))], 2)
    data = {
        "x": get("L0_attn_x"), "Wkv": get("L0_attn_Wkv"), "bkv": get("L0_attn_bkv"), "bq": by_partition(get("L0_attn_bq")),
        "WqH": get("L0_attn_Wq").reshape(D, HEADS, D).transpose(1, 0, 2), "Wo": get("L0_attn_Wo"),
        "router_w": get("L0_ffn_router_w"), "w_0": w_0, "w_1": w_1, "W_in": get("L1_attn_W_in"),
        "W_delta": get("L1_attn_W_delta"), "b_delta": by_partition(get("L1_attn_b_delta")), "W_B": get("L1_attn_W_B"),
        "W_C": get("L1_attn_W_C"), "A_log": get("L1_attn_A_log"), "D_param": by_partition(get("L1_attn_D_param")),
        "W_out": get("L1_attn_W_out"), "gate_wT": get("L1_ffn_gate_w").T,
        "cst": cst, "peT": positions(),
    }
    nc = bacc.Bacc("TRN2", target_bir_lowering=False, num_devices=1)
    arrays, args = {}, {}
    for name, a in data.items():
        a = np.ascontiguousarray(a)
        arrays[f"in_{name}"] = a
        args[name] = nc.dram_tensor(f"in_{name}", a.shape, mybir.dt.from_np(a.dtype), kind="ExternalInput").ap()
    out = nc.dram_tensor("out_0", (B, T, D), F32, kind="ExternalOutput").ap()
    scratch = {
        "rows_in": [nc.dram_tensor(f"rows_in{m}", (TILES[m] * P, D), F32, kind="Internal").ap() for m in range(2)],
        "rows_out": [nc.dram_tensor(f"rows_out{m}", (TILES[m] * P, D), F32, kind="Internal").ap() for m in range(2)],
    }
    build(nc, args, out, scratch)
    r = run(nc, [arrays], core_ids=[0])
    return r.results[0]["out_0"]
```

```python
from contextlib import ExitStack

import numpy as np

import concourse.bass as bass
from concourse import mybir

ALU = mybir.AluOpType
ACT = mybir.ActivationFunctionType
F32 = mybir.dt.float32
BF16 = mybir.dt.bfloat16
F32R = mybir.dt.float32r
I32 = mybir.dt.int32
U32 = mybir.dt.uint32
AX_X = mybir.AxisListType.X

P = 128
B, T, D = 2, 1024, 128
NT = B * T // P
TB = T // P
BANK = 512
HEADS = 8
EPS = 1e-5
SCALE = float(D) ** -0.5
MASKED = -1e30
STATE = 16
INNER = 2
KEPT = 3e38
SHARED = 2

MOE = [(14, 1, 2), (8, 2, 4)]
TILES = [4 * -(-((B * T * k + e * (P - 1)) // P) // 4) for e, k, _ in MOE]
QUADS = TILES[0] // 4
PAIRS = TILES[1] // 2
LATE = PAIRS - (STATE - 4)
EARLY = 4
W_ROW = [2 * f * P + (2 + D if m == 0 else 0) for m, (_, _, f) in enumerate(MOE)]


def small_constants():
    k, m = np.arange(P)[:, None], np.arange(P)[None, :]
    parts = {
        "ident": (k == m),
        "causal": np.where(m > k, MASKED, 0.0),
        "before": (k < m),
        "pick": (k % 32 == np.arange(32)[None, :]) & (k < 96),
        "iota": np.broadcast_to(np.arange(16)[None, :] - 16.0, (P, 16)),
        "first": np.broadcast_to(np.arange(max(TILES))[None, :] * P, (P, max(TILES))),
    }
    at, cols, where = 0, [], {}
    for name, a in parts.items():
        a = np.asarray(a, np.float32)
        where[name] = (at, at + a.shape[1])
        at += a.shape[1]
        cols.append(a)
    return np.ascontiguousarray(np.concatenate(cols, 1)), where


def positions():
    pos = np.arange(T, dtype=np.float32)[:, None]
    step = np.exp(np.float32(-np.log(10000.0)) * np.arange(0, D, 2, dtype=np.float32) / np.float32(D))
    angle = pos * step.astype(np.float32)[None, :]
    pe = np.zeros((T, D), np.float32)
    pe[:, 0::2] = np.sin(angle)
    pe[:, 1::2] = np.cos(angle)
    return np.ascontiguousarray(pe.T)


def build(nc, A, out, scratch):
    _, WHERE = small_constants()
    with ExitStack() as ctx:
        def sb(name, shape, dt=F32):
            return ctx.enter_context(nc.sbuf_tensor(name, shape, dt))

        def sem(name):
            return ctx.enter_context(nc.semaphore(name))

        X = sb("X", [P, NT, D])
        XN = sb("XN", [P, NT, D])
        XNT = sb("XNT", [P, B * T])
        CST = sb("CST", [P, sum(b - a for a, b in list(WHERE.values())[-1:]) + list(WHERE.values())[-1][0]])
        cst = {n: CST[:, a:b] for n, (a, b) in WHERE.items()}
        ident = cst["ident"]
        identb = sb("identb", [P, P], BF16)
        causalb = sb("causalb", [P, P], BF16)
        beforeb = sb("beforeb", [P, P], BF16)
        onesb = sb("onesb", [P, P], BF16)
        ones1 = sb("ones1", [1, P])
        zero = sb("zero", [P, BANK])
        wgate = [sb(f"wgate{m}", [P, MOE[m][0]]) for m in range(2)]
        stats = sb("stats", [P, NT, 6])
        mv = sb("mv", [P, NT, 2])
        lnt = sb("lnt", [P, 6, NT])
        EM = 14
        lg = sb("lg", [P, NT * EM])
        oh = sb("oh", [P, 3, NT * EM])
        ohb = sb("ohb", [P, NT * EM], BF16)
        rt = sb("rt", [P, 5, NT * EM])
        seg = [sb(f"seg{m}", [P, NT * MOE[m][0]]) for m in range(2)]
        rs1 = sb("rs1", [P, 12, NT])
        re1 = sb("re1", [P, 6, 16])
        rei = sb("rei", [P, 2, 16], I32)
        tl = sb("tl", [P, max(TILES) * EM])
        wsel = [sb(f"wsel{m}", [P, MOE[m][1], NT]) for m in range(2)]
        slot = [sb(f"slot{m}", [P, MOE[m][1], NT], U32) for m in range(2)]
        eid = [sb(f"eid{m}", [P, TILES[m]], I32) for m in range(2)]
        mw0 = sb("mw0", [P, 8, W_ROW[0]])
        MX = sb("MX", [P, 8, D])
        MXT = sb("MXT", [P, 8, P])
        MH = sb("MH", [P, 8, P])
        MY = sb("MY", [P, 8, D])
        GA = sb("GA", [P, NT, D])
        w_in = sb("w_in", [P, 4 * D])
        w_dl = sb("w_dl", [P, 2, 2 * D])
        b_dl = sb("b_dl", [P, 2])
        w_bc = sb("w_bc", [P, 2, 32])
        a_lg = sb("a_lg", [P, 2, STATE])
        a_sc = sb("a_sc", [P, 2, STATE])
        d_par = sb("d_par", [P, 2])
        w_out = sb("w_out", [P, 2, D])

        with ExitStack() as first_layer:
            def sb1(name, shape, dt=F32):
                return first_layer.enter_context(nc.sbuf_tensor(name, shape, dt))

            peT = sb1("peT", [P, T])
            wkv = sb1("wkv", [P, 2 * D])
            bk = sb1("bk", [P, 1])
            bv = sb1("bv", [1, D])
            bq = sb1("bq", [P, HEADS])
            wo = sb1("wo", [P, HEADS, D])
            wq = sb1("wq", [P, 2, D])
            KH, KL = sb1("KH", [P, B, T], F32R), sb1("KL", [P, B, T], F32R)
            VH, VL = sb1("VH", [P, NT, D], F32R), sb1("VL", [P, NT, D], F32R)
            QH, QL = sb1("QH", [P, T], F32R), sb1("QL", [P, T], F32R)
            QF = sb1("QF", [P, BANK])
            PR = sb1("PR", [P, 2, T])
            PTH, PTL = sb1("PTH", [P, 12, BANK], F32R), sb1("PTL", [P, 12, BANK], F32R)
            OT = sb1("OT", [P, 2, BANK])
            nmax = sb1("nmax", [P, 4])
            rsum = sb1("rsum", [P, TB])
            rinv = sb1("rinv", [P, TB])

        def sb2(name, shape, dt=F32):
            return ctx.enter_context(nc.sbuf_tensor(name, shape, dt))

        R3 = sb2("R3", [P, T], BF16)
        DU = sb2("DU", [P, 2, T])
        UT = sb2("UT", [P, 2, T])
        SR = sb2("SR", [P, 2, T])
        pickb = sb2("pickb", [P, 32, P], BF16)
        DL = sb2("DL", [P, 2, T])
        DA = sb2("DA", [P, 2, T])
        DB = sb2("DB", [P, 2, T])
        HS = sb2("HS", [P, 2, T])
        HC = sb2("HC", [P, 2, T])
        YA = sb2("YA", [P, 2, T])
        DU1 = sb2("DU1", [P, 2, T])
        GB = sb2("GB", [P, NT, D])
        mw1 = sb2("mw1", [P, 4, W_ROW[1]])
        chunks = lambda ap: ap.rearrange("p (c t) -> p c t", c=2)
        mw0_flat = mw0[:].rearrange("p a n -> p (a n)")
        UT1 = chunks(GA[:].rearrange("p t d -> p (t d)"))
        SR1, DL1 = chunks(mw0_flat[:, 0:2 * T]), chunks(mw0_flat[:, 2 * T:4 * T])
        UTb, SRb, DLb, DUb = (UT[:], UT1), (SR[:], SR1), (DL[:], DL1), (DU[:], DU1[:])
        S1b = (DA[:], DU1[:])
        S2b = (DB[:], chunks(GB[:].rearrange("p t d -> p (t d)")))
        S3b = (HS[:], chunks(XNT[:]))
        R3b = (R3[:], zero[:].bitcast(BF16))
        c_half = MXT[:, 4:8, :].rearrange("p i n -> p (i n)")
        G1b = (UT[:].rearrange("p c (t d) -> p (c t) d", d=D), GB[:])
        PS = ctx.enter_context(nc.psum_tensor("PS", [P, 8, BANK], F32))

        def bank(k, n=BANK):
            return PS[:, k, 0:n]

        s_x = sem("x_loaded")
        s_cst = sem("constants_loaded")
        s_cnv = sem("constants_converted")
        s_wat = sem("attention_weights_loaded")
        s_wsc = sem("scan_weights_loaded")
        s_zero = sem("zero_tile_ready")
        s_zf = sem("rows_zeroed")
        s_v = sem("vector_step")
        s_var = sem("variance_ready")
        s_sd = sem("deviation_ready")
        s_xn = sem("normalised_ready")
        s_tp = sem("transposed_in_psum")
        s_xnt = sem("transposed_ready")
        s_lg = sem("logits_in_psum")
        s_lgr = sem("logits_read")
        s_kp = sem("keys_in_psum")
        s_ke = sem("keys_ready")
        s_vp = sem("values_in_psum")
        s_ve = sem("values_ready")
        s_ein = sem("gate_exponent_in")
        s_eout = sem("gate_exponent_out")
        s_ohb = sem("onehot_ready")
        s_rk = sem("ranks_in_psum")
        s_rkr = sem("ranks_read")
        s_slot = sem("slots_ready")
        s_eid = sem("tile_experts_ready")
        s_sc = [sem(f"rows_scattered{m}") for m in range(2)]
        s_wq = [sem(f"wq_loaded{i}") for i in range(2)]
        s_qp = sem("query_in_psum")
        s_qr = sem("query_left_psum")
        s_qh = sem("query_high_ready")
        s_qe = sem("query_ready")
        s_kf = sem("key_summed")
        s_kh = sem("key_high_ready")
        s_vh = sem("value_high_ready")
        s_qk = sem("scores_ready")
        s_nm = sem("negmax_ready")
        s_ex = sem("probs_ready")
        s_tc = sem("probs_transposed")
        s_ea = sem("probsT_high_ready")
        s_ed = sem("probsT_ready")
        s_pv = sem("head_out_in_psum")
        s_ue = sem("head_out_ready")
        s_ri = sem("inverse_sum_ready")
        s_wo = sem("projected_in_psum")
        s_we = sem("projected_added")
        s_mw = [[sem(f"expert_weights{m}{i}") for i in range(2)] for m in range(2)]
        s_mx = [[sem(f"expert_rows{m}{i}") for i in range(2)] for m in range(2)]
        s_mtp = [sem(f"expert_rowsT_in_psum{m}") for m in range(2)]
        s_mt = [sem(f"expert_rowsT_ready{m}") for m in range(2)]
        s_mhp = [sem(f"expert_hidden_in_psum{m}") for m in range(2)]
        s_mh = [sem(f"expert_hidden_ready{m}") for m in range(2)]
        s_myp = [sem(f"expert_out_in_psum{m}") for m in range(2)]
        s_my = [sem(f"expert_out_ready{m}") for m in range(2)]
        s_mo = [[sem(f"expert_out_stored{m}{i}") for i in range(2)] for m in range(2)]
        s_g0 = [sem(f"first_rows_gathered{b}") for b in range(B)]
        s_g1 = [sem(f"second_rows_gathered{q}") for q in range(4)]
        s_gu = sem("gathered_added")
        s_up = sem("inner_in_psum")
        s_ue2 = sem("inner_ready")
        s_dp = sem("delta_in_psum")
        s_da1 = sem("delta_abs_ready")
        s_dr = sem("delta_psum_read")
        s_dw = sem("delta_one_plus_ready")
        s_dl = sem("delta_log_ready")
        s_du = sem("delta_u_ready")
        s_bp = sem("bc_rows_in_psum")
        s_r3 = sem("bc_split_ready")
        s_as = sem("decay_rates_ready")
        s_b = sem("b_spread")
        s_c = sem("c_spread")
        s_dA = sem("decay_ready")
        s_db = sem("drive_ready")
        s_sn = sem("state_ready")
        s_hc = sem("state_c_ready")
        s_cc = sem("c_copied")
        s_hp = sem("state_c_last_quarter_ready")
        s_ya = sem("y_added")
        s_yb = sem("y_base_ready")
        s_yp = sem("y_added_in_psum")
        s_yt = sem("y_gated")
        s_op = sem("scan_out_in_psum")
        s_oe = sem("scan_out_added")
        s_end = sem("output_stored")

        xs = scratch["rows_in"]
        ys = scratch["rows_out"]
        zero_fills = sum(-(-TILES[m] * D // BANK) for m in range(2))

        def bc(ap, axis, n):
            shape = list(ap.shape)
            return ap.unsqueeze(axis).broadcast_to(shape[:axis] + [n] + shape[axis:])

        def turned(pt, i, part, c):
            n, at = (i + 1, 0) if i < 4 else (4, 4) if part == 0 else (i - 3, 8)
            src = PS[:, 4 + c % 2, 0:n * P].rearrange("p (j q) -> p j q", q=P)
            return pt[:, at:at + n, (i % 4) * P:(i % 4 + 1) * P], src

        TURN_BANK = (4, 6, 2, 6)
        RANK_BANK = (7, 2)
        INNER_BANKS = ((1, 2, 3), (4, 5, 6, 7))
        STEP_BANKS = ((4, 5, 2, 3), (4, 5, 6, 7))
        OUT_BANK = (4, 0)

        block = ctx.enter_context(nc.Block())

        @block.sync
        def _(sp):
            for q in range(4):
                sp.dma_start(X[:, 4 * q:4 * q + 4, :],
                             A["x"].rearrange("b (t p) d -> p (b t) d", p=P)[:, 4 * q:4 * q + 4, :]
                             ).then_inc(s_x, 16)
            sp.dma_start(CST[:], A["cst"]).then_inc(s_cst, 16)
            for dst, src in ((wkv[:], A["Wkv"]), (peT[:], A["peT"]),
                             (bk[:], A["bkv"][0:D].rearrange("(p o) -> p o", o=1)),
                             (bv[:], A["bkv"][D:2 * D].rearrange("(o d) -> o d", o=1)),
                             (bq[:], A["bq"]),
                             (wgate[0][:], A["router_w"]),
                             (wo[:], A["Wo"].rearrange("(h p) d -> p h d", p=P)),
                             (wgate[1][:], A["gate_wT"])):
                sp.dma_start(dst, src).then_inc(s_wat, 16)
            sp.wait_ge(s_zero, 1)
            for m in range(2):
                flat = xs[m].rearrange("(p r) d -> p (r d)", p=P)
                for c in range(0, TILES[m] * D, 512):
                    w = min(512, TILES[m] * D - c)
                    sp.dma_start(flat[:, c:c + w], zero[:, 0:w]).then_inc(s_zf, 16)
            for dst, src in ((w_in[:], A["W_in"]),
                             (w_dl[:], A["W_delta"].rearrange("(k p) n -> p k n", p=P)),
                             (b_dl[:], A["b_delta"]),
                             (w_bc[:, :, 0:STATE], A["W_B"].rearrange("(k p) n -> p k n", p=P)),
                             (w_bc[:, :, STATE:32], A["W_C"].rearrange("(k p) n -> p k n", p=P)),
                             (a_lg[:], A["A_log"].rearrange("(k p) n -> p k n", p=P)),
                             (d_par[:], A["D_param"]),
                             (w_out[:], A["W_out"].rearrange("(k p) n -> p k n", p=P))):
                sp.dma_start(dst, src).then_inc(s_wsc, 16)

            def load_wq(g, h, i, free):
                if free is not None:
                    sp.wait_ge(s_qp, free)
                sp.dma_start(wq[:, i, :], A["WqH"][h]).then_inc(s_wq[i], 16)

            def attention_loads(b):
                load_wq(8 * b, 0, 0, None if b == 0 else 16 * b - 2)
                load_wq(8 * b + 1, 1, 1, None if b == 0 else 16 * b)
                with sp.Fori(1, 4) as r:
                    load_wq(None, 2 * r, 0, 16 * b + 4 * r - 2)
                    load_wq(None, 2 * r + 1, 1, 16 * b + 4 * r)

            def expert_loads(m):
                e_n, k_n, f_n = MOE[m]
                sp.wait_ge(s_eid, m + 1)
                sp.wait_ge(s_sc[m], 16 * NT * k_n)

                tiles, groups = (4, QUADS) if m == 0 else (2, PAIRS)
                mw = (mw0, mw1)[m]

                def group(p, s, first):
                    if not first:
                        sp.wait_ge(s_mtp[m], p - 1)
                    sp.dma_start(MX[:, tiles * s:tiles * s + tiles, :],
                                 xs[m][bass.ds(p * tiles * P, tiles * P), :].rearrange("(i p) d -> p i d", p=P)
                                 ).then_inc(s_mx[m][s], 16)
                    if not first:
                        sp.wait_ge((s_my, s_myp)[m][m], p - 1)
                    for i in range(tiles):
                        e = sp.value_load(eid[m][0:1, bass.ds(tiles * p + i, 1)], min_val=0, max_val=e_n - 1)
                        sp.dma_start(mw[:, tiles * s + i, :], A[f"w_{m}"][bass.ds(e, 1)].rearrange("o p n -> (o p) n")
                                     ).then_inc(s_mw[m][s], 16)

                group(0, 0, True)
                group(1, 1, True)
                with sp.Fori(1, groups // 2) as r:
                    group(2 * r, 0, False)
                    group(2 * r + 1, 1, False)

            attention_loads(0)
            expert_loads(0)
            attention_loads(1)
            sp.wait_ge(s_myp[0], QUADS)
            sp.wait_ge(s_we, 4 * HEADS)
            expert_loads(1)
            ov = out.rearrange("b (t p) d -> p (b t) d", p=P)
            for q in range(4):
                sp.wait_ge(*((s_gu, NT + 8 * (q + 1)) if q < 2 else (s_oe, q + 1)))
                sp.dma_start(ov[:, 4 * q:4 * q + 4, :], X[:, 4 * q:4 * q + 4, :]).then_inc(s_end, 16)
            sp.wait_ge(s_end, 64)

        @block.gpsimd
        def _(pool):
            nc.gpsimd.memset(zero[:], 0.0).then_inc(s_zero, 1)

            def scatter(m, tiles):
                for k in range(MOE[m][1]):
                    for t in tiles:
                        nc.gpsimd.indirect_dma_start(
                            out=xs[m][:, :], out_offset=bass.IndirectOffsetOnAxis(ap=slot[m][:, k, t:t + 1], axis=0),
                            in_=XN[:, t, :], in_offset=None).then_inc(s_sc[m], 16)

            def gather(m, k, t, dst, s):
                nc.gpsimd.indirect_dma_start(
                    out=dst, out_offset=None, in_=ys[m][:, :],
                    in_offset=bass.IndirectOffsetOnAxis(ap=slot[m][:, k, t:t + 1], axis=0)).then_inc(s, 16)

            def query_low(g, hf):
                pool.wait_ge(s_qh, 2 * g + hf + 1)
                sl = slice(hf * BANK, (hf + 1) * BANK)
                nc.gpsimd.tensor_tensor(QL[:, sl], QF[:], QH[:, sl].bitcast(F32), ALU.subtract).then_inc(s_qe, 1)

            def attention(b):
                query_low(8 * b, 0)
                for h in range(HEADS):
                    query_low(8 * b + h, 1)
                    if b == 0:
                        if h == 0:
                            pool.wait_ge(s_slot, 1)
                            pool.wait_ge(s_zf, 16 * zero_fills)
                        scatter(0, (2 * h, 2 * h + 1))
                    else:
                        for t in (2 * h, 2 * h + 1):
                            gather(0, 0, t, GA[:, t, :], s_g0[t // TB])
                    if h < HEADS - 1:
                        query_low(8 * b + h + 1, 0)

            attention(0)
            for i in range(2):
                pool.wait_ge(s_mo[0][i], 16 * (QUADS // 2))
            attention(1)

            pool.wait_ge(s_slot, 2)
            scatter(1, range(NT))

            def quarter(b, n, late=None):
                pool.wait_ge(s_sn, 32 * b + 2 * n + 2)
                if late is None:
                    pool.wait_ge(s_ya, 32 * b + 2 * n)
                else:
                    pool.wait_ge(s_yp, late)
                pool.wait_ge(s_cc, STATE * b + n + 1 - SHARED)
                nc.gpsimd.tensor_tensor(HC[:, 1, BANK:T], HS[:, 1, BANK:T], c_half, ALU.mult).then_inc(s_hp, 1)

            def add(b, n, c, shared=True):
                if c == 0 and shared:
                    quarter(b, n)
                if c == 1 and shared:
                    pool.wait_ge(s_hp, STATE * b + n + 1 - SHARED)
                pool.wait_ge(s_hc, 32 * b + 2 * n + c + 1)
                pool.wait_ge(s_ya, 32 * b + 2 * n + c - 1)
                nc.gpsimd.tensor_tensor(YA[:, c, :], YA[:, c, :], HC[:, c, :], ALU.add).then_inc(s_ya, 1)

            def start(b):
                if b:
                    quarter(b, 0)
                    pool.wait_ge(s_hp, STATE * b + 1 - SHARED)
                for c in range(2):
                    pool.wait_ge(s_hc, 32 * b + c + 1)
                    if b:
                        pool.wait_ge(s_yt, 2 * b - 1 + c)
                    nc.gpsimd.tensor_copy(YA[:, c, :], HC[:, c, :]).then_inc(s_ya, 1)

            start(0)
            for n in range(1, SHARED):
                add(0, n, 0, False)
                add(0, n, 1, False)
            with pool.Fori(SHARED, STATE) as n:
                add(0, n, 0)
                add(0, n, 1)
            start(1)
            with pool.Fori(1, LATE) as n:
                add(1, n, 0)
                add(1, n, 1)
            for i in range(2):
                pool.wait_ge(s_mo[1][i], 16 * (PAIRS // 2))
            rows = [(q, k, t) for q in range(4) for k in range(2) for t in range(4)]
            each = -(-len(rows) // (STATE - LATE))
            for n in range(LATE, STATE):
                for q, k, t in rows[each * (n - LATE):each * (n - LATE + 1)]:
                    gather(1, k, 4 * q + t, G1b[q // 2][:, 8 * (q % 2) + 4 * k + t, :], s_g1[q])
                quarter(1, n, 2 * (n - LATE) if n > LATE else None)

        @block.scalar
        def _(act):
            def deviation(ph):
                act.wait_ge(s_var, ph + 1)
                r = slice((ph % 2) * TB, (ph % 2 + 1) * TB)
                nc.scalar.activation(lnt[:, 1, r], lnt[:, 0, r], ACT.Sqrt).then_inc(s_sd, 1)

            def take_transposed(ph):
                for q in range(2):
                    act.wait_ge(s_tp, 2 * ph + q + 1)
                    nc.scalar.copy(XNT[:, (2 * (ph % 2) + q) * BANK:(2 * (ph % 2) + q + 1) * BANK],
                                   bank(TURN_BANK[ph] + q)).then_inc(s_xnt, 1)

            def gate_exp(ph):
                act.wait_ge(s_ein, ph + 1)
                n = NT * MOE[0][0] if ph == 0 else NT
                src = rt[:, 0, 0:n] if ph == 0 else rs1[:, 5, :]
                dst = rt[:, 1, 0:n] if ph == 0 else rs1[:, 6, :]
                nc.scalar.activation(dst, src, ACT.Exp).then_inc(s_eout, 1)

            for ph in range(2):
                deviation(ph)
                take_transposed(ph)
            for q in range(4):
                act.wait_ge(s_vp, q + 1)
                nc.scalar.copy(VH[:, 4 * q:4 * q + 4, :], bank((5, 6, 7, 1)[q])).then_inc(s_vh, 1)
                act.wait_ge(s_kf, 2 * q + 2)
                nc.scalar.copy(KH[:, q // 2, (q % 2) * BANK:(q % 2 + 1) * BANK], QF[:]).then_inc(s_kh, 1)
            gate_exp(0)

            def out_evac(s, done):
                act.wait_ge(s_pv, done)
                nc.scalar.copy(OT[:, s, :], bank(6)).then_inc(s_ue, 1)

            def query_high(g, hf):
                act.wait_ge(s_qr, 2 * g + hf + 1)
                nc.scalar.copy(QH[:, hf * BANK:(hf + 1) * BANK], QF[:]).then_inc(s_qh, 1)

            def high(g, i):
                for part in range(1 if i < 4 else 2):
                    c = i if i < 4 else 4 + 2 * (i - 4) + part
                    act.wait_ge(s_tc, 12 * g + c + 1)
                    dst, src = turned(PTH, i, part, c)
                    nc.scalar.copy(dst, src).then_inc(s_ea, 1)

            def exps(g, i):
                act.wait_ge(s_nm, 8 * g + i + 1)
                nk = (i + 1) * P
                s = i % 2
                sc = PS[:, 2 * s:2 * s + 2, :].rearrange("p a n -> p (a n)")
                nc.scalar.activation(PR[:, s, 0:nk], sc[:, 0:nk], ACT.Exp, bias=nmax[:, i % 4:i % 4 + 1],
                                     accum_out=rsum[:, i:i + 1]).then_inc(s_ex, 1)

            def head(g, pending, follow, last=False):
                for i in range(8):
                    if i == 5 and last:
                        act.wait_ge(s_wsc, 16 * 8)
                        nc.scalar.activation(a_sc[:], a_lg[:], ACT.Exp).then_inc(s_as, 1)
                        deviation(2)
                    if i == 3:
                        query_high(g, 1)
                    if i == 7 and follow:
                        query_high(g + 1, 0)
                    if i == 0 and pending:
                        out_evac(0, 2 * g - 1)
                        high(g - 1, 7)
                    if i == 4 and pending:
                        out_evac(1, 2 * g)
                    if i >= 1:
                        high(g, i - 1)
                    exps(g, i)

            def attention(b):
                query_high(8 * b, 0)
                head(8 * b, False, True)
                with act.Fori(8 * b + 1, 8 * b + 7) as g:
                    head(g, True, True)
                g = 8 * b + 7
                head(g, True, False, b == 1)
                g += 1
                out_evac(0, 2 * g - 1)
                high(g - 1, 7)
                if b == 1:
                    take_transposed(2)
                out_evac(1, 2 * g)

            def experts_first():
                def quad(p, s):
                    for i in range(4):
                        for c in range(2):
                            if c == 0 and i % 2 == 0:
                                act.wait_ge(s_mhp[0], 2 * p + i // 2 + 1)
                            w = mw0[:, 4 * s + i, 4 * P:4 * P + 2]
                            r = nc.scalar.activation(MH[:, 2 * i + c, :], PS[:, 2 + i // 2, (2 * (i % 2) + c) * P:(2 * (i % 2) + c + 1) * P],
                                                     ACT.Gelu, bias=w[:, c:c + 1])
                        r.then_inc(s_mh[0], 1)

                def store(p, s):
                    act.wait_ge(s_my[0], p + 1)
                    act.dma_start(ys[0][bass.ds(p * 4 * P, 4 * P), :].rearrange("(i p) d -> p i d", p=P), MY[:, 4 * s:4 * s + 4, :]
                                  ).then_inc(s_mo[0][s], 16)

                with act.Fori(0, QUADS // 2) as r:
                    for s in range(2):
                        quad(2 * r + s, s)
                        store(2 * r + s, s)

            def pair_in(p):
                act.wait_ge(s_mtp[1], p + 1)
                nc.scalar.copy(MXT[:, 0:2, :], PS[:, 4, 0:2 * P].rearrange("p (i n) -> p i n", i=2)).then_inc(s_mt[1], 1)

            def pair_out(p, s, times):
                act.wait_ge(s_myp[1], p)
                if times is not None:
                    act.wait_ge(s_mo[1][s], times)
                nc.scalar.copy(MY[:, 2 * s:2 * s + 2, :], PS[:, 7, 0:2 * P].rearrange("p (i n) -> p i n", i=2)).then_inc(s_my[1], 1)
                act.wait_ge(s_my[1], p)
                act.dma_start(ys[1][bass.ds((p - 1) * 2 * P, 2 * P), :].rearrange("(i p) d -> p i d", p=P), MY[:, 2 * s:2 * s + 2, :]
                              ).then_inc(s_mo[1][s], 16)

            def pair_hidden(p):
                for i in range(2):
                    act.wait_ge(s_mhp[1], 2 * p + i + 1)
                    nc.scalar.activation(MH[:, 4 * i:4 * i + 4, :], bank(5 + i).rearrange("p (c n) -> p c n", n=P),
                                         ACT.Relu).then_inc(s_mh[1], 1)

            attention(0)
            experts_first()
            attention(1)
            def inner(b):
                for q in range(8):
                    act.wait_ge(s_up, 8 * b + q + 1)
                    c, hf = q // 2, q % 2
                    dst = (UTb if c < 2 else SRb)[b][:, c % 2, hf * BANK:(hf + 1) * BANK]
                    nc.scalar.activation(dst, bank(INNER_BANKS[b][q % len(INNER_BANKS[b])]), ACT.Silu).then_inc(s_ue2, 1)

            def step_sizes(b):
                for q in range(4):
                    act.wait_ge(s_dp, 4 * b + q + 1)
                    c, sl = q // 2, slice((q % 2) * BANK, (q % 2 + 1) * BANK)
                    nc.scalar.activation(S1b[b][:, c, sl], bank(STEP_BANKS[b][q]), ACT.Abs, bias=b_dl[:, c:c + 1]).then_inc(s_da1, 1)
                    nc.scalar.activation(DLb[b][:, c, sl], bank(STEP_BANKS[b][q]), ACT.Relu, bias=b_dl[:, c:c + 1]).then_inc(s_dr, 1)
                act.wait_ge(s_da1, 5 * b + 4)
                nc.scalar.activation(S2b[b], S1b[b], ACT.Exp, scale=-1.0).then_inc(s_da1, 1)

            def logarithm(b):
                act.wait_ge(s_dw, b + 1)
                nc.scalar.activation(S3b[b], S1b[b], ACT.Ln).then_inc(s_dl, 1)

            def decay(b, n, free):
                for c in range(2):
                    if free:
                        act.wait_ge(s_sn, 32 * b + 2 * n + c - 1)
                    nc.scalar.activation(DA[:, c, :], DLb[b][:, c, :], ACT.Exp,
                                         scale=a_sc[:, c, bass.ds(n, 1)]).then_inc(s_dA, 1)

            def copy_c(b, n, free=True):
                act.wait_ge(s_c, STATE * b + n + 1)
                if free:
                    act.wait_ge(s_hp, STATE * b + n - SHARED)
                nc.scalar.copy(c_half, bank(3)).then_inc(s_cc, 1)

            def beside(b, n, p, s, times):
                decay(b, n, True)
                copy_c(b, n)
                pair_in(p)
                pair_out(p, 1 - s, times)
                pair_hidden(p)

            inner(0)
            deviation(3)
            step_sizes(0)
            take_transposed(3)
            logarithm(0)
            nc.scalar.copy(pickb[:], bc(cst["pick"], 2, P)).then_inc(s_as, 1)
            act.wait_ge(s_gu, NT)
            inner(1)
            act.wait_ge(s_du, 1)
            decay(0, 0, False)
            gate_exp(1)
            step_sizes(1)
            decay(0, 1, True)
            logarithm(1)
            decay(0, SHARED, True)
            copy_c(0, SHARED, False)
            with act.Fori(SHARED + 1, EARLY) as n:
                decay(0, n, True)
                copy_c(0, n)
            decay(0, EARLY, True)
            copy_c(0, EARLY)
            pair_in(0)
            pair_hidden(0)
            beside(0, EARLY + 1, 1, 1, None)
            decay(0, EARLY + 2, True)
            copy_c(0, EARLY + 2)
            pair_in(2)
            pair_out(2, 1, None)
            pair_hidden(2)
            beside(0, EARLY + 3, 3, 1, 16)
            with act.Fori(2, (STATE - EARLY) // 2) as r:
                beside(0, EARLY + 2 * r, 2 * r, 0, 16 * r - 16)
                beside(0, EARLY + 2 * r + 1, 2 * r + 1, 1, 16 * r)
            done = STATE - EARLY
            with act.Fori(0, LATE // 2) as r:
                beside(1, 2 * r, done + 2 * r, 0, 16 * r + 8 * done - 16)
                beside(1, 2 * r + 1, done + 2 * r + 1, 1, 16 * r + 8 * done)
            pair_out(PAIRS, 1, 8 * PAIRS - 16)
            with act.Fori(LATE, STATE) as n:
                decay(1, n, True)
                copy_c(1, n)

        @block.tensor
        def _(pe):
            mm = nc.tensor.matmul

            def transposes(ph):
                for q in range(2):
                    pe.wait_ge(s_xn, 2 * ph + q + 1)
                    for t in range(4):
                        r = nc.tensor.transpose(PS[:, TURN_BANK[ph] + q, t * P:(t + 1) * P],
                                                XN[:, TB * (ph % 2) + 4 * q + t, :], ident)
                    r.then_inc(s_tp, 1)

            def logits(ph):
                m, b = ph // 2, ph % 2
                e_n = MOE[m][0]
                pe.wait_ge(s_xnt, 2 * ph + 2)
                for t in range(TB * b, TB * b + TB):
                    r = mm(PS[:, 0, t * e_n:(t + 1) * e_n], XNT[:, t * P:(t + 1) * P], wgate[m][:], start=True, stop=True)
                if b:
                    r.then_inc(s_lg, 1)

            def ranks(ph):
                n = NT * MOE[ph][0]
                pe.wait_ge(s_ohb, ph + 1)
                mm(PS[:, RANK_BANK[ph], 0:n], beforeb[:], ohb[:, 0:n], start=True, stop=True)
                mm(PS[:, RANK_BANK[ph], 256:256 + n], onesb[:], ohb[:, 0:n], start=True, stop=True).then_inc(s_rk, 1)

            pe.wait_ge(s_cst, 16)
            transposes(0)
            transposes(1)
            pe.wait_ge(s_wat, 16 * 8)
            logits(0)
            logits(1)
            for q in range(4):
                mm(bank(1 + q), wkv[:, 0:D], XNT[:, q * BANK:(q + 1) * BANK], start=True, stop=True).then_inc(s_kp, 1)
            pe.wait_ge(s_cnv, 1)
            for q in range(4):
                if q == 3:
                    pe.wait_ge(s_kf, 1)
                bk_ = (5, 6, 7, 1)[q]
                for t in range(4):
                    dst = PS[:, bk_, t * D:(t + 1) * D]
                    mm(dst, XNT[:, (4 * q + t) * P:(4 * q + t + 1) * P], wkv[:, D:2 * D], start=True, stop=False)
                    r = mm(dst, ones1[:], bv[:], start=False, stop=True)
                r.then_inc(s_vp, 1)
            pe.wait_ge(s_ve, 3)
            ranks(0)
            pe.wait_ge(s_ke, 4)
            pe.wait_ge(s_ve, 4)
            pe.wait_ge(s_rkr, 1)

            def query(g, h, b, hf):
                r = mm(bank(7), wq[:, h % 2 if isinstance(h, int) else parity[0], :],
                       XNT[:, b * T + hf * BANK:b * T + (hf + 1) * BANK], start=True, stop=True)
                r.then_inc(s_qp, 1)

            parity = [0]

            def three(dst, a, b_, ra, rb, first):
                mm(dst, a[0][ra], b_[0][rb], start=first, stop=False, skip_group_check=True)
                mm(dst, a[0][ra], b_[1][rb], start=False, stop=False, skip_group_check=True)
                return mm(dst, a[1][ra], b_[0][rb], start=False, stop=True, skip_group_check=True)

            def scores(g, b, i, free):
                if free:
                    pe.wait_ge(s_ex, 8 * g + i - 1)
                nk = (i + 1) * P
                s = 2 * (i % 2)
                q = (slice(None), slice(i * P, (i + 1) * P))
                for lo in range(0, nk, BANK):
                    hi = min(nk, lo + BANK)
                    three(PS[:, s + lo // BANK, 0:hi - lo], (QH, QL), (KH, KL), q, (slice(None), b, slice(lo, hi)), True)
                mm(PS[:, s + i // 4, (i % 4) * P:(i % 4 + 1) * P], identb[:], causalb[:], start=False, stop=True,
                   skip_group_check=True).then_inc(s_qk, 1)

            def turn(g, i, first=False):
                pe.wait_ge(s_ex, 8 * g + i + 1)
                for part in range(1 if i < 4 else 2):
                    c = i if i < 4 else 4 + 2 * (i - 4) + part
                    if not (first and c < 2):
                        pe.wait_ge(s_ed, 12 * g + c - 1)
                    lo, hi = 4 * part, min(i + 1, 4 * part + 4)
                    for j in range(lo, hi):
                        r = nc.tensor.transpose(PS[:, 4 + c % 2, (j - lo) * P:(j - lo + 1) * P],
                                                PR[:, i % 2, j * P:(j + 1) * P], ident)
                    r.then_inc(s_tc, 1)

            def out_part(g, b, group, part, free=True):
                if part == 0:
                    pe.wait_ge(s_ed, 12 * g + (11 if group else 4))
                    if group or free:
                        pe.wait_ge(s_ue, 2 * g + group)
                if part == 2 and group:
                    pe.wait_ge(s_ed, 12 * g + 12)
                for j in ((2 * part, 2 * part + 1) if group else (part,)):
                    lo = max(0, j - 4 * group) * P
                    r = three(PS[:, 6, lo:BANK], (VH, VL), (PTH, PTL), (slice(None), b * TB + j, slice(None)),
                              (slice(None), 4 * group + j, slice(lo, BANK)), j == 0)
                if part == 3:
                    r.then_inc(s_pv, 1)

            def inner(b, steps=range(8)):
                banks = INNER_BANKS[b]
                for q in steps:
                    c, hf = q // 2, q % 2
                    if q >= len(banks):
                        pe.wait_ge(s_ue2, 8 * b + q - len(banks) + 1)
                    if b and q == 0:
                        pe.wait_ge(s_dr, 4)
                        pe.wait_ge(s_xnt, 8)
                    mm(bank(banks[q % len(banks)]), w_in[:, c * P:(c + 1) * P],
                       XNT[:, b * T + hf * BANK:b * T + (hf + 1) * BANK], start=True, stop=True).then_inc(s_up, 1)

            def project(g, h, s):
                pe.wait_ge(s_ue, 2 * g + 1 + s)
                for t in range(4):
                    r = mm(PS[:, 7, t * P:(t + 1) * P], OT[:, s, t * P:(t + 1) * P],
                           wo[:, bass.ds(h, 1), :].rearrange("p o d -> p (o d)"), start=True, stop=True)
                r.then_inc(s_wo, 1)

            def head(g, b, h, s, pending, follow):
                pe.wait_ge(s_qe, 2 * g + 1)
                for i in range(8):
                    if i == 4:
                        pe.wait_ge(s_qe, 2 * g + 2)
                    scores(g, b, i, not (isinstance(g, int) and g == 0 and i < 2))
                    if i == 0 and pending:
                        out_part(g - 1, b, 0, 3)
                        turn(g - 1, 7)
                    if pending and 1 <= i <= 4:
                        out_part(g - 1, b, 1, i - 1)
                    if i >= 5:
                        out_part(g, b, 0, i - 5, not (isinstance(g, int) and g == 0))
                    if i >= 1:
                        turn(g, i - 1, isinstance(g, int) and g == 0)
                    if i == 1 and pending:
                        pe.wait_ge(s_qr, 2 * g + 1)
                        project(g - 1, h - 1, 0)
                    if i == 2:
                        pe.wait_ge(*((s_we, 2 * g - 1) if pending else (s_qr, 2 * g + 1)))
                        parity[0] = s
                        query(g, h, b, 1)
                    if i == 5 and pending:
                        pe.wait_ge(s_qr, 2 * g + 2)
                        project(g - 1, h - 1, 1)
                    if i == 6 and follow is not None:
                        pe.wait_ge(*((s_we, 2 * g) if pending else (s_qr, 2 * g + 2)))
                        pe.wait_ge(s_wq[1 - s], follow)
                        parity[0] = 1 - s
                        query(g + 1, h + 1, b, 0)

            def attention(b):
                pe.wait_ge(s_wq[0], 64 * b + 16)
                query(8 * b, 0, b, 0)
                head(8 * b, b, 0, 0, False, 64 * b + 16)
                with pe.Fori(0, 3) as r:
                    head(8 * b + 1 + 2 * r, b, 1 + 2 * r, 1, True, 64 * b + 16 * r + 32)
                    head(8 * b + 2 + 2 * r, b, 2 + 2 * r, 0, True, 64 * b + 16 * r + 32)
                g = 8 * b + 7
                head(g, b, 7, 1, True, None)
                out_part(g, b, 0, 3)
                turn(g, 7)
                if b == 1:
                    transposes(2)
                for part in range(4):
                    out_part(g, b, 1, part)
                pe.wait_ge(s_we, 2 * g)
                project(g, 7, 0)
                if b == 1:
                    pe.wait_ge(s_xnt, 6)
                    pe.wait_ge(s_wsc, 16 * 8)
                    inner(0, range(3))
                pe.wait_ge(s_we, 2 * g + 1)
                project(g, 7, 1)
                if b == 0:
                    pe.wait_ge(s_we, 2 * g + 2)

            def experts_first():
                def turn_rows(p, s, times, first=False):
                    pe.wait_ge(s_mx[0][s], 16 * times)
                    if not first:
                        pe.wait_ge(s_mt[0], p - 1)
                    for i in range(4):
                        r = nc.tensor.transpose(PS[:, s, i * P:(i + 1) * P], MX[:, 4 * s + i, :], ident)
                    r.then_inc(s_mtp[0], 1)

                def hidden(p, s, times):
                    pe.wait_ge(s_mt[0], p + 1)
                    pe.wait_ge(s_mw[0][s], 64 * times)
                    for i in range(4):
                        for c in range(2):
                            r = mm(PS[:, 2 + i // 2, (2 * (i % 2) + c) * P:(2 * (i % 2) + c + 1) * P],
                                   mw0[:, 4 * s + i, c * P:(c + 1) * P], MXT[:, 4 * s + i, :], start=True, stop=True)
                        if i % 2:
                            r.then_inc(s_mhp[0], 1)

                def result(p, s, first=False):
                    if not first:
                        pe.wait_ge(s_my[0], p)
                    for i in range(4):
                        pe.wait_ge(s_mh[0], 4 * p + i + 1)
                        for c in range(2):
                            r = mm(PS[:, 4, i * P:(i + 1) * P], MH[:, 2 * i + c, :], mw0[:, 4 * s + i, (2 + c) * P:(3 + c) * P],
                                   start=(c == 0), stop=(c == 1))
                    r.then_inc(s_myp[0], 1)

                turn_rows(0, 0, 1, True)
                hidden(0, 0, 1)
                turn_rows(1, 1, 1, True)
                result(0, 0, True)
                hidden(1, 1, 1)
                with pe.Fori(1, QUADS // 2) as r:
                    for s in range(2):
                        turn_rows(2 * r + s, s, r + 1)
                        result(2 * r + s - 1, 1 - s)
                        hidden(2 * r + s, s, r + 1)
                result(QUADS - 1, 1)
                pe.wait_ge(s_my[0], QUADS)

            def turn_pair(p, s, times):
                pe.wait_ge(s_mx[1][s], 16 * times)
                if not (isinstance(p, int) and p == 0):
                    pe.wait_ge(s_mt[1], p)
                for i in range(2):
                    r = nc.tensor.transpose(PS[:, 4, i * P:(i + 1) * P], MX[:, 2 * s + i, :], ident)
                r.then_inc(s_mtp[1], 1)

            def hidden_pair(p, s, times):
                pe.wait_ge(s_mt[1], p + 1)
                pe.wait_ge(s_mw[1][s], 32 * times)
                for i in range(2):
                    for c in range(4):
                        r = mm(PS[:, 5 + i, c * P:(c + 1) * P], mw1[:, 2 * s + i, c * P:(c + 1) * P], MXT[:, i, :],
                               start=True, stop=True)
                    r.then_inc(s_mhp[1], 1)

            def result_pair(p, s):
                if not (isinstance(p, int) and p == 0):
                    pe.wait_ge(s_my[1], p)
                for i in range(2):
                    pe.wait_ge(s_mh[1], 2 * p + i + 1)
                    for c in range(4):
                        r = mm(PS[:, 7, i * P:(i + 1) * P], MH[:, 4 * i + c, :], mw1[:, 2 * s + i, (4 + c) * P:(5 + c) * P],
                               start=(c == 0), stop=(c == 3))
                r.then_inc(s_myp[1], 1)

            attention(0)
            experts_first()
            attention(1)
            def step_sizes(b):
                pe.wait_ge(s_ue2, 8 * b + 8)
                for q in range(4):
                    c, hf = q // 2, q % 2
                    for k in range(2):
                        r = mm(bank(STEP_BANKS[b][q]), w_dl[:, k, c * P:(c + 1) * P], UTb[b][:, k, hf * BANK:(hf + 1) * BANK],
                               start=(k == 0), stop=(k == 1))
                    r.then_inc(s_dp, 1)

            def bc_rows(b):
                if b:
                    pe.wait_ge(s_dr, 8)
                for hf in range(2):
                    for k in range(2):
                        r = mm(PS[0:32, 4 * b + hf, :], w_bc[:, k, :], UTb[b][:, k, hf * BANK:(hf + 1) * BANK],
                               start=(k == 0), stop=(k == 1))
                r.then_inc(s_bp, 1)

            def spread_row(b, at, row):
                for hf in range(2):
                    r = mm(bank(at + hf), pickb[:, bass.ds(row, 1), :].rearrange("p o m -> p (o m)"),
                           R3b[b][:, hf * BANK:(hf + 1) * BANK], start=True, stop=True)
                return r

            def spread_b(b, n, free=True):
                if free:
                    pe.wait_ge(s_db, 32 * b + 2 * n)
                spread_row(b, 0, n).then_inc(s_b, 1)

            def spread_c(b, n, free=True, shared=True):
                if free:
                    pe.wait_ge(s_hc, 32 * b + 2 * n)
                    if shared:
                        pe.wait_ge(s_hp, STATE * b + n - SHARED)
                spread_row(b, 2, n + STATE).then_inc(s_c, 1)

            def spread(b, n, free, shared=True):
                spread_b(b, n, free)
                spread_c(b, n, free, shared)

            def through_identity(src, c, first):
                for hf in range(2):
                    r = mm(bank(4 + 2 * c + hf), ident, src[:, c, hf * BANK:(hf + 1) * BANK], start=first, stop=True,
                           skip_group_check=True)
                return r

            def add_y(n, c, first=False):
                pe.wait_ge(s_hc, 32 + 2 * n + c + 1)
                if c == 1:
                    pe.wait_ge(s_hp, STATE + n + 1 - SHARED)
                through_identity(HC, c, first).then_inc(s_yp, 1)

            def beside(b, n, p, s, times):
                spread(b, n, True)
                turn_pair(p, s, times)
                result_pair(p - 1, 1 - s)
                hidden_pair(p, s, times)

            def scan_out(b):
                pe.wait_ge(s_yt, 2 * b + 2)
                for q in range(2):
                    for t in range(4):
                        tt = 4 * q + t
                        for k in range(2):
                            r = mm(PS[:, OUT_BANK[b] + q, t * P:(t + 1) * P], SRb[b][:, k, tt * P:(tt + 1) * P], w_out[:, k, :],
                                   start=(k == 0), stop=(k == 1))
                    r.then_inc(s_op, 1)

            inner(0, range(3, 8))
            step_sizes(0)
            logits(2)
            transposes(3)
            logits(3)
            inner(1)
            ranks(1)
            pe.wait_ge(s_lgr, 2)
            bc_rows(0)
            step_sizes(1)
            pe.wait_ge(s_rkr, 2)
            pe.wait_ge(s_r3, 1)
            pe.wait_ge(s_as, 2)
            spread(0, 0, False)
            bc_rows(1)
            for n in range(1, SHARED + 1):
                spread(0, n, True, False)
            with pe.Fori(SHARED + 1, EARLY) as n:
                spread(0, n, True)
            spread(0, EARLY, True)
            pe.wait_ge(s_r3, 2)
            turn_pair(0, 0, 1)
            hidden_pair(0, 0, 1)
            beside(0, EARLY + 1, 1, 1, 1)
            with pe.Fori(1, (STATE - EARLY) // 2) as r:
                beside(0, EARLY + 2 * r, 2 * r, 0, r + 1)
                beside(0, EARLY + 2 * r + 1, 2 * r + 1, 1, r + 1)
            done = STATE - EARLY
            beside(1, 0, done, 0, done // 2 + 1)
            spread_b(1, 1)
            pe.wait_ge(s_mt[1], done + 1)
            pe.wait_ge(s_mh[1], 2 * (done + 1))
            scan_out(0)
            spread_c(1, 1)
            pe.wait_ge(s_oe, 2)
            turn_pair(done + 1, 1, done // 2 + 1)
            result_pair(done, 0)
            hidden_pair(done + 1, 1, done // 2 + 1)
            with pe.Fori(1, LATE // 2) as r:
                beside(1, 2 * r, done + 2 * r, 0, r + done // 2 + 1)
                beside(1, 2 * r + 1, done + 2 * r + 1, 1, r + done // 2 + 1)
            result_pair(PAIRS - 1, 1)
            spread(1, LATE, True)
            pe.wait_ge(s_my[1], PAIRS)

            def late(n, part_of_base=None):
                spread_b(1, n + 1)
                add_y(n, 0, n is LATE)
                spread_c(1, n + 1)
                add_y(n, 1, n is LATE)
                if part_of_base is not None:
                    pe.wait_ge(s_yb, 3 + part_of_base)
                    through_identity(YA, part_of_base, False)

            late(LATE, 0)
            late(LATE + 1, 1)
            with pe.Fori(LATE + 2, STATE - 1) as n:
                late(n)
            add_y(STATE - 1, 0)
            add_y(STATE - 1, 1)
            scan_out(1)
            pe.wait_ge(s_oe, 4)

        @block.vector
        def _(dve):
            count = [0]

            def link(ins):
                count[0] += 1
                ins.then_inc(s_v, 1)
                dve.wait_ge(s_v, count[0])

            ts, tt = nc.vector.tensor_scalar, nc.vector.tensor_tensor
            stt, cp = nc.vector.scalar_tensor_tensor, nc.vector.tensor_copy

            def batch_tiles(ph):
                return range(TB * (ph % 2), TB * (ph % 2 + 1))

            def statistics(ph):
                for t in batch_tiles(ph):
                    if ph < 2 and t % 4 == 0:
                        dve.wait_ge(s_x, 16 * (t // 4 + 1))
                    r = nc.vector.bn_stats(stats[:, t, :], X[:, t, :])
                link(r)

            def variance(ph):
                r = batch_tiles(ph)
                for t in r:
                    i = nc.vector.bn_aggr(mv[:, t, :], stats[:, t, :])
                link(i)
                ts(lnt[:, 0, r[0]:r[-1] + 1], mv[:, r[0]:r[-1] + 1, 1], EPS, None, ALU.add).then_inc(s_var, 1)

            def rows_out(ph):
                tiles = batch_tiles(ph)
                ve, sd, r0, a, r1 = (lnt[:, i, tiles[0]:tiles[-1] + 1] for i in range(5))
                dve.wait_ge(s_var, ph + 1)
                dve.wait_ge(s_sd, ph + 1)
                link(nc.vector.reciprocal(r0, sd))
                link(tt(a, r0, r0, ALU.mult))
                link(tt(a, a, ve, ALU.mult))
                link(ts(a, a, -0.5, 1.5, ALU.mult, ALU.add))
                link(tt(r1, r0, a, ALU.mult))
                if ph >= 2:
                    dve.wait_ge(s_sc[0], 16 * NT)
                for t in tiles:
                    r = ts(XN[:, t, :], X[:, t, :], mv[:, t, 0:1], lnt[:, 4, t:t + 1], ALU.subtract, ALU.mult)
                    if t % 4 == 3:
                        r.then_inc(s_xn, 1)

            def route(m):
                e_n, k_n, _ = MOE[m]
                n = NT * e_n
                v3 = lambda ap: ap.rearrange("p (t e) -> p t e", e=e_n)
                L = v3(lg[:, 0:n])
                dve.wait_ge(s_lg, m + 1)
                cp(lg[:, 0:n], PS[:, 0, 0:n]).then_inc(s_lgr, 1)
                dve.wait_ge(s_lgr, m + 1)
                iota = bc(cst["iota"][:, 0:e_n], 1, NT)
                mx = [rs1[:, 0, :], rs1[:, 1, :]]
                for k in range(k_n):
                    src = L
                    if k:
                        link(stt(v3(rt[:, 0, 0:n]), v3(oh[:, 0, 0:n]), -KEPT, L, ALU.mult, ALU.add))
                        src = v3(rt[:, 0, 0:n])
                    link(nc.vector.tensor_reduce(mx[k], src, AX_X, ALU.max))
                    link(tt(v3(rt[:, 1, 0:n]), src, bc(mx[k], 2, e_n), ALU.is_equal))
                    link(tt(v3(rt[:, 2, 0:n]), v3(rt[:, 1, 0:n]), iota, ALU.mult))
                    link(nc.vector.tensor_reduce(rs1[:, 2 + k, :], v3(rt[:, 2, 0:n]), AX_X, ALU.min))
                    link(tt(v3(oh[:, k, 0:n]), iota, bc(rs1[:, 2 + k, :], 2, e_n), ALU.is_equal))
                if k_n == 1:
                    cp(ohb[:, 0:n], oh[:, 0, 0:n]).then_inc(s_ohb, 1)
                    tt(v3(rt[:, 0, 0:n]), L, bc(mx[0], 2, e_n), ALU.subtract).then_inc(s_ein, 1)
                else:
                    tt(ohb[:, 0:n], oh[:, 0, 0:n], oh[:, 1, 0:n], ALU.add).then_inc(s_ohb, 1)
                    tt(rs1[:, 5, :], mx[1], mx[0], ALU.subtract).then_inc(s_ein, 1)

            def place(m):
                e_n, k_n, _ = MOE[m]
                n = NT * e_n
                v3 = lambda ap: ap.rearrange("p (t e) -> p t e", e=e_n)
                et = lambda ap: ap.rearrange("p (e t) -> p e t", t=NT)
                link(cp(et(rt[:, 2, 0:n]), tl[:, 256:256 + n].rearrange("p (t e) -> p e t", e=e_n)))
                link(nc.vector.tensor_tensor_scan(rt[:, 3, 0:n], seg[m][:], rt[:, 2, 0:n], 0.0, ALU.mult, ALU.add))
                total = et(rt[:, 3, 0:n])[:, :, NT - 1]
                link(ts(rei[:, 0, 0:e_n], total, float(P - 1), None, ALU.add))
                link(ts(rei[:, 1, 0:e_n], rei[:, 0, 0:e_n], 7, 7, ALU.logical_shift_right, ALU.logical_shift_left))
                link(cp(re1[:, 0, 0:e_n], rei[:, 1, 0:e_n]))
                link(nc.vector.tensor_tensor_scan(re1[:, 1, 0:e_n], re1[:, 3, 0:e_n], re1[:, 0, 0:e_n], 0.0, ALU.mult, ALU.add))
                link(tt(re1[:, 2, 0:e_n], re1[:, 1, 0:e_n], re1[:, 0, 0:e_n], ALU.subtract))
                link(tt(rt[:, 3, 0:n], rt[:, 3, 0:n], rt[:, 2, 0:n], ALU.subtract))
                link(tt(v3(rt[:, 4, 0:n]), v3(tl[:, 0:n]), rt[:, 3, 0:n].rearrange("p (e t) -> p t e", t=NT), ALU.add))
                link(tt(v3(rt[:, 4, 0:n]), v3(rt[:, 4, 0:n]), bc(re1[:, 2, 0:e_n], 1, NT), ALU.add))
                for k in range(k_n):
                    link(tt(rt[:, 2, 0:n], rt[:, 4, 0:n], oh[:, k, 0:n], ALU.mult))
                    link(nc.vector.tensor_reduce(rs1[:, 7 + k, :], v3(rt[:, 2, 0:n]), AX_X, ALU.add))
                    r = cp(slot[m][:, k, :], rs1[:, 7 + k, :])
                r.then_inc(s_slot, 1)
                tn = TILES[m]
                cmp = tl[:, 0:tn * e_n].rearrange("p (j e) -> p j e", e=e_n)
                link(tt(cmp, bc(re1[:, 1, 0:e_n], 1, tn), bc(cst["first"][:, 0:tn], 2, e_n), ALU.is_le))
                link(nc.vector.tensor_reduce(lg[:, 0:tn], cmp, AX_X, ALU.add))
                ts(eid[m][:], lg[:, 0:tn], float(e_n - 1), None, ALU.min).then_inc(s_eid, 1)

            def pick_weights(m):
                e_n, k_n, _ = MOE[m]
                n = NT * e_n
                v3 = lambda ap: ap.rearrange("p (t e) -> p t e", e=e_n)
                dve.wait_ge(s_eout, m + 1)
                if k_n == 1:
                    link(nc.vector.tensor_reduce(rs1[:, 4, :], v3(rt[:, 1, 0:n]), AX_X, ALU.add))
                    link(nc.vector.reciprocal(wsel[m][:, 0, :], rs1[:, 4, :]))
                else:
                    link(ts(rs1[:, 4, :], rs1[:, 6, :], 1.0, None, ALU.add))
                    link(nc.vector.reciprocal(wsel[m][:, 0, :], rs1[:, 4, :]))
                    link(tt(wsel[m][:, 1, :], wsel[m][:, 0, :], rs1[:, 6, :], ALU.mult))

            def take_ranks(m):
                dve.wait_ge(s_rk, m + 1)
                n = NT * MOE[m][0]
                for at in (0, 256):
                    r = cp(tl[:, at:at + n], PS[:, RANK_BANK[m], at:at + n])
                r.then_inc(s_rkr, 1)
                dve.wait_ge(s_rkr, m + 1)

            nc.vector.memset(onesb[:], 1.0)
            nc.vector.memset(ones1[:], 1.0)
            link(nc.vector.memset(re1[:, 3, :], 1.0))
            for m in range(2):
                link(nc.vector.memset(seg[m][:], 1.0))
                link(nc.vector.memset(seg[m][:].rearrange("p (e t) -> p e t", t=NT)[:, :, 0:1], 0.0))
            dve.wait_ge(s_cst, 16)
            cp(identb[:], ident)
            cp(causalb[:], cst["causal"])
            cp(beforeb[:], cst["before"]).then_inc(s_cnv, 1)
            for ph in range(2):
                statistics(ph)
                variance(ph)
                rows_out(ph)

            def keys_values():
                dve.wait_ge(s_wat, 16 * 8)
                for q in range(4):
                    dve.wait_ge(s_kp, q + 1)
                    b, sl = q // 2, slice((q % 2) * BANK, (q % 2 + 1) * BANK)
                    if q:
                        dve.wait_ge(s_ke, q)
                    stt(QF[:], bank(1 + q), bk[:, 0:1], peT[:, sl], ALU.add, ALU.add).then_inc(s_kf, 1)
                    dve.wait_ge(s_kf, 2 * q + 1)
                    ts(QF[:], QF[:], SCALE, None, ALU.mult).then_inc(s_kf, 1)
                    dve.wait_ge(s_vh, q + 1)
                    tt(VL[:, 4 * q:4 * q + 4, :], bank((5, 6, 7, 1)[q]).rearrange("p (t d) -> p t d", d=D),
                       VH[:, 4 * q:4 * q + 4, :].bitcast(F32), ALU.subtract).then_inc(s_ve, 1)
                    dve.wait_ge(s_kh, q + 1)
                    tt(KL[:, b, sl], QF[:], KH[:, b, sl].bitcast(F32), ALU.subtract).then_inc(s_ke, 1)

            route(0)
            keys_values()
            take_ranks(0)

            def q_evac(g, hf, first=False):
                dve.wait_ge(s_qp, 2 * g + hf + 1)
                if not first:
                    dve.wait_ge(s_qe, 2 * g + hf)
                h = g - 8 * batch[0]
                stt(QF[:], bank(7), bq[:, bass.ds(h, 1)], peT[:, hf * BANK:(hf + 1) * BANK], ALU.add,
                    ALU.add).then_inc(s_qr, 1)

            batch = [0]

            def neg_max(g, i):
                dve.wait_ge(s_qk, 8 * g + i + 1)
                s = i % 2
                sc = PS[:, 2 * s:2 * s + 2, :].rearrange("p a n -> p (a n)")
                nc.vector.tensor_reduce(nmax[:, i % 4:i % 4 + 1], sc[:, 0:(i + 1) * P], AX_X, ALU.max,
                                        negate=True).then_inc(s_nm, 1)

            def low(g, i):
                for part in range(1 if i < 4 else 2):
                    c = i if i < 4 else 4 + 2 * (i - 4) + part
                    dve.wait_ge(s_ea, 12 * g + c + 1)
                    dst, src = turned(PTL, i, part, c)
                    tt(dst, src, turned(PTH, i, part, c)[0].bitcast(F32), ALU.subtract).then_inc(s_ed, 1)

            def inverse(g, s):
                dve.wait_ge(s_ex, 8 * g + 4 + 4 * s)
                nc.vector.reciprocal(rinv[:, 4 * s:4 * s + 4], rsum[:, 4 * s:4 * s + 4]).then_inc(s_ri, 1)

            def add_out(g, s, x_prev):
                dve.wait_ge(s_wo, 2 * g + 1 + s)
                dve.wait_ge(s_ri, 2 * g + 1 + s)
                if x_prev:
                    dve.wait_ge(s_we, 2 * g + s - 1)
                for t in range(4):
                    q = 4 * s + t
                    x = X[:, 8 * batch[0] + q, :]
                    r = stt(x, PS[:, 7, t * P:(t + 1) * P], rinv[:, q:q + 1], x, ALU.mult, ALU.add)
                r.then_inc(s_we, 1)

            def head(g, pending, follow, x_prev=True, beside=None):
                for i in range(8):
                    neg_max(g, i)
                    if beside and i in beside:
                        beside[i]()
                    if i == 0 and pending:
                        low(g - 1, 7)
                        inverse(g - 1, 1)
                    if i >= 1:
                        low(g, i - 1)
                    if i == 1 and pending:
                        add_out(g - 1, 0, x_prev)
                    if i == 2:
                        q_evac(g, 1)
                    if i == 4:
                        inverse(g, 0)
                    if i == 5 and pending:
                        add_out(g - 1, 1, x_prev)
                    if i == 6 and follow:
                        q_evac(g + 1, 0)

            def attention_start(b):
                batch[0] = b
                q_evac(8 * b, 0, b == 0)
                head(8 * b, False, True)

            def attention_rest(b):
                g = 8 * b + 1
                head(g, True, True, False)
                with dve.Fori(g + 1, g + 6) as gg:
                    head(gg, True, True)
                g = 8 * b + 7
                head(g, True, False, beside=b and {0: lambda: combine_first(0), 2: lambda: statistics(2),
                                                   3: lambda: variance(2), 6: lambda: rows_out(2)})
                low(g, 7)
                inverse(g, 1)
                add_out(g, 0, True)
                add_out(g, 1, True)

            def experts_first():
                def rows(p, s):
                    dve.wait_ge(s_mtp[0], p + 1)
                    cp(MXT[:, 4 * s:4 * s + 4, :], bank(s).rearrange("p (i n) -> p i n", n=P)).then_inc(s_mt[0], 1)

                def result(p, s, times):
                    dve.wait_ge(s_myp[0], p + 1)
                    if times is not None:
                        dve.wait_ge(s_mo[0][s], 16 * times)
                    tt(MY[:, 4 * s:4 * s + 4, :], bank(4).rearrange("p (i n) -> p i n", n=P),
                       mw0[:, 4 * s:4 * s + 4, 4 * P + 2:4 * P + 2 + D], ALU.add).then_inc(s_my[0], 1)

                rows(0, 0)
                rows(1, 1)
                result(0, 0, None)
                rows(2, 0)
                result(1, 1, None)
                with dve.Fori(1, QUADS // 2 - 1) as r:
                    rows(2 * r + 1, 1)
                    result(2 * r, 0, r)
                    rows(2 * r + 2, 0)
                    result(2 * r + 1, 1, r)
                rows(QUADS - 1, 1)
                result(QUADS - 2, 0, QUADS // 2 - 1)
                result(QUADS - 1, 1, QUADS // 2 - 1)

            def combine_first(b):
                dve.wait_ge(s_g0[b], 16 * TB)
                for t in batch_tiles(b):
                    r = stt(X[:, t, :], GA[:, t, :], wsel[0][:, 0, t:t + 1], X[:, t, :], ALU.mult, ALU.add)
                    r.then_inc(s_gu, 1)
                dve.wait_ge(s_gu, TB * (b + 1))

            def combine_second(b):
                for q in (2 * b, 2 * b + 1):
                    dve.wait_ge(s_g1[q], 16 * 8)
                    for k in range(2):
                        if k:
                            dve.wait_ge(s_gu, NT + 8 * q + 4)
                        for t in range(4):
                            x = X[:, 4 * q + t, :]
                            stt(x, G1b[q // 2][:, 8 * (q % 2) + 4 * k + t, :], wsel[1][:, k, 4 * q + t:4 * q + t + 1], x,
                                ALU.mult, ALU.add).then_inc(s_gu, 1)

            attention_start(0)
            pick_weights(0)
            place(0)
            attention_rest(0)
            experts_first()
            attention_start(1)
            attention_rest(1)
            dve.wait_ge(s_we, 32)
            combine_first(1)
            def step_sizes(b):
                w, e, ln, dl = S1b[b], S2b[b], S3b[b], DLb[b]
                dve.wait_ge(s_da1, 5 * b + 5)
                ts(w, e, 1.0, None, ALU.add).then_inc(s_dw, 1)
                dve.wait_ge(s_dw, b + 1)
                link(stt(e, w, 1.0, e, ALU.subtract, ALU.subtract))
                dve.wait_ge(s_dr, 4 * b + 4)
                link(tt(dl, dl, e, ALU.subtract))
                dve.wait_ge(s_dl, b + 1)
                link(tt(dl, dl, ln, ALU.add))
                dve.wait_ge(s_ue2, 8 * b + 8)
                tt(DUb[b], dl, UTb[b], ALU.mult).then_inc(s_du, 1)
                dve.wait_ge(s_du, b + 1)

            def bc_parts(b):
                dve.wait_ge(s_bp, b + 1)
                bcr = PS[0:32, 4 * b:4 * b + 2, :].rearrange("p a n -> p (a n)")
                rest, mid, r3 = S2b[b][0:32, 0, :], S3b[b][0:32, 0, 0:BANK].bitcast(BF16), R3b[b]
                link(cp(r3[0:32, :], bcr))
                link(tt(rest, bcr, r3[0:32, :], ALU.subtract))
                link(cp(mid, rest))
                link(cp(r3[32:64, :], mid))
                link(tt(rest, rest, mid, ALU.subtract))
                cp(r3[64:96, :], rest).then_inc(s_r3, 1)

            def state(b, n, free, mid=None, late=False, shared=2):
                u = 32 * b + 2 * n
                dve.wait_ge(s_b, 16 * b + n + 1)
                for c in range(2):
                    if free:
                        dve.wait_ge(s_sn, u + c - 1)
                    spread = PS[:, 0:2, :].rearrange("p a n -> p (a n)")
                    tt(DB[:, c, :], DUb[b][:, c, :], spread, ALU.mult).then_inc(s_db, 1)
                for c in range(2):
                    dve.wait_ge(s_dA, u + c + 1)
                    dve.wait_ge(s_db, u + c + 1)
                    if free:
                        dve.wait_ge(s_hc, u + c - 1)
                        if c == 1 and shared > 1:
                            dve.wait_ge(s_hp, STATE * b + n - SHARED)
                    nc.vector.tensor_tensor_scan(HS[:, c, :], DA[:, c, :], DB[:, c, :], 0.0, ALU.mult,
                                                 ALU.add).then_inc(s_sn, 1)
                if mid:
                    mid()
                dve.wait_ge(s_c, 16 * b + n + 1)
                if shared:
                    dve.wait_ge(s_cc, STATE * b + n + 1 - SHARED)
                for c in range(2):
                    dve.wait_ge(s_sn, u + c + 1)
                    if late:
                        dve.wait_ge(s_yp, 2 * n - 2 * LATE - 1 + c)
                    elif free:
                        dve.wait_ge(s_ya, u + c - 1)
                    w = BANK if c == 1 and shared else T
                    spread = PS[:, 2:4, :].rearrange("p a n -> p (a n)")
                    tt(HC[:, c, 0:w], HS[:, c, 0:w], spread[:, 0:w], ALU.mult).then_inc(s_hc, 1)

            def with_skip(b):
                for c in range(2):
                    dve.wait_ge(s_ya, 32 * b + 2 * (LATE if b else STATE))
                    stt(YA[:, c, :], UTb[b][:, c, :], d_par[:, c:c + 1], YA[:, c, :], ALU.mult, ALU.add).then_inc(s_yb, 1)
                dve.wait_ge(s_yb, 2 * b + 2)

            def gated(b):
                for c in range(2):
                    y = YA[:, c, :]
                    if b:
                        dve.wait_ge(s_yp, 2 * (STATE - LATE) - 1 + c)
                        y = PS[:, 4 + 2 * c:6 + 2 * c, :].rearrange("p a n -> p (a n)")
                    tt(SRb[b][:, c, :], y, SRb[b][:, c, :], ALU.mult).then_inc(s_yt, 1)

            def scan_out(b):
                for q in range(2):
                    dve.wait_ge(s_op, 2 * b + q + 1)
                    x = X[:, 8 * b + 4 * q:8 * b + 4 * q + 4, :].rearrange("p t d -> p (t d)")
                    tt(x, bank(OUT_BANK[b] + q), x, ALU.add).then_inc(s_oe, 1)

            statistics(3)
            variance(3)
            rows_out(3)
            dve.wait_ge(s_as, 1)
            link(ts(a_sc[:], a_sc[:], -1.0, None, ALU.mult))
            link(nc.vector.memset(R3[96:128, :], 0.0))
            step_sizes(0)
            route(1)
            take_ranks(1)
            place(1)
            bc_parts(0)
            pick_weights(1)
            dve.wait_ge(s_r3, 1)
            state(0, 0, False, shared=0)
            dve.wait_ge(s_zf, 16 * zero_fills)

            def second_batch():
                step_sizes(1)
                bc_parts(1)

            state(0, 1, True, second_batch, shared=0)
            state(0, 2, True, shared=1)
            with dve.Fori(3, STATE) as n:
                state(0, n, True)
            state(1, 0, True)
            with_skip(0)
            gated(0)
            state(1, 1, True, lambda: scan_out(0))
            with dve.Fori(2, LATE) as n:
                state(1, n, True)

            state(1, LATE, True, lambda: with_skip(1))
            with dve.Fori(LATE + 1, STATE) as n:
                state(1, n, True, late=True)
            dve.wait_ge(s_oe, 2)
            combine_second(0)
            gated(1)
            combine_second(1)
            dve.wait_ge(s_gu, NT + 32)
            scan_out(1)


def kernel(**inputs):
    import concourse.bacc as bacc
    from concourse.bass_utils import run_bass_kernel_spmd as run

    get = lambda n: np.asarray(inputs[n])
    by_partition = lambda a: a.reshape(-1, P).T
    cst, _ = small_constants()

    def rows_of(w):
        e, r, n = w.shape
        return w.reshape(e, r // P, P, n).transpose(0, 2, 1, 3).reshape(e, P, -1)

    b1, b2 = get("L0_ffn_b1"), get("L0_ffn_b2")
    w_0 = np.concatenate([rows_of(get("L0_ffn_w1")), rows_of(get("L0_ffn_w2")), b1.reshape(-1, 2, P).transpose(0, 2, 1),
                          np.broadcast_to(b2[:, None, :], (b2.shape[0], P, D))], 2)
    w_1 = np.concatenate([rows_of(get("L1_ffn_w1").transpose(0, 2, 1)), rows_of(get("L1_ffn_w2").transpose(0, 2, 1))], 2)
    data = {
        "x": get("L0_attn_x"), "Wkv": get("L0_attn_Wkv"), "bkv": get("L0_attn_bkv"), "bq": by_partition(get("L0_attn_bq")),
        "WqH": get("L0_attn_Wq").reshape(D, HEADS, D).transpose(1, 0, 2), "Wo": get("L0_attn_Wo"),
        "router_w": get("L0_ffn_router_w"), "w_0": w_0, "w_1": w_1, "W_in": get("L1_attn_W_in"),
        "W_delta": get("L1_attn_W_delta"), "b_delta": by_partition(get("L1_attn_b_delta")), "W_B": get("L1_attn_W_B"),
        "W_C": get("L1_attn_W_C"), "A_log": get("L1_attn_A_log"), "D_param": by_partition(get("L1_attn_D_param")),
        "W_out": get("L1_attn_W_out"), "gate_wT": get("L1_ffn_gate_w").T,
        "cst": cst, "peT": positions(),
    }
    nc = bacc.Bacc("TRN2", target_bir_lowering=False, num_devices=1)
    arrays, args = {}, {}
    for name, a in data.items():
        a = np.ascontiguousarray(a)
        arrays[f"in_{name}"] = a
        args[name] = nc.dram_tensor(f"in_{name}", a.shape, mybir.dt.from_np(a.dtype), kind="ExternalInput").ap()
    out = nc.dram_tensor("out_0", (B, T, D), F32, kind="ExternalOutput").ap()
    scratch = {
        "rows_in": [nc.dram_tensor(f"rows_in{m}", (TILES[m] * P, D), F32, kind="Internal").ap() for m in range(2)],
        "rows_out": [nc.dram_tensor(f"rows_out{m}", (TILES[m] * P, D), F32, kind="Internal").ap() for m in range(2)],
    }
    build(nc, args, out, scratch)
    r = run(nc, [arrays], core_ids=[0])
    return r.results[0]["out_0"]
```
